# Optimizing a Trainium2 kernel written in Bass

```python
import numpy as np
import jax
import jax.numpy as jnp

def _softmax(x, axis=-1):
    return jax.nn.softmax(x, axis=axis)

def _gelu(x):
    return jax.nn.gelu(x, approximate=True)

def _silu(x):
    return jax.nn.silu(x)

def _sigmoid(x):
    return jax.nn.sigmoid(x)

def _layernorm(x, axis=-1, eps=1e-05):
    m = jnp.mean(x, axis=axis, keepdims=True)
    v = jnp.var(x, axis=axis, keepdims=True)
    return (x - m) / jnp.sqrt(v + eps)

def _scatter_add(tgt, idx, src, axis=0):
    return tgt.at[idx].add(src)

def _segment_sum(src, seg, n):
    return jax.ops.segment_sum(src, seg, n)
kernel_name = 'mk_gnn_ffn_d4_gnn_r16_c24d12'

def setup_inputs(seed: int=0):
    np.random.seed(seed)
    _w = jnp.asarray

    def _rec_inputs():
        import jax
        import jax.numpy as jnp
        _gk = jax.random.key(seed)
        x = -0.0003713 + 1 * jax.random.normal(jax.random.fold_in(_gk, 1), (3125, 256), jnp.float32)
        _s = jax.random.randint(jax.random.fold_in(_gk, 2), (25000,), 0, 3125, jnp.int32)
        _d = jax.random.randint(jax.random.fold_in(_gk, 3), (25000,), 0, 3125, jnp.int32)
        _loop = jnp.arange(3125, dtype=jnp.int32)
        src = jnp.concatenate([_s, _d, _loop])
        dst = jnp.concatenate([_d, _s, _loop])
        _o = jnp.argsort(dst, stable=True)
        src = src[_o]
        dst = dst[_o]
        edge_attr_64 = 0.000312547 + 1.00004 * jax.random.normal(jax.random.fold_in(_gk, 12), (53125, 64), jnp.float32)
        edge_weight = jax.random.uniform(jax.random.fold_in(_gk, 14), (53125,), jnp.float32, 0.0, 1)
        return (x, src, dst, edge_attr_64, edge_weight)
    x, src, dst, edge_attr_64, edge_weight = _rec_inputs()

    def _L0_gnn_setup():
        import jax, jax.numpy as jnp
        import numpy as np
        N = 3125
        E = 50000
        F_IN = 256
        K = 8
        F_OUT = 32
        NEG_SLOPE = 0.2
        key = jax.random.key(seed)
        k1, k2, k3, k4, k5, k6 = jax.random.split(key, 6)
        x = jax.random.normal(k1, (N, F_IN), dtype=jnp.float32)
        edge_index = jax.random.randint(k2, (2, E), 0, N, dtype=jnp.int64)
        W = jax.random.normal(k3, (F_IN, K * F_OUT), dtype=jnp.float32) * (2.0 / (F_IN + K * F_OUT)) ** 0.5
        b = jax.random.uniform(k4, (K * F_OUT,), dtype=jnp.float32)
        a_src = jax.random.normal(k5, (1, K, F_OUT), dtype=jnp.float32) * (2.0 / (K * F_OUT + 1)) ** 0.5
        a_trg = jax.random.normal(k6, (1, K, F_OUT), dtype=jnp.float32) * (2.0 / (K * F_OUT + 1)) ** 0.5
        return {'x': x, 'edge_index': edge_index, 'W': W, 'b': b, 'a_src': a_src, 'a_trg': a_trg}
    _L0_gnn_all = _L0_gnn_setup()
    _L0_gnn_in = {k: v for k, v in _L0_gnn_all.items() if k in ('W', 'b', 'a_src', 'a_trg')}
    del _L0_gnn_all

    def _L0_ffn_setup():
        import math
        import jax, jax.numpy as jnp
        import numpy as np
        CAPACITY_FACTOR = 1.25
        TOP_K = 2
        LN_EPS = 1e-05

        def _layer_norm(x, gamma, beta):
            mu = jnp.mean(x, axis=-1, keepdims=True)
            var = jnp.var(x, axis=-1, keepdims=True)
            return (x - mu) * jax.lax.rsqrt(var + LN_EPS) * gamma + beta
        key = jax.random.key(seed)
        ks = jax.random.split(key, 4)
        B, S, D, F, E = (8, 256, 256, 512, 8)
        x = jax.random.normal(ks[0], (B, S, D), dtype=jnp.float32)
        Wr = jax.random.normal(ks[1], (D, E), dtype=jnp.float32) / np.sqrt(D)
        br = jnp.zeros((E,), jnp.float32)
        W1 = jax.random.normal(ks[2], (E, D, F), dtype=jnp.float32) / np.sqrt(D)
        b1 = jnp.zeros((E, F), jnp.float32)
        W2 = jax.random.normal(ks[3], (E, F, D), dtype=jnp.float32) / np.sqrt(F)
        b2 = jnp.zeros((E, D), jnp.float32)
        gamma = jnp.ones((D,), jnp.float32)
        beta = jnp.zeros((D,), jnp.float32)
        return {'x': x, 'Wr': Wr, 'br': br, 'W1': W1, 'b1': b1, 'W2': W2, 'b2': b2, 'gamma': gamma, 'beta': beta}
    _L0_ffn_all = _L0_ffn_setup()
    _L0_ffn_in = {k: v for k, v in _L0_ffn_all.items() if k in ('Wr', 'br', 'W1', 'b1', 'W2', 'b2', 'gamma', 'beta')}
    del _L0_ffn_all

    def _L1_gnn_setup():
        import jax, jax.numpy as jnp
        import numpy as np
        N_NODES = 6250
        N_EDGES = 100000
        D_IN = 256
        D_OUT = 256
        key = jax.random.key(seed)
        k1, k2, k3, k4, k5 = jax.random.split(key, 5)
        x = jax.random.normal(k1, (N_NODES, D_IN), dtype=jnp.float32)
        edge_src = jax.random.randint(k2, (N_EDGES,), 0, N_NODES, dtype=jnp.int32)
        edge_dst = jax.random.randint(k3, (N_EDGES,), 0, N_NODES, dtype=jnp.int32)
        edge_val = jax.random.uniform(k4, (N_EDGES,), dtype=jnp.float32)
        stdv = 1.0 / np.sqrt(D_OUT)
        weight = jax.random.uniform(k5, (D_IN, D_OUT), dtype=jnp.float32, minval=-stdv, maxval=stdv)
        return {'x': x, 'edge_src': edge_src, 'edge_dst': edge_dst, 'edge_val': edge_val, 'weight': weight}
    _L1_gnn_all = _L1_gnn_setup()
    _L1_gnn_in = {k: v for k, v in _L1_gnn_all.items() if k in ('weight',)}
    del _L1_gnn_all

    def _L1_ffn_setup():
        import jax, jax.numpy as jnp
        import numpy as np
        E, D, H, TOP_K = (6, 256, 256, 2)
        ROUTER_H = D // 2
        key = jax.random.key(seed)
        ks = jax.random.split(key, 12)
        s = 1.0 / np.sqrt(D)
        sh = 1.0 / np.sqrt(H)
        sr = 1.0 / np.sqrt(ROUTER_H)
        return {'features': jax.random.normal(ks[0], (8, 256, D), dtype=jnp.float32), 'router_w1': jax.random.uniform(ks[1], (D, ROUTER_H), jnp.float32, -s, s), 'router_b1': jnp.zeros((ROUTER_H,), jnp.float32), 'router_w2': jax.random.uniform(ks[2], (ROUTER_H, E), jnp.float32, -sr, sr), 'router_b2': jnp.zeros((E,), jnp.float32), 'expert_w1': jax.random.uniform(ks[3], (E, D, H), jnp.float32, -s, s), 'expert_b1': jnp.zeros((E, H), jnp.float32), 'expert_w2': jax.random.uniform(ks[4], (E, H, H), jnp.float32, -sh, sh), 'expert_b2': jnp.zeros((E, H), jnp.float32), 'expert_w3': jax.random.uniform(ks[5], (E, H, D), jnp.float32, -sh, sh), 'expert_b3': jnp.zeros((E, D), jnp.float32)}
    _L1_ffn_all = _L1_ffn_setup()
    _L1_ffn_in = {k: v for k, v in _L1_ffn_all.items() if k in ('router_w1', 'router_b1', 'router_w2', 'router_b2', 'expert_w1', 'expert_b1', 'expert_w2', 'expert_b2', 'expert_w3', 'expert_b3')}
    del _L1_ffn_all

    def _L2_gnn_setup():
        import jax, jax.numpy as jnp
        import numpy as np
        N = 3125
        E = 50000
        D = 256

        def _gcn_norm(edge_index, n_nodes):
            loop = jnp.arange(n_nodes, dtype=edge_index.dtype)
            row = jnp.concatenate([edge_index[0], loop])
            col = jnp.concatenate([edge_index[1], loop])
            deg = jax.ops.segment_sum(jnp.ones_like(col, dtype=jnp.float32), col, num_segments=n_nodes)
            dinv = jnp.where(deg > 0, jax.lax.rsqrt(deg), 0.0)
            norm = dinv[row] * dinv[col]
            return (row, col, norm)

        def _gcn_conv(h, row, col, norm, W, b, n_nodes):
            h = h @ W.T
            msg = h[row] * norm[:, None]
            out = jax.ops.segment_sum(msg, col, num_segments=n_nodes)
            return out + b
        key = jax.random.key(seed)
        ks = jax.random.split(key, 8)
        scale = 1.0 / np.sqrt(D)
        x = jax.random.normal(ks[0], (N, D), dtype=jnp.float32)
        edge_index = jax.random.randint(ks[1], (2, E), 0, N, dtype=jnp.int32)
        W1 = jax.random.normal(ks[2], (D, D), dtype=jnp.float32) * scale
        b1 = jnp.zeros((D,), dtype=jnp.float32)
        W2 = jax.random.normal(ks[3], (D, D), dtype=jnp.float32) * scale
        b2 = jnp.zeros((D,), dtype=jnp.float32)
        W3 = jax.random.normal(ks[4], (D, D), dtype=jnp.float32) * scale
        b3 = jnp.zeros((D,), dtype=jnp.float32)
        return {'x': x, 'edge_index': edge_index, 'W1': W1, 'b1': b1, 'W2': W2, 'b2': b2, 'W3': W3, 'b3': b3}
    _L2_gnn_all = _L2_gnn_setup()
    _L2_gnn_in = {k: v for k, v in _L2_gnn_all.items() if k in ('W1', 'b1', 'W2', 'b2', 'W3', 'b3')}
    del _L2_gnn_all

    def _L2_ffn_setup():
        import jax, jax.numpy as jnp
        import numpy as np
        B, K, D = (512, 16, 256)
        E = 32
        H = int(D * 0.25)
        key = jax.random.key(seed)
        ks = jax.random.split(key, 7)
        d_rs = D ** (-0.5)
        h_rs = H ** (-0.5)
        x = jax.random.normal(ks[0], (B, K, D), dtype=jnp.float32)
        router_w = jax.random.uniform(ks[1], (E, D), jnp.float32, -d_rs, d_rs)
        router_b = jax.random.uniform(ks[2], (E,), jnp.float32, -d_rs, d_rs)
        W1 = jax.random.uniform(ks[3], (E, D, H), jnp.float32, -h_rs, h_rs)
        b1 = jax.random.uniform(ks[4], (E, H), jnp.float32, -h_rs, h_rs)
        W2 = jax.random.uniform(ks[5], (E, H, D), jnp.float32, -d_rs, d_rs)
        b2 = jax.random.uniform(ks[6], (E, D), jnp.float32, -d_rs, d_rs)
        return {'x': x, 'router_w': router_w, 'router_b': router_b, 'W1': W1, 'b1': b1, 'W2': W2, 'b2': b2}
    _L2_ffn_all = _L2_ffn_setup()
    _L2_ffn_in = {k: v for k, v in _L2_ffn_all.items() if k in ('router_w', 'router_b', 'W1', 'b1', 'W2', 'b2')}
    del _L2_ffn_all

    def _L3_gnn_setup():
        import jax, jax.numpy as jnp
        import numpy as np
        N, E, H, DE = (625, 15625, 256, 64)
        EPS = 1e-05

        def _lin_init(k, fan_in, shape):
            s = 1.0 / np.sqrt(fan_in)
            return jax.random.uniform(k, shape, jnp.float32, -s, s)
        key = jax.random.key(seed)
        ks = jax.random.split(key, 12)
        x = jax.random.normal(ks[0], (N, H), jnp.float32)
        edge_index = jax.random.randint(ks[1], (2, E), 0, N)
        edge_attr = jax.random.normal(ks[2], (E, DE), jnp.float32)
        d_in = H + DE
        W1 = _lin_init(ks[3], d_in, (d_in, H))
        b1 = _lin_init(ks[4], d_in, (H,))
        W2 = _lin_init(ks[5], H, (H, H))
        b2 = _lin_init(ks[6], H, (H,))
        Wg = _lin_init(ks[7], d_in, (d_in, H))
        bg = _lin_init(ks[8], d_in, (H,))
        gamma = jnp.ones((H,), jnp.float32)
        beta = jnp.zeros((H,), jnp.float32)
        return {'x': x, 'edge_index': edge_index, 'edge_attr': edge_attr, 'W1': W1, 'b1': b1, 'W2': W2, 'b2': b2, 'Wg': Wg, 'bg': bg, 'gamma': gamma, 'beta': beta}
    _L3_gnn_all = _L3_gnn_setup()
    _L3_gnn_in = {k: v for k, v in _L3_gnn_all.items() if k in ('W1', 'b1', 'W2', 'b2', 'Wg', 'bg', 'gamma', 'beta')}
    del _L3_gnn_all

    def _L3_ffn_setup():
        import jax, jax.numpy as jnp
        import numpy as np
        E = 8
        K = 2
        D = 256
        H = 512
        DOUT = 256
        EPS = 1e-05
        key = jax.random.key(seed)
        ks = jax.random.split(key, 9)
        s = 0.02
        return {'x': jax.random.normal(ks[0], (4, 512, D), jnp.float32), 'gamma': 1.0 + 0.05 * jax.random.normal(ks[1], (D,), jnp.float32), 'beta': 0.05 * jax.random.normal(ks[2], (D,), jnp.float32), 'Wr': 0.01 * jax.random.normal(ks[3], (D, E), jnp.float32), 'br': jnp.zeros((E,), jnp.float32), 'W1': s * jax.random.normal(ks[4], (E, D, H), jnp.float32), 'b1': s * jax.random.normal(ks[5], (E, H), jnp.float32), 'W2': s * jax.random.normal(ks[6], (E, H, DOUT), jnp.float32), 'b2': s * jax.random.normal(ks[7], (E, DOUT), jnp.float32)}
    _L3_ffn_all = _L3_ffn_setup()
    _L3_ffn_in = {k: v for k, v in _L3_ffn_all.items() if k in ('gamma', 'beta', 'Wr', 'br', 'W1', 'b1', 'W2', 'b2')}
    del _L3_ffn_all
    return {'x': x, 'src': src, 'dst': dst, 'edge_attr_64': edge_attr_64, 'edge_weight': edge_weight, 'L0_gnn_W': _L0_gnn_in['W'], 'L0_gnn_b': _L0_gnn_in['b'], 'L0_gnn_a_src': _L0_gnn_in['a_src'], 'L0_gnn_a_trg': _L0_gnn_in['a_trg'], 'L0_ffn_Wr': _L0_ffn_in['Wr'], 'L0_ffn_br': _L0_ffn_in['br'], 'L0_ffn_W1': _L0_ffn_in['W1'], 'L0_ffn_b1': _L0_ffn_in['b1'], 'L0_ffn_W2': _L0_ffn_in['W2'], 'L0_ffn_b2': _L0_ffn_in['b2'], 'L0_ffn_gamma': _L0_ffn_in['gamma'], 'L0_ffn_beta': _L0_ffn_in['beta'], 'L1_gnn_weight': _L1_gnn_in['weight'], 'L1_ffn_router_w1': _L1_ffn_in['router_w1'], 'L1_ffn_router_b1': _L1_ffn_in['router_b1'], 'L1_ffn_router_w2': _L1_ffn_in['router_w2'], 'L1_ffn_router_b2': _L1_ffn_in['router_b2'], 'L1_ffn_expert_w1': _L1_ffn_in['expert_w1'], 'L1_ffn_expert_b1': _L1_ffn_in['expert_b1'], 'L1_ffn_expert_w2': _L1_ffn_in['expert_w2'], 'L1_ffn_expert_b2': _L1_ffn_in['expert_b2'], 'L1_ffn_expert_w3': _L1_ffn_in['expert_w3'], 'L1_ffn_expert_b3': _L1_ffn_in['expert_b3'], 'L2_gnn_W1': _L2_gnn_in['W1'], 'L2_gnn_b1': _L2_gnn_in['b1'], 'L2_gnn_W2': _L2_gnn_in['W2'], 'L2_gnn_b2': _L2_gnn_in['b2'], 'L2_gnn_W3': _L2_gnn_in['W3'], 'L2_gnn_b3': _L2_gnn_in['b3'], 'L2_ffn_router_w': _L2_ffn_in['router_w'], 'L2_ffn_router_b': _L2_ffn_in['router_b'], 'L2_ffn_W1': _L2_ffn_in['W1'], 'L2_ffn_b1': _L2_ffn_in['b1'], 'L2_ffn_W2': _L2_ffn_in['W2'], 'L2_ffn_b2': _L2_ffn_in['b2'], 'L3_gnn_W1': _L3_gnn_in['W1'], 'L3_gnn_b1': _L3_gnn_in['b1'], 'L3_gnn_W2': _L3_gnn_in['W2'], 'L3_gnn_b2': _L3_gnn_in['b2'], 'L3_gnn_Wg': _L3_gnn_in['Wg'], 'L3_gnn_bg': _L3_gnn_in['bg'], 'L3_gnn_gamma': _L3_gnn_in['gamma'], 'L3_gnn_beta': _L3_gnn_in['beta'], 'L3_ffn_gamma': _L3_ffn_in['gamma'], 'L3_ffn_beta': _L3_ffn_in['beta'], 'L3_ffn_Wr': _L3_ffn_in['Wr'], 'L3_ffn_br': _L3_ffn_in['br'], 'L3_ffn_W1': _L3_ffn_in['W1'], 'L3_ffn_b1': _L3_ffn_in['b1'], 'L3_ffn_W2': _L3_ffn_in['W2'], 'L3_ffn_b2': _L3_ffn_in['b2']}

def reference(x, src, dst, edge_attr_64, edge_weight, L0_gnn_W, L0_gnn_b, L0_gnn_a_src, L0_gnn_a_trg, L0_ffn_Wr, L0_ffn_br, L0_ffn_W1, L0_ffn_b1, L0_ffn_W2, L0_ffn_b2, L0_ffn_gamma, L0_ffn_beta, L1_gnn_weight, L1_ffn_router_w1, L1_ffn_router_b1, L1_ffn_router_w2, L1_ffn_router_b2, L1_ffn_expert_w1, L1_ffn_expert_b1, L1_ffn_expert_w2, L1_ffn_expert_b2, L1_ffn_expert_w3, L1_ffn_expert_b3, L2_gnn_W1, L2_gnn_b1, L2_gnn_W2, L2_gnn_b2, L2_gnn_W3, L2_gnn_b3, L2_ffn_router_w, L2_ffn_router_b, L2_ffn_W1, L2_ffn_b1, L2_ffn_W2, L2_ffn_b2, L3_gnn_W1, L3_gnn_b1, L3_gnn_W2, L3_gnn_b2, L3_gnn_Wg, L3_gnn_bg, L3_gnn_gamma, L3_gnn_beta, L3_ffn_gamma, L3_ffn_beta, L3_ffn_Wr, L3_ffn_br, L3_ffn_W1, L3_ffn_b1, L3_ffn_W2, L3_ffn_b2):
    import jax
    import jax.numpy as jnp

    def _L0_gnn_ref(x, edge_index, W, b, a_src, a_trg):
        import jax, jax.numpy as jnp
        import numpy as np
        N = 3125
        E = 50000
        F_IN = 256
        K = 8
        F_OUT = 32
        NEG_SLOPE = 0.2
        n = x.shape[0]
        loops = jnp.arange(n, dtype=edge_index.dtype)
        src = jnp.concatenate([edge_index[0], loops])
        trg = jnp.concatenate([edge_index[1], loops])
        h_prime = (x @ W + b).reshape(n, K, F_OUT)
        h_src = jnp.sum(h_prime * a_src, axis=2)
        h_trg = jnp.sum(h_prime * a_trg, axis=2)
        e = h_src[src] + h_trg[trg]
        e = jax.nn.leaky_relu(e, negative_slope=NEG_SLOPE)
        e = e - jnp.max(e)
        exp_e = jnp.exp(e)
        denom = jax.ops.segment_sum(exp_e, trg, num_segments=n)
        alpha = exp_e / (denom[trg] + 1e-10)
        msg = h_prime[src] * alpha[:, :, None]
        out = jax.ops.segment_sum(msg, trg, num_segments=n)
        return out.reshape(n, K * F_OUT)

    def _L0_ffn_ref(x, Wr, br, W1, b1, W2, b2, gamma, beta):
        import math
        import jax, jax.numpy as jnp
        import numpy as np
        CAPACITY_FACTOR = 1.25
        TOP_K = 2
        LN_EPS = 1e-05

        def _layer_norm(x, gamma, beta):
            mu = jnp.mean(x, axis=-1, keepdims=True)
            var = jnp.var(x, axis=-1, keepdims=True)
            return (x - mu) * jax.lax.rsqrt(var + LN_EPS) * gamma + beta
        B, S, D = x.shape
        E = Wr.shape[1]
        N = B * S
        K = TOP_K
        logits = jnp.mean(x, axis=1) @ Wr + br
        routing_weights = jax.nn.softmax(logits, axis=-1)
        capacity = float(math.ceil(N * CAPACITY_FACTOR / E))
        expected_loads = routing_weights.sum(axis=0) * (N / B)
        scale = jnp.where(expected_loads > capacity, capacity / expected_loads, 1.0)
        routing_weights = jax.nn.softmax(routing_weights * scale, axis=-1)
        rw_tok = jnp.broadcast_to(routing_weights[:, None, :], (B, S, E)).reshape(N, E)
        top_w, top_i = jax.lax.top_k(rw_tok, K)
        top_w = jax.nn.softmax(top_w, axis=-1)
        xf = x.reshape(N, D)
        h = jax.nn.gelu(jnp.einsum('nd,edf->enf', xf, W1) + b1[:, None, :], approximate=False)
        y = jnp.einsum('enf,efd->end', h, W2) + b2[:, None, :]
        w_dense = jnp.zeros((N, E), x.dtype).at[jnp.arange(N)[:, None], top_i].add(top_w)
        out = jnp.einsum('ne,end->nd', w_dense, y).reshape(B, S, D)
        out = _layer_norm(out + x, gamma, beta)
        return out

    def _L1_gnn_ref(x, edge_src, edge_dst, edge_val, weight):
        import jax, jax.numpy as jnp
        import numpy as np
        N_NODES = 6250
        N_EDGES = 100000
        D_IN = 256
        D_OUT = 256
        msgs = x[edge_src] * edge_val[:, None]
        agg = jax.ops.segment_sum(msgs, edge_dst, num_segments=x.shape[0])
        return agg @ weight

    def _L1_ffn_ref(features, router_w1, router_b1, router_w2, router_b2, expert_w1, expert_b1, expert_w2, expert_b2, expert_w3, expert_b3):
        import jax, jax.numpy as jnp
        import numpy as np
        E, D, H, TOP_K = (6, 256, 256, 2)
        ROUTER_H = D // 2
        rh = jax.nn.relu(features @ router_w1 + router_b1)
        expert_logits = jax.nn.softmax(rh @ router_w2 + router_b2, axis=-1)
        top_w, top_i = jax.lax.top_k(expert_logits, TOP_K)
        routing_weights = jax.nn.softmax(top_w, axis=-1)
        h1 = jax.nn.relu(jnp.einsum('bsd,edh->bseh', features, expert_w1) + expert_b1)
        h2 = jax.nn.relu(jnp.einsum('bseh,ehf->bsef', h1, expert_w2) + expert_b2)
        expert_out = jnp.einsum('bsef,efo->bseo', h2, expert_w3) + expert_b3
        sel = jnp.take_along_axis(expert_out, top_i[:, :, :, None], axis=2)
        combined = jnp.sum(sel * routing_weights[..., None], axis=2)
        return combined

    def _L2_gnn_ref(x, edge_index, W1, b1, W2, b2, W3, b3):
        import jax, jax.numpy as jnp
        import numpy as np
        N = 3125
        E = 50000
        D = 256

        def _gcn_norm(edge_index, n_nodes):
            loop = jnp.arange(n_nodes, dtype=edge_index.dtype)
            row = jnp.concatenate([edge_index[0], loop])
            col = jnp.concatenate([edge_index[1], loop])
            deg = jax.ops.segment_sum(jnp.ones_like(col, dtype=jnp.float32), col, num_segments=n_nodes)
            dinv = jnp.where(deg > 0, jax.lax.rsqrt(deg), 0.0)
            norm = dinv[row] * dinv[col]
            return (row, col, norm)

        def _gcn_conv(h, row, col, norm, W, b, n_nodes):
            h = h @ W.T
            msg = h[row] * norm[:, None]
            out = jax.ops.segment_sum(msg, col, num_segments=n_nodes)
            return out + b
        n_nodes = x.shape[0]
        row, col, norm = _gcn_norm(edge_index, n_nodes)
        h = jax.nn.relu(_gcn_conv(x, row, col, norm, W1, b1, n_nodes))
        h = jax.nn.relu(_gcn_conv(h, row, col, norm, W2, b2, n_nodes))
        out = _gcn_conv(h, row, col, norm, W3, b3, n_nodes)
        return out

    def _L2_ffn_ref(x, router_w, router_b, W1, b1, W2, b2):
        import jax, jax.numpy as jnp
        import numpy as np
        B, K, D = (512, 16, 256)
        E = 32
        H = int(D * 0.25)
        xf = x.reshape(-1, D)
        logits = xf @ router_w.T + router_b
        idx = jnp.argmax(logits, axis=-1)
        w1t = jnp.take(W1, idx, axis=0)
        h = jnp.einsum('nd,ndh->nh', xf, w1t) + jnp.take(b1, idx, axis=0)
        h = jax.nn.relu(h)
        w2t = jnp.take(W2, idx, axis=0)
        out = jnp.einsum('nh,nhd->nd', h, w2t) + jnp.take(b2, idx, axis=0)
        out = jax.nn.relu(out)
        return out.reshape(x.shape)

    def _L3_gnn_ref(x, edge_index, edge_attr, W1, b1, W2, b2, Wg, bg, gamma, beta):
        import jax, jax.numpy as jnp
        import numpy as np
        N, E, H, DE = (625, 15625, 256, 64)
        EPS = 1e-05

        def _lin_init(k, fan_in, shape):
            s = 1.0 / np.sqrt(fan_in)
            return jax.random.uniform(k, shape, jnp.float32, -s, s)
        src, dst = (edge_index[0], edge_index[1])
        ei = jnp.concatenate([x[src], edge_attr], axis=-1)
        core = jnp.maximum(ei @ W1 + b1, 0.0) @ W2 + b2
        gate = jax.nn.sigmoid(ei @ Wg + bg)
        msg = gate * core
        agg = jax.ops.segment_sum(msg, dst, num_segments=x.shape[0])
        out = agg + x
        mu = jnp.mean(out, axis=-1, keepdims=True)
        var = jnp.var(out, axis=-1, keepdims=True)
        out = (out - mu) * jax.lax.rsqrt(var + EPS) * gamma + beta
        return out

    def _L3_ffn_ref(x, gamma, beta, Wr, br, W1, b1, W2, b2):
        import jax, jax.numpy as jnp
        import numpy as np
        E = 8
        K = 2
        D = 256
        H = 512
        DOUT = 256
        EPS = 1e-05
        mu = jnp.mean(x, axis=-1, keepdims=True)
        var = jnp.mean(jnp.square(x - mu), axis=-1, keepdims=True)
        xn = (x - mu) * jax.lax.rsqrt(var + EPS) * gamma + beta
        logits = jnp.einsum('bsd,de->bse', xn, Wr) + br
        top_vals, top_idx = jax.lax.top_k(logits, K)
        w = jax.nn.softmax(top_vals, axis=-1)
        w_full = jnp.einsum('bsk,bske->bse', w, jax.nn.one_hot(top_idx, E, dtype=w.dtype))
        y = jnp.zeros(x.shape[:-1] + (DOUT,), x.dtype)
        for e in range(E):
            h = jax.nn.gelu(jnp.einsum('bsd,dh->bsh', xn, W1[e]) + b1[e], approximate=False)
            y_e = jnp.einsum('bsh,hd->bsd', h, W2[e]) + b2[e]
            y = y + y_e * w_full[..., e, None]
        return y
    edge_index = jnp.stack([src, dst])
    x = x + _L0_gnn_ref(_layernorm(x, axis=-1), edge_index, L0_gnn_W, L0_gnn_b, L0_gnn_a_src, L0_gnn_a_trg)
    x = x + _L0_ffn_ref(_layernorm(x, axis=-1)[None], L0_ffn_Wr, L0_ffn_br, L0_ffn_W1, L0_ffn_b1, L0_ffn_W2, L0_ffn_b2, L0_ffn_gamma, L0_ffn_beta)[0]
    x = x + _L1_gnn_ref(_layernorm(x, axis=-1), src, dst, edge_weight, L1_gnn_weight)
    x = x + _L1_ffn_ref(_layernorm(x, axis=-1)[None], L1_ffn_router_w1, L1_ffn_router_b1, L1_ffn_router_w2, L1_ffn_router_b2, L1_ffn_expert_w1, L1_ffn_expert_b1, L1_ffn_expert_w2, L1_ffn_expert_b2, L1_ffn_expert_w3, L1_ffn_expert_b3)[0]
    x = x + _L2_gnn_ref(_layernorm(x, axis=-1), edge_index, L2_gnn_W1, L2_gnn_b1, L2_gnn_W2, L2_gnn_b2, L2_gnn_W3, L2_gnn_b3)
    x = x + _L2_ffn_ref(_layernorm(x, axis=-1)[None], L2_ffn_router_w, L2_ffn_router_b, L2_ffn_W1, L2_ffn_b1, L2_ffn_W2, L2_ffn_b2)[0]
    x = x + _L3_gnn_ref(_layernorm(x, axis=-1), edge_index, edge_attr_64, L3_gnn_W1, L3_gnn_b1, L3_gnn_W2, L3_gnn_b2, L3_gnn_Wg, L3_gnn_bg, L3_gnn_gamma, L3_gnn_beta)
    x = x + _L3_ffn_ref(_layernorm(x, axis=-1)[None], L3_ffn_gamma, L3_ffn_beta, L3_ffn_Wr, L3_ffn_br, L3_ffn_W1, L3_ffn_b1, L3_ffn_W2, L3_ffn_b2)[0]
    return x

_drawn_inputs = setup_inputs


def setup_inputs(seed=0):
    import zlib

    import numpy as np

    out = dict(_drawn_inputs(seed))
    spreads = {'L0_ffn_br': (0.0, 2.0),
     'L0_ffn_b1': (0.0, 0.1),
     'L0_ffn_b2': (0.0, 0.1),
     'L0_ffn_gamma': (1.0, 0.2),
     'L0_ffn_beta': (0.0, 0.1),
     'L1_ffn_router_b1': (0.0, 0.493),
     'L1_ffn_router_b2': (0.0, 0.59),
     'L1_ffn_expert_b1': (0.0, 0.8),
     'L1_ffn_expert_b2': (0.0, 0.661),
     'L1_ffn_expert_b3': (0.0, 0.312),
     'L2_gnn_b1': (0.0, 0.446),
     'L2_gnn_b2': (0.0, 0.388),
     'L2_gnn_b3': (0.0, 0.1),
     'L3_gnn_gamma': (1.0, 0.2),
     'L3_gnn_beta': (0.0, 0.288),
     'L3_ffn_br': (0.0, 0.731)}
    factors = {'L1_ffn_expert_w1': 2.855,
     'L2_ffn_router_b': 3.671,
     'L2_ffn_b1': 8.0,
     'L2_ffn_b2': 6.939,
     'L3_gnn_b1': 4.38,
     'L3_gnn_bg': 8.0,
     'L3_ffn_gamma': 8.0,
     'L3_ffn_beta': 8.0,
     'L3_ffn_Wr': 5.253,
     'L3_ffn_W1': 3.799,
     'L3_ffn_b1': 27.893,
     'L3_ffn_W2': 3.711,
     'L3_ffn_b2': 32.818,
     'L0_ffn_Wr': 8.0}
    for name, (base, spread) in spreads.items():
        noise = np.random.default_rng([zlib.crc32(name.encode()), seed]).standard_normal(out[name].shape)
        drawn = base * np.exp(spread * noise) if base else spread * noise
        out[name] = jnp.asarray(drawn.astype(out[name].dtype))
    for name, factor in factors.items():
        out[name] = (out[name] * factor).astype(out[name].dtype)
    return out
```

```python
from contextlib import ExitStack

import concourse.bass as bass
from concourse import mybir

F32 = mybir.dt.float32
I32 = mybir.dt.int32
ALU = mybir.AluOpType
ACT = mybir.ActivationFunctionType
X = mybir.AxisListType.X
RMAX = bass.bass_isa.ReduceOp.max

P = 125
NT = 25
N = P * NT
NCH = 425
D = 256
KD = D // 128
RING = 5
GR = 10
HEADS, HF = 8, 32
HROW = HF + 1
EPS = 1e-5
BT = 4
NB = NT // BT
EX = HEADS + 1
MASKED = -1e38


class Signal:

    def __init__(self, sem):
        self.sem = sem
        self.base = 0

    def at(self, n):
        return n + self.base

    def passed(self, n):
        self.base += n


class Signals:

    def __init__(self, sig):
        self.loaded = sig("loaded")
        self.chain = sig("chain")
        self.act_step = sig("act_step")
        self.pe_step = sig("pe_step")
        self.pool_step = sig("pool_step")
        self.gate_pool = sig("gate_pool")
        self.gate_act = sig("gate_act")
        self.gate_pe = sig("gate_pe")
        self.rows_ready = sig("rows_ready")
        self.turned = sig("turned")
        self.evicted = sig("evicted")
        self.xn_copied = sig("xn_copied")
        self.stored = sig("stored")
        self.used = sig("used")
        self.one_hot = sig("one_hot")
        self.agg_ready = sig("agg_ready")
        self.added = sig("added")
        self.staged = sig("staged")
        self.tile_ready = sig("tile_ready")
        self.hid_ready = sig("hid_ready")
        self.hid_done = sig("hid_done")
        self.y_ready = sig("y_ready")
        self.y_done = sig("y_done")
        self.wt_staged = sig("wt_staged")
        self.ea_turned = sig("ea_turned")
        self.eaT_ready = sig("eaT_ready")
        self.pre_ready = sig("pre_ready")
        self.relu_done = sig("relu_done")
        self.gpre_done = sig("gpre_done")
        self.gate_done = sig("gate_done")
        self.core_ready = sig("core_ready")
        self.msg_done = sig("msg_done")


def rounds(eng, count, body):
    body(0, True)
    with eng.Fori(1, count) as i:
        body(i, False)


def build(nc, io, out, stop=99):
    with ExitStack() as ctx:
        build_in(nc, io, out, ctx, stop)


def build_in(nc, io, out, ctx, stop):
    def sb(name, shape, dt=F32, c=ctx):
        return c.enter_context(nc.sbuf_tensor(name, shape, dt))

    def sig(name):
        return Signal(ctx.enter_context(nc.semaphore(name)))

    xres = sb("xres", [P, NT, D])
    xn = sb("xn", [P, NT, D])
    featT = sb("featT", [128, KD, N + P])
    stage = sb("stage", [128, RING, 512])
    ident = sb("ident", [128, 128])
    iota = sb("iota", [P, P])
    ones = sb("ones", [128, 128])
    row0 = sb("row0", [P, P])
    src_i = sb("src_i", [P, NCH], I32)
    dst_i = sb("dst_i", [P, NCH], I32)
    dloc = sb("dloc", [P, NCH])
    ew = sb("ew", [P, NCH])
    base_i = sb("base_i", [1, NCH], I32)
    dinv = sb("dinv", [P, NT])
    idx = sb("idx", [P, GR], I32)
    stats = sb("stats", [P, NT, 6])
    small = sb("small", [P, 8, NT])
    ps = ctx.enter_context(nc.psum_tensor("ps", [128, 8, 512], F32))

    g = Signals(sig)
    gath = [sig(f"gathered{j}") for j in range(GR)]
    store = [sig(f"row_store{j}") for j in range(RING)]
    wload = [sig(f"weights{e}") for e in range(8)]

    def hold(eng, ns, gate, s, count):
        eng.wait_ge(s.sem, s.at(count))
        ns.sem_inc(gate.sem)

    def hold_act(s, count):
        hold(nc.scalar, nc.scalar, g.gate_act, s, count)

    def hold_pool(s, count):
        hold(nc.gpsimd, nc.gpsimd, g.gate_pool, s, count)

    def hold_pe(s, count):
        hold(nc.tensor, nc.tensor, g.gate_pe, s, count)

    def dram(name, shape):
        return nc.dram_tensor(name, shape, F32).ap()

    t_att = dram("t_att", [N, HEADS * HROW])
    t_hs = dram("t_hs", [N, HEADS])
    t_ht = dram("t_ht", [N, HEADS])
    t_row = dram("t_row", [N, D])
    t_row2 = dram("t_row2", [N, D])
    t_edge = dram("t_edge", [N, 2 * D])

    def prepare():
        with ExitStack() as c:
            rows = 85
            raw_i = sb("raw_i", [rows, 2, RING, P], I32, c)
            raw_f = sb("raw_f", [rows, 3, RING, P], F32, c)
            dst_f = sb("dst_f", [P, NCH], F32, c)
            with nc.Block() as block:
                @block.sync
                def _(sp):
                    for a, t in enumerate((io["src"], io["dst"])):
                        sp.dma_start(raw_i[:, a], t.rearrange("(r q p) -> q r p", q=rows, p=P)).then_inc(g.loaded.sem, 16)
                    sp.dma_start(raw_f[:, 2], io["edge_weight"].rearrange("(r q p) -> q r p", q=rows, p=P)).then_inc(g.loaded.sem, 16)

                @block.gpsimd
                def _(pool):
                    pool.dma_start(xres[:], io["x"].rearrange("(t p) d -> p t d", p=P)).then_inc(g.stored.sem, 16)
                    nc.gpsimd.iota(iota[:], [[1, P]], base=0, channel_multiplier=0,
                                   allow_small_or_imprecise_dtypes=True).then_inc(g.pool_step.sem, 1)
                    nc.gpsimd.memset(ones[:], 1.0).then_inc(g.pool_step.sem, 1)
                    pool.wait_ge(g.pool_step.sem, 2)
                    nc.gpsimd.affine_select(out=ident[:], in_=ones[:], pattern=[[-1, 128]], compare_op=ALU.is_equal,
                                            fill=0.0, base=0, channel_multiplier=1).then_inc(g.pool_step.sem, 1)
                    nc.gpsimd.affine_select(out=row0[:], in_=ones[0:P, 0:P], pattern=[[0, P]], compare_op=ALU.is_equal,
                                            fill=0.0, base=0, channel_multiplier=1).then_inc(g.pool_step.sem, 1)
                    pool.wait_ge(g.stored.sem, 16)

                @block.vector
                def _(dve):
                    dve.wait_ge(g.loaded.sem, 48)
                    nc.vector.tensor_copy(raw_f[:, 0:2], raw_i[:]).then_inc(g.chain.sem, 1)
                    for a in range(3):
                        dve.wait_ge(g.turned.sem, a + 1)
                        if a == 0:
                            nc.vector.tensor_copy(src_i[:], ps[0:P, 0, 0:NCH]).then_inc(g.chain.sem, 1)
                        elif a == 1:
                            nc.vector.tensor_copy(dst_i[:], ps[0:P, 1, 0:NCH]).then_inc(g.chain.sem, 1)
                            nc.vector.tensor_copy(dst_f[:], ps[0:P, 1, 0:NCH]).then_inc(g.chain.sem, 1)
                            nc.vector.tensor_copy(base_i[:], ps[0:1, 1, 0:NCH]).then_inc(g.chain.sem, 1)
                        else:
                            nc.vector.tensor_copy(ew[:], ps[0:P, 2, 0:NCH]).then_inc(g.chain.sem, 1)
                    dve.wait_ge(g.turned.sem, 4)
                    nc.vector.tensor_tensor(dloc[:], dst_f[:], ps[0:P, 3, 0:NCH], ALU.subtract).then_inc(g.chain.sem, 1)

                @block.tensor
                def _(pe):
                    pe.wait_ge(g.pool_step.sem, 4)
                    pe.wait_ge(g.chain.sem, 1)
                    for a in range(3):
                        for r in range(RING):
                            mm = nc.tensor.transpose(ps[0:P, a, r * rows:(r + 1) * rows], raw_f[:, a, r, :], ident[0:rows, 0:rows])
                        mm.then_inc(g.turned.sem, 1)
                    pe.wait_ge(g.chain.sem, 4)
                    nc.tensor.matmul(ps[0:P, 3, 0:NCH], row0[:], dst_f[:], start=True, stop=True).then_inc(g.turned.sem, 1)
        g.loaded.passed(48), g.stored.passed(16), g.pool_step.passed(4), g.chain.passed(7), g.turned.passed(4)

    def normalize(tag, src, gamma=None, beta=None, to_xn=False, to_featT=False, table=None, scale=None, add_to_x=False):
        with ExitStack() as c:
            gb = sb(tag + "_gb", [P, 2, D], F32, c) if gamma is not None else None
            nper = 1 + (2 if gamma is not None else 0) + (1 if scale is not None else 0)
            mean2, diff, m2, var, sd, rstd, mean = (small[:, k, :] for k in range(7))
            PRE = NT + 6
            PER = nper - 1 + (1 if add_to_x else 0)
            with nc.Block() as block:
                @block.sync
                def _(sp):
                    if gamma is not None:
                        sp.dma_start(gb[:, 0, :], gamma.partition_broadcast(P)).then_inc(g.loaded.sem, 16)
                        sp.dma_start(gb[:, 1, :], beta.partition_broadcast(P)).then_inc(g.loaded.sem, 16)
                    if table is not None:
                        def body(i, first):
                            for j in range(RING):
                                sp.wait_ge(g.rows_ready.sem, g.rows_ready.at(RING * i + j + 1))
                                sp.dma_start(table[bass.ds(P * RING * i + P * j, P), :], stage[0:P, j, 0:D]).then_inc(store[j].sem, 16)
                        rounds(sp, NT // RING, body)
                        for j in range(RING):
                            sp.wait_ge(store[j].sem, store[j].at(16 * NT // RING))

                @block.vector
                def _(dve):
                    ch = g.chain
                    def stat(i, first):
                        nc.vector.bn_stats(stats[:, bass.ds(i, 1), :], src[:, bass.ds(i, 1), :]).then_inc(ch.sem, 1)
                    rounds(dve, NT, stat)
                    dve.wait_ge(ch.sem, ch.at(NT))
                    nc.vector.tensor_tensor(mean2, stats[:, :, 1], stats[:, :, 4], ALU.add).then_inc(ch.sem, 1)
                    nc.vector.tensor_tensor(diff, stats[:, :, 1], stats[:, :, 4], ALU.subtract).then_inc(ch.sem, 1)
                    nc.vector.tensor_tensor(m2, stats[:, :, 2], stats[:, :, 5], ALU.add).then_inc(ch.sem, 1)
                    dve.wait_ge(ch.sem, ch.at(NT + 3))
                    nc.vector.tensor_tensor(var, diff, diff, ALU.mult).then_inc(ch.sem, 1)
                    nc.vector.tensor_scalar(mean, mean2, 0.5, None, ALU.mult).then_inc(ch.sem, 1)
                    dve.wait_ge(ch.sem, ch.at(NT + 5))
                    nc.vector.scalar_tensor_tensor(var, var, D / 4.0, m2, ALU.mult, ALU.add).then_inc(g.pool_step.sem, 1)
                    dve.wait_ge(g.pool_step.sem, g.pool_step.at(1))
                    nc.vector.tensor_scalar(var, var, 1.0 / D, EPS, ALU.mult, ALU.add).then_inc(ch.sem, 1)
                    dve.wait_ge(g.act_step.sem, g.act_step.at(1))
                    nc.vector.reciprocal(rstd, sd).then_inc(g.pool_step.sem, 1)
                    dve.wait_ge(g.pool_step.sem, g.pool_step.at(2))
                    if gamma is not None:
                        dve.wait_ge(g.loaded.sem, g.loaded.at(32))

                    def body(i, first):
                        for j in range(RING):
                            n = RING * i + j
                            st = stage[0:P, j, 0:D]
                            if not first:
                                if to_xn:
                                    dve.wait_ge(g.xn_copied.sem, g.xn_copied.at(n - RING + 1))
                                if to_featT:
                                    dve.wait_ge(g.turned.sem, g.turned.at(n - RING + 1))
                                if table is not None:
                                    dve.wait_ge(store[j].sem, store[j].at(16 * i))
                                if add_to_x:
                                    dve.wait_ge(ch.sem, ch.at(PRE + PER * (n - RING + 1)))
                            k = 0
                            last = nc.vector.tensor_scalar(st, src[:, bass.ds(n, 1), :].rearrange("p a d -> p (a d)"), mean[:, bass.ds(n, 1)],
                                                           rstd[:, bass.ds(n, 1)], ALU.subtract, ALU.mult)
                            if gamma is not None:
                                for q, op in ((0, ALU.mult), (1, ALU.add)):
                                    last.then_inc(ch.sem, 1)
                                    k += 1
                                    dve.wait_ge(ch.sem, ch.at(PRE + PER * n + k))
                                    last = nc.vector.tensor_tensor(st, st, gb[:, q, :], op)
                            if scale is not None:
                                last.then_inc(ch.sem, 1)
                                k += 1
                                dve.wait_ge(ch.sem, ch.at(PRE + PER * n + k))
                                last = nc.vector.tensor_scalar(st, st, scale[:, bass.ds(n, 1)], None, ALU.mult)
                            last.then_inc(g.rows_ready.sem, 1)
                            if add_to_x:
                                dve.wait_ge(g.rows_ready.sem, g.rows_ready.at(n + 1))
                                xt = xres[:, bass.ds(n, 1), :].rearrange("p a d -> p (a d)")
                                nc.vector.tensor_tensor(xt, xt, st, ALU.add).then_inc(ch.sem, 1)
                    rounds(dve, NT // RING, body)

                @block.scalar
                def _(act):
                    act.wait_ge(g.chain.sem, g.chain.at(PRE))
                    nc.scalar.activation(sd, var, ACT.Sqrt).then_inc(g.act_step.sem, 1)

                    def body(i, first):
                        for j in range(RING):
                            n = RING * i + j
                            if to_xn:
                                hold_act(g.rows_ready, n + 1)
                                nc.scalar.copy(xn[:, bass.ds(n, 1), :].rearrange("p a d -> p (a d)"), stage[0:P, j, 0:D]).then_inc(g.xn_copied.sem, 1)
                            if to_featT:
                                hold_act(g.turned, n + 1)
                                nc.scalar.copy(featT[:, :, bass.ds(P * n, P)],
                                               ps[:, j, 0:KD * P].rearrange("p (k t) -> p k t", k=KD)).then_inc(g.evicted.sem, 1)
                    if to_xn or to_featT:
                        rounds(act, NT // RING, body)

                @block.tensor
                def _(pe):
                    def body(i, first):
                        for j in range(RING):
                            n = RING * i + j
                            pe.wait_ge(g.rows_ready.sem, g.rows_ready.at(n + 1))
                            if not first:
                                pe.wait_ge(g.evicted.sem, g.evicted.at(n - RING + 1))
                            for k in range(KD):
                                mm = nc.tensor.transpose(ps[:, j, k * P:(k + 1) * P], stage[0:P, j, k * 128:(k + 1) * 128], ident[0:P, 0:P])
                            mm.then_inc(g.turned.sem, 1)
                    if to_featT:
                        rounds(pe, NT // RING, body)
        g.chain.passed(PRE + PER * NT), g.pool_step.passed(2), g.act_step.passed(1), g.rows_ready.passed(NT)
        if gamma is not None:
            g.loaded.passed(32)
        if to_xn:
            g.xn_copied.passed(NT)
        if to_featT:
            g.turned.passed(NT), g.evicted.passed(NT)
        if table is not None:
            for s in store:
                s.passed(16 * NT // RING)

    def tiles(load, weights_in, turn_weights, pe_ops, dve_ops, per, sp_rows=None, extra=None):
        NL = len(load)
        NW = len(turn_weights)
        ch = g.chain
        with nc.Block() as block:
            @block.sync
            def _(sp):
                for d, s in load:
                    sp.dma_start(d, s).then_inc(g.loaded.sem, 16)
                if sp_rows is not None:
                    def body(i, first):
                        for j in range(RING):
                            n = RING * i + j
                            sp.wait_ge(ch.sem, ch.at(per * (n + 1)))
                            for d, s in sp_rows(n, j):
                                sp.dma_start(d, s).then_inc(store[j].sem, 16)
                    rounds(sp, NT // RING, body)
                    k = len(sp_rows(0, 0))
                    for j in range(RING):
                        sp.wait_ge(store[j].sem, store[j].at(16 * k * NT // RING))

            @block.scalar
            def _(act):
                def body(i, first):
                    for j in range(RING):
                        n = RING * i + j
                        if not first:
                            hold_act(g.tile_ready, n - RING + 1)
                        last = nc.scalar.copy(stage[:, j, 0:KD * P].rearrange("p (k t) -> p k t", k=KD), featT[:, :, bass.ds(P * n, P)])
                        if extra is not None:
                            last.then_inc(g.act_step.sem, 1)
                            last = nc.scalar.copy(stage[0:EX, j, KD * P:KD * P + P], extra[:, bass.ds(P * n, P)])
                        last.then_inc(g.staged.sem, 1)
                rounds(act, NT // RING, body)

            @block.tensor
            def _(pe):
                if NL:
                    pe.wait_ge(g.loaded.sem, g.loaded.at(16 * NL))
                for w, (d, s, rows) in enumerate(turn_weights):
                    if w >= 2:
                        pe.wait_ge(g.pe_step.sem, g.pe_step.at(w - 1))
                    nc.tensor.transpose(ps[0:128, 6 + w % 2, 0:rows], s, ident[0:rows, 0:rows]).then_inc(g.turned.sem, 1)
                if NW:
                    pe.wait_ge(g.pe_step.sem, g.pe_step.at(NW))

                def body(i, first):
                    for j in range(RING):
                        n = RING * i + j
                        pe.wait_ge(g.staged.sem, g.staged.at(n + 1))
                        if extra is not None:
                            pe.wait_ge(g.act_step.sem, g.act_step.at(n + 1))
                        if not first:
                            pe.wait_ge(ch.sem, ch.at(per * (n - RING + 1)))
                        pe_ops(j, stage[:, j, 0:KD * P].rearrange("p (k t) -> p k t", k=KD)).then_inc(g.tile_ready.sem, 1)
                rounds(pe, NT // RING, body)

            @block.vector
            def _(dve):
                if NL:
                    dve.wait_ge(g.loaded.sem, g.loaded.at(16 * NL))
                for w, (d, s, rows) in enumerate(turn_weights):
                    dve.wait_ge(g.turned.sem, g.turned.at(w + 1))
                    nc.vector.tensor_copy(d, ps[0:128, 6 + w % 2, 0:rows]).then_inc(g.pe_step.sem, 1)

                def body(i, first):
                    for j in range(RING):
                        n = RING * i + j
                        dve.wait_ge(g.tile_ready.sem, g.tile_ready.at(n + 1))
                        if sp_rows is not None and not first:
                            dve.wait_ge(store[j].sem, store[j].at(16 * len(sp_rows(0, 0)) * i))
                        dve_ops(dve, n, j, per * n)
                rounds(dve, NT // RING, body)
        g.loaded.passed(16 * NL), g.turned.passed(NW), g.pe_step.passed(NW)
        g.staged.passed(NT), g.tile_ready.passed(NT), ch.passed(per * NT)
        if extra is not None:
            g.act_step.passed(NT)
        if sp_rows is not None:
            for s in store:
                s.passed(16 * len(sp_rows(0, 0)) * NT // RING)

    def tile_of(t, n):
        return t[:, bass.ds(n, 1), :].rearrange("p a d -> p (a d)")

    def times(w, width):
        def pe_ops(j, x):
            for k in range(KD):
                mm = nc.tensor.matmul(ps[0:P, j, 0:width], x[:, k, :], w[:, k, 0:width], start=(k == 0), stop=(k == KD - 1))
            return mm
        return pe_ops

    def halves(w):
        return w.rearrange("(k p) f -> p k f", p=128)

    def wait_chain(dve, count):
        dve.wait_ge(g.chain.sem, g.chain.at(count))

    def att_project(own):
        with ExitStack() as c:
            w = sb("att_w", [128, KD, D], F32, c)
            b = sb("att_b", [P, D], F32, c)
            a = sb("att_a", [P, 2, D], F32, c)
            rows = sb("ap_rows", [P, RING, HROW, HEADS], F32, c)
            prod = sb("att_prod", [P, 2, D], F32, c)
            hst = sb("att_hst", [P, RING, 2, HEADS], F32, c)
            with nc.Block() as block:
                @block.vector
                def _(dve):
                    nc.vector.memset(rows[:], 1.0)

            def use(dve, n, j, c0):
                ch = g.chain.sem
                h = rows[:, j, 0:HF, :].rearrange("p f h -> p h f")
                nc.vector.tensor_tensor(h, ps[0:P, j, 0:D].rearrange("p (h f) -> p h f", h=HEADS),
                                        b[:].rearrange("p (h f) -> p h f", h=HEADS), ALU.add).then_inc(ch, 1)
                wait_chain(dve, c0 + 1)
                for s in range(2):
                    nc.vector.tensor_tensor(prod[:, s, :].rearrange("p (h f) -> p h f", h=HEADS), h,
                                            a[:, s, :].rearrange("p (h f) -> p h f", h=HEADS), ALU.mult).then_inc(ch, 1)
                wait_chain(dve, c0 + 3)
                nc.vector.tensor_reduce(hst[:, j, :, :], prod[:].rearrange("p s (h f) -> p s h f", h=HEADS), X, ALU.add).then_inc(ch, 1)
                nc.vector.tensor_copy(tile_of(xn, n), rows[:, j, 0:HF, :].rearrange("p f h -> p (f h)")).then_inc(ch, 1)
                wait_chain(dve, c0 + 4)
                nc.vector.tensor_tensor(tile_of(own, n), hst[:, j, 0, :], hst[:, j, 1, :], ALU.add).then_inc(ch, 1)

            tiles([(w[:], halves(io["L0_gnn_W"])), (b[:], io["L0_gnn_b"].partition_broadcast(P)),
                   (a[:, 0, :], io["L0_gnn_a_src"].rearrange("a h f -> (a h f)").partition_broadcast(P)),
                   (a[:, 1, :], io["L0_gnn_a_trg"].rearrange("a h f -> (a h f)").partition_broadcast(P))],
                  None, [], times(w, D), use, 6,
                  sp_rows=lambda n, j: [(t_att[bass.ds(P * n, P), :], rows[:, j].rearrange("p f h -> p (f h)")),
                                        (t_hs[bass.ds(P * n, P), :], hst[:, j, 0, :]),
                                        (t_ht[bass.ds(P * n, P), :], hst[:, j, 1, :])])

    def gathers(pool, parts, free, sources):
        def fill(i, h, first):
            if not first:
                hold_pool(free, GR * i + RING * h - RING)
            for q, (table, ids) in enumerate(parts):
                last = nc.gpsimd.tensor_copy(sources[q][0][:, RING * h:RING * h + RING], ids[:, bass.ds(GR * i + RING * h, RING)])
                last.then_inc(g.pool_step.sem, 1)
            hold_pool(g.pool_step, len(parts) * (2 * i + h + 1))
            for j in range(RING * h, RING * h + RING):
                for q, (table, ids) in enumerate(parts):
                    nc.gpsimd.indirect_dma_start(out=sources[q][1][:, j, :], out_offset=None, in_=table,
                                                 in_offset=bass.IndirectOffsetOnAxis(ap=sources[q][0][:, j:j + 1], axis=0)).then_inc(gath[j].sem, 16)
        fill(0, 0, True), fill(0, 1, True)
        with pool.Fori(1, NCH // GR) as i:
            fill(i, 0, False), fill(i, 1, False)
        fill(NCH // GR, 0, False)

    def gathers_passed(parts):
        g.pool_step.passed(parts * (NCH // RING))
        for j in range(GR):
            gath[j].passed(16 * parts * (NCH // GR + (1 if j < RING else 0)))

    def chunks(eng, body, lead=0):
        with eng.Fori(0, NCH // GR) as i:
            for j in range(GR):
                body(GR * i + j, i, j)
        for j in range(NCH % GR):
            body(NCH - NCH % GR + j, NCH // GR, j)

    def att_weights(ex, own):
        with ExitStack() as c:
            rs = sb("hs_rows", [P, GR, HEADS], F32, c)
            rt = sb("ht_rows", [P, GR, HEADS], F32, c)
            idx2 = sb("idx2", [P, GR], I32, c)
            top = sb("top", [P, 4], F32, c)
            flat = ex[:].rearrange("p c h -> p (c h)")
            flat_own = own[:].rearrange("p t h -> p (t h)")
            with nc.Block() as block:
                @block.gpsimd
                def _(pool):
                    gathers(pool, [(t_hs, src_i), (t_ht, dst_i)], g.used, [(idx, rs), (idx2, rt)])
                    pool.wait_ge(g.chain.sem, g.chain.at(5))
                    nc.gpsimd.partition_all_reduce(top[:, 1:2], top[:, 0:1], P, RMAX).then_inc(g.pe_step.sem, 1)

                @block.vector
                def _(dve):
                    def half(i, h):
                        for j in range(RING * h, RING * h + RING):
                            dve.wait_ge(gath[j].sem, gath[j].at(32 * i + 32))
                        nc.vector.tensor_tensor(ex[:, bass.ds(GR * i + RING * h, RING), :], rs[:, RING * h:RING * h + RING, :],
                                                rt[:, RING * h:RING * h + RING, :], ALU.add).then_inc(g.used.sem, RING)
                    with dve.Fori(0, NCH // GR) as i:
                        half(i, 0), half(i, 1)
                    half(NCH // GR, 0)
                    dve.wait_ge(g.used.sem, g.used.at(NCH))
                    nc.vector.scalar_tensor_tensor(flat, flat, 0.2, flat, ALU.mult, ALU.max).then_inc(g.chain.sem, 1)
                    nc.vector.scalar_tensor_tensor(flat_own, flat_own, 0.2, flat_own, ALU.mult, ALU.max).then_inc(g.chain.sem, 1)
                    wait_chain(dve, 2)
                    nc.vector.tensor_reduce(top[:, 2:3], flat, X, ALU.max).then_inc(g.chain.sem, 1)
                    nc.vector.tensor_reduce(top[:, 3:4], flat_own, X, ALU.max).then_inc(g.chain.sem, 1)
                    wait_chain(dve, 4)
                    nc.vector.tensor_tensor(top[:, 0:1], top[:, 2:3], top[:, 3:4], ALU.max).then_inc(g.chain.sem, 1)
                    dve.wait_ge(g.pe_step.sem, g.pe_step.at(1))
                    nc.vector.tensor_scalar(top[:, 2:3], top[:, 1:2], -1.0, None, ALU.mult).then_inc(g.chain.sem, 1)

                @block.scalar
                def _(act):
                    act.wait_ge(g.chain.sem, g.chain.at(6))
                    nc.scalar.activation(flat, flat, ACT.Exp, bias=top[:, 2:3])
                    nc.scalar.activation(flat_own, flat_own, ACT.Exp, bias=top[:, 2:3])
        gathers_passed(2)
        g.used.passed(NCH), g.chain.passed(6), g.pe_step.passed(1)

    def edge_pass(tag, table, weight=None, ex=None, extra=None, loops=False):
        width = HEADS * HROW if ex is not None else D
        with ExitStack() as c:
            rows = sb(tag + "_rows", [P, GR, width], F32, c)
            hot = sb(tag + "_hot", [P, RING, P], F32, c)
            mw = width + 1
            msg = sb(tag + "_msg", [P, RING, mw], F32, c) if ex is not None else None
            zeroed = 3 if ex is not None else 1
            per = 2 if ex is not None else 1
            with nc.Block() as block:
                @block.gpsimd
                def _(pool):
                    gathers(pool, [(table, src_i)], g.used if ex is not None else g.agg_ready, [(idx, rows)])

                @block.vector
                def _(dve):
                    nc.vector.memset(featT[:, :, N:] if loops else featT[:], 0.0).then_inc(g.added.sem, 1)
                    if loops:
                        dve.wait_ge(g.evicted.sem, g.evicted.at(NT))
                    if ex is not None:
                        nc.vector.memset(extra[:], 0.0).then_inc(g.added.sem, 1)
                        nc.vector.memset(msg[:], 1.0).then_inc(g.added.sem, 1)
                    dve.wait_ge(g.added.sem, g.added.at(zeroed))

                    def ready(n, i, j):
                        if ex is not None:
                            dve.wait_ge(gath[j].sem, gath[j].at(16 * i + 16))
                            nc.vector.tensor_tensor(msg[:, j % RING, 0:width].rearrange("p (f h) -> p f h", h=HEADS),
                                                    rows[:, j, :].rearrange("p (f h) -> p f h", h=HEADS),
                                                    ex[:, bass.ds(n, 1), :].to_broadcast([P, HROW, HEADS]),
                                                    ALU.mult).then_inc(g.used.sem, 1)
                        nc.vector.tensor_scalar(hot[:, j % RING, :], iota[:], dloc[:, bass.ds(n, 1)],
                                                weight[:, bass.ds(n, 1)] if weight is not None else None, ALU.is_equal,
                                                ALU.mult if weight is not None else ALU.bypass).then_inc(g.one_hot.sem, 1)

                    def add(n, j):
                        b = nc.vector.value_load(base_i[0:1, bass.ds(n, 1)], min_val=0, max_val=N - 1)
                        dve.wait_ge(g.agg_ready.sem, g.agg_ready.at(n + 1))
                        wait_added = g.added.at(zeroed + per * n)
                        dve.wait_ge(g.added.sem, wait_added)
                        f = featT[:, :, bass.ds(b, P)]
                        nc.vector.tensor_tensor(f, f, ps[:, j % RING, 0:KD * P].rearrange("p (k t) -> p k t", k=KD), ALU.add).then_inc(g.added.sem, 1)
                        if ex is not None:
                            e = extra[:, bass.ds(b, P)]
                            nc.vector.tensor_tensor(e, e, ps[0:EX, j % RING, KD * P:KD * P + P], ALU.add).then_inc(g.added.sem, 1)

                    ready(0, 0, 0)
                    with dve.Fori(0, NCH // GR) as i:
                        for j in range(GR):
                            ready(GR * i + j + 1, i + (j + 1) // GR, (j + 1) % GR)
                            add(GR * i + j, j)
                    for j in range(NCH % GR):
                        n = NCH - NCH % GR + j
                        if n + 1 < NCH:
                            ready(n + 1, NCH // GR, j + 1)
                        add(n, j)

                if loops:
                    @block.sync
                    def _(sp):
                        def body(i, first):
                            for j in range(RING):
                                if not first:
                                    sp.wait_ge(g.turned.sem, g.turned.at(RING * (i - 1) + j + 1))
                                sp.dma_start(stage[0:P, j, 0:D], table[bass.ds(P * RING * i + P * j, P), :]).then_inc(store[j].sem, 16)
                        rounds(sp, NT // RING, body)

                    @block.scalar
                    def _(act):
                        def body(i, first):
                            for j in range(RING):
                                n = RING * i + j
                                hold_act(g.turned, n + 1)
                                nc.scalar.copy(featT[:, :, bass.ds(P * n, P)],
                                               ps[:, j, 0:KD * P].rearrange("p (k t) -> p k t", k=KD)).then_inc(g.evicted.sem, 1)
                        rounds(act, NT // RING, body)

                @block.tensor
                def _(pe):
                    def turn(i, first):
                        for j in range(RING):
                            n = RING * i + j
                            pe.wait_ge(store[j].sem, store[j].at(16 * i + 16))
                            if not first:
                                pe.wait_ge(g.evicted.sem, g.evicted.at(n - RING + 1))
                            for k in range(KD):
                                mm = nc.tensor.transpose(ps[:, j, k * P:(k + 1) * P], stage[0:P, j, k * 128:(k + 1) * 128], ident[0:P, 0:P])
                            mm.then_inc(g.turned.sem, 1)
                    if loops:
                        rounds(pe, NT // RING, turn)
                        pe.wait_ge(g.evicted.sem, g.evicted.at(NT))

                    def body(n, i, j, first):
                        if ex is not None:
                            pe.wait_ge(g.used.sem, g.used.at(n + 1))
                        else:
                            pe.wait_ge(gath[j].sem, gath[j].at(16 * i + 16))
                        pe.wait_ge(g.one_hot.sem, g.one_hot.at(n + 1))
                        if not (first and j < RING):
                            pe.wait_ge(g.added.sem, g.added.at(zeroed + per * (n - RING + 1)))
                        for k in range(KD):
                            lhs = (msg[:, j % RING] if ex is not None else rows[:, j])[:, k * 128:(k + 1) * 128]
                            mm = nc.tensor.matmul(ps[:, j % RING, k * P:(k + 1) * P], lhs, hot[:, j % RING, :], start=True, stop=True)
                        if ex is not None:
                            lhs = msg[:, j % RING, D:D + EX]
                            mm = nc.tensor.matmul(ps[0:EX, j % RING, KD * P:KD * P + P], lhs, hot[:, j % RING, :], start=True, stop=True)
                        mm.then_inc(g.agg_ready.sem, 1)
                    for j in range(GR):
                        body(j, 0, j, True)
                    with pe.Fori(1, NCH // GR) as i:
                        for j in range(GR):
                            body(GR * i + j, i, j, False)
                    for j in range(NCH % GR):
                        body(NCH - NCH % GR + j, NCH // GR, j, False)
        gathers_passed(1)
        g.agg_ready.passed(NCH), g.one_hot.passed(NCH), g.added.passed(zeroed + per * NCH)
        if ex is not None:
            g.used.passed(NCH)
        if loops:
            g.turned.passed(NT), g.evicted.passed(NT)
            for s in store:
                s.passed(16 * NT // RING)

    def turn_back(extra_rows):
        def pe_ops(j, x):
            for k in range(KD):
                mm = nc.tensor.transpose(ps[0:P, j, k * 128:(k + 1) * 128], x[:, k, :], ident[:])
            if extra_rows:
                mm = nc.tensor.transpose(ps[0:P, j, D:D + EX], stage[0:EX, j, KD * P:KD * P + P], ident[0:EX, 0:EX])
            return mm
        return pe_ops

    def att_finish(extra, own):
        with ExitStack() as c:
            den = sb("den", [P, 2, HEADS], F32, c)
            deg = sb("deg", [P, 2, NT], F32, c)
            o = sb("att_o", [P, 2, D], F32, c)

            def use(dve, n, j, c0):
                ch = g.chain.sem
                by_head = lambda ap: ap.rearrange("p (f h) -> p f h", h=HEADS)
                w = own[:, bass.ds(n, 1), :]
                nc.vector.scalar_tensor_tensor(den[:, 0, :], ps[0:P, j, D:D + HEADS], 1e-10, tile_of(own, n), ALU.add, ALU.add).then_inc(ch, 1)
                nc.vector.tensor_copy(deg[:, 0, bass.ds(n, 1)], ps[0:P, j, D + HEADS:D + EX]).then_inc(ch, 1)
                nc.vector.tensor_tensor(by_head(o[:, 1, :]), by_head(tile_of(xn, n)), w.to_broadcast([P, HF, HEADS]), ALU.mult).then_inc(ch, 1)
                wait_chain(dve, c0 + 3)
                nc.vector.reciprocal(den[:, 1, :], den[:, 0, :]).then_inc(ch, 1)
                nc.vector.tensor_tensor(o[:, 1, :], o[:, 1, :], ps[0:P, j, 0:D], ALU.add).then_inc(ch, 1)
                wait_chain(dve, c0 + 5)
                nc.vector.tensor_tensor(o[:, 0, :].rearrange("p (h f) -> p f h", h=HEADS), by_head(o[:, 1, :]),
                                        den[:, 1, :].unsqueeze(1).to_broadcast([P, HF, HEADS]), ALU.mult).then_inc(ch, 1)
                wait_chain(dve, c0 + 6)
                nc.vector.tensor_tensor(tile_of(xres, n), tile_of(xres, n), o[:, 0, :], ALU.add).then_inc(ch, 1)

            tiles([], None, [], turn_back(True), use, 7, extra=extra)
            with nc.Block() as block:
                @block.vector
                def _(dve):
                    nc.vector.tensor_scalar(deg[:, 1, :], deg[:, 0, :], 1.0, None, ALU.add).then_inc(g.chain.sem, 1)
                    dve.wait_ge(g.act_step.sem, g.act_step.at(1))
                    nc.vector.reciprocal(dinv[:], deg[:, 0, :]).then_inc(g.chain.sem, 1)

                @block.scalar
                def _(act):
                    act.wait_ge(g.chain.sem, g.chain.at(1))
                    nc.scalar.activation(deg[:, 0, :], deg[:, 1, :], ACT.Sqrt).then_inc(g.act_step.sem, 1)
            g.chain.passed(2), g.act_step.passed(1)

    def sum_finish():
        with ExitStack() as c:
            w = sb("sum_w", [128, KD, D], F32, c)

            def use(dve, n, j, c0):
                nc.vector.tensor_tensor(tile_of(xres, n), tile_of(xres, n), ps[0:P, j, 0:D], ALU.add).then_inc(g.chain.sem, 1)
            tiles([(w[:], halves(io["L1_gnn_weight"]))], None, [], times(w, D), use, 1)

    def conv_finish(layer, table):
        with ExitStack() as c:
            raw = sb(f"conv_raw{layer}", [128, KD, D], F32, c)
            w = sb(f"conv_w{layer}", [128, KD, D], F32, c)
            b = sb(f"conv_b{layer}", [P, D], F32, c)
            h = sb(f"conv_h{layer}", [P, RING, D], F32, c)
            blocks = [(w[:, k, o * 128:(o + 1) * 128], raw[:, o, k * 128:(k + 1) * 128], 128) for o in range(KD) for k in range(KD)]

            def use(dve, n, j, c0):
                ch = g.chain.sem
                nc.vector.scalar_tensor_tensor(h[:, j, :], ps[0:P, j, 0:D], dinv[:, bass.ds(n, 1)], b[:], ALU.mult, ALU.add).then_inc(ch, 1)
                wait_chain(dve, c0 + 1)
                if table is not None:
                    nc.vector.tensor_scalar(h[:, j, :], h[:, j, :], 0.0, dinv[:, bass.ds(n, 1)], ALU.max, ALU.mult).then_inc(ch, 1)
                else:
                    nc.vector.tensor_tensor(tile_of(xres, n), tile_of(xres, n), h[:, j, :], ALU.add).then_inc(ch, 1)
            tiles([(raw[:], halves(io[f"L2_gnn_W{layer}"])), (b[:], io[f"L2_gnn_b{layer}"].partition_broadcast(P))],
                  None, blocks, times(w, D), use, 2,
                  sp_rows=(lambda n, j: [(table[bass.ds(P * n, P), :], h[:, j, :])]) if table is not None else None)

    def edge_project():
        with ExitStack() as c:
            w = sb("ep_w", [128, KD, 2 * D], F32, c)
            b = sb("ep_b", [P, 2 * D], F32, c)
            h = sb("ep_h", [P, RING, 2 * D], F32, c)

            def use(dve, n, j, c0):
                nc.vector.tensor_tensor(h[:, j, :], ps[0:P, j, :], b[:], ALU.add).then_inc(g.chain.sem, 1)
            tiles([(w[:, :, 0:D], halves(io["L3_gnn_W1"][0:D, :])), (w[:, :, D:2 * D], halves(io["L3_gnn_Wg"][0:D, :])),
                   (b[:, 0:D], io["L3_gnn_b1"].partition_broadcast(P)), (b[:, D:2 * D], io["L3_gnn_bg"].partition_broadcast(P))],
                  None, [], times(w, 2 * D), use, 1,
                  sp_rows=lambda n, j: [(t_edge[bass.ds(P * n, P), :], h[:, j, :])])

    def edge_gated():
        DE = 64
        with ExitStack() as c:
            rows = sb("eg_rows", [P, GR, 2 * D], F32, c)
            hot = sb("eg_hot", [P, RING, P], F32, c)
            ea = sb("eg_ea", [P, RING, DE], F32, c)
            eaT = sb("eg_eaT", [DE, RING, P], F32, c)
            w1 = sb("eg_w1", [DE, D], F32, c)
            wg = sb("eg_wg", [DE, D], F32, c)
            w2 = sb("eg_w2", [128, KD, D], F32, c)
            b2 = sb("eg_b2", [P, D], F32, c)
            rT = sb("eg_rT", [128, RING, KD, P], F32, c)
            gt = sb("eg_gate", [P, RING, D], F32, c)
            msg = sb("eg_msg", [P, RING, D], F32, c)
            TB, PB, GB, CB, AB = 0, 1, 3, 5, 6
            NL = 4

            def steps(eng, parts):
                top = max(l for l, _ in parts)
                for n in range(-top, 0):
                    for l, f in parts:
                        if n + l >= 0:
                            f(n + l, (n + l) // GR, (n + l) % GR, True)
                for j in range(GR):
                    for l, f in parts:
                        f(j + l, (j + l) // GR, (j + l) % GR, j + l < GR)
                with eng.Fori(1, NCH // GR) as i:
                    for j in range(GR):
                        for l, f in parts:
                            f(GR * i + j + l, i + (j + l) // GR, (j + l) % GR, False)
                for n in range(NCH - NCH % GR, NCH):
                    for l, f in parts:
                        if n + l < NCH:
                            f(n + l, (n + l) // GR, (n + l) % GR, False)

            with nc.Block() as block:
                @block.gpsimd
                def _(pool):
                    gathers(pool, [(t_edge, src_i)], g.gpre_done, [(idx, rows)])

                @block.sync
                def _(sp):
                    sp.dma_start(w1[:], io["L3_gnn_W1"][D:D + DE, :]).then_inc(g.loaded.sem, 16)
                    sp.dma_start(wg[:], io["L3_gnn_Wg"][D:D + DE, :]).then_inc(g.loaded.sem, 16)
                    sp.dma_start(w2[:], halves(io["L3_gnn_W2"])).then_inc(g.loaded.sem, 16)
                    sp.dma_start(b2[:], io["L3_gnn_b2"].partition_broadcast(P)).then_inc(g.loaded.sem, 16)

                    def body(i, first):
                        for j in range(RING):
                            n = RING * i + j
                            if not first:
                                sp.wait_ge(g.ea_turned.sem, g.ea_turned.at(n - RING + 1))
                            sp.dma_start(ea[:, j, :], io["edge_attr_64"][bass.ds(P * RING * i + P * j, P), :]).then_inc(store[j].sem, 16)
                    rounds(sp, NCH // RING, body)

                @block.tensor
                def _(pe):
                    pe.wait_ge(g.loaded.sem, g.loaded.at(16 * NL))

                    def turn(n, i, j, first):
                        s = j % RING
                        i5 = 2 * i + (j // RING)
                        if not (first and j < 1):
                            pe.wait_ge(g.eaT_ready.sem, g.eaT_ready.at(n))
                        hold_pe(store[s], 16 * i5 + 16)
                        nc.tensor.transpose(ps[0:DE, TB, 0:P], ea[:, s, :], ident[0:P, 0:P]).then_inc(g.ea_turned.sem, 1)

                    def pre(n, i, j, first):
                        s = j % RING
                        pe.wait_ge(gath[j].sem, gath[j].at(16 * i + 16))
                        pe.wait_ge(g.eaT_ready.sem, g.eaT_ready.at(n + 1))
                        if not (first and j < 2):
                            pe.wait_ge(g.relu_done.sem, g.relu_done.at(n - 1))
                            pe.wait_ge(g.gate_done.sem, g.gate_done.at(n - 1))
                        for k in range(KD):
                            o = ps[:, PB + j % 2, k * P:(k + 1) * P]
                            nc.tensor.matmul(o, rows[:, j, k * 128:(k + 1) * 128], ident[0:P, 0:P], start=True, stop=False)
                            nc.tensor.matmul(o, w1[:, k * 128:(k + 1) * 128], eaT[:, s, :], start=False, stop=True)
                        nc.tensor.matmul(ps[0:P, GB + j % 2, 0:D], eaT[:, s, :], wg[:], start=True, stop=True).then_inc(g.pre_ready.sem, 1)

                    def core(n, i, j, first):
                        pe.wait_ge(g.relu_done.sem, g.relu_done.at(n + 1))
                        if not (first and j < 1):
                            pe.wait_ge(g.msg_done.sem, g.msg_done.at(2 * n))
                        for k in range(KD):
                            mm = nc.tensor.matmul(ps[0:P, CB, 0:D], rT[:, j % RING, k, :], w2[:, k, :], start=(k == 0), stop=(k == KD - 1))
                        mm.then_inc(g.core_ready.sem, 1)

                    def agg(n, i, j, first):
                        pe.wait_ge(g.msg_done.sem, g.msg_done.at(2 * n + 2))
                        pe.wait_ge(g.one_hot.sem, g.one_hot.at(n + 1))
                        if not (first and j < 2):
                            pe.wait_ge(g.added.sem, g.added.at(n))
                        for k in range(KD):
                            mm = nc.tensor.matmul(ps[:, AB + j % 2, k * P:(k + 1) * P], msg[:, j % RING, k * 128:(k + 1) * 128], hot[:, j % RING, :], start=True, stop=True)
                        mm.then_inc(g.agg_ready.sem, 1)
                    steps(pe, [(3, turn), (2, pre), (1, core), (0, agg)])

                @block.scalar
                def _(act):
                    def attr(n, i, j, first):
                        hold_act(g.ea_turned, n + 1)
                        if not (first and j < RING):
                            hold_act(g.pre_ready, n - RING + 1)
                        nc.scalar.copy(eaT[:, j % RING, :], ps[0:DE, TB, 0:P]).then_inc(g.eaT_ready.sem, 1)

                    def relu(n, i, j, first):
                        hold_act(g.pre_ready, n + 1)
                        if not (first and j < RING):
                            hold_act(g.core_ready, n - RING + 1)
                        nc.scalar.activation(rT[:, j % RING], ps[:, PB + j % 2, 0:KD * P].rearrange("p (k t) -> p k t", k=KD), ACT.Relu).then_inc(g.relu_done.sem, 1)

                    def gate(n, i, j, first):
                        hold_act(g.gpre_done, n + 1)
                        nc.scalar.activation(gt[:, j % RING, :], gt[:, j % RING, :], ACT.Sigmoid).then_inc(g.gate_done.sem, 1)
                    steps(act, [(2, attr), (1, relu), (1, gate)])

                @block.vector
                def _(dve):
                    nc.vector.memset(featT[:], 0.0).then_inc(g.added.sem, 1)
                    dve.wait_ge(g.loaded.sem, g.loaded.at(16 * NL))

                    def gpre(n, i, j, first):
                        s = j % RING
                        dve.wait_ge(g.pre_ready.sem, g.pre_ready.at(n + 1))
                        if not (first and j < RING):
                            dve.wait_ge(g.msg_done.sem, g.msg_done.at(2 * (n - RING + 1)))
                        nc.vector.tensor_tensor(gt[:, s, :], ps[0:P, GB + j % 2, 0:D], rows[:, j, D:2 * D], ALU.add).then_inc(g.gpre_done.sem, 1)
                        if not (first and j < RING):
                            dve.wait_ge(g.agg_ready.sem, g.agg_ready.at(n - RING + 1))
                        nc.vector.tensor_scalar(hot[:, s, :], iota[:], dloc[:, bass.ds(n, 1)], None, ALU.is_equal).then_inc(g.one_hot.sem, 1)

                    def message(n, i, j, first):
                        s = j % RING
                        dve.wait_ge(g.core_ready.sem, g.core_ready.at(n + 1))
                        if not (first and j < RING):
                            dve.wait_ge(g.agg_ready.sem, g.agg_ready.at(n - RING + 1))
                        nc.vector.tensor_tensor(msg[:, s, :], ps[0:P, CB, 0:D], b2[:], ALU.add).then_inc(g.msg_done.sem, 1)
                        dve.wait_ge(g.msg_done.sem, g.msg_done.at(2 * n + 1))
                        dve.wait_ge(g.gate_done.sem, g.gate_done.at(n + 1))
                        nc.vector.tensor_tensor(msg[:, s, :], msg[:, s, :], gt[:, s, :], ALU.mult).then_inc(g.msg_done.sem, 1)

                    def add(n, i, j, first):
                        b = nc.vector.value_load(base_i[0:1, bass.ds(n, 1)], min_val=0, max_val=N - 1)
                        dve.wait_ge(g.agg_ready.sem, g.agg_ready.at(n + 1))
                        dve.wait_ge(g.added.sem, g.added.at(n + 1))
                        f = featT[:, :, bass.ds(b, P)]
                        nc.vector.tensor_tensor(f, f, ps[:, AB + j % 2, 0:KD * P].rearrange("p (k t) -> p k t", k=KD), ALU.add).then_inc(g.added.sem, 1)
                    steps(dve, [(2, gpre), (1, message), (0, add)])
        gathers_passed(1)
        for s in store:
            s.passed(16 * NCH // RING)
        g.loaded.passed(16 * NL), g.added.passed(1 + NCH), g.msg_done.passed(2 * NCH)
        for s in (g.ea_turned, g.eaT_ready, g.pre_ready, g.relu_done, g.gpre_done, g.gate_done, g.core_ready, g.one_hot, g.agg_ready):
            s.passed(NCH)

    def sums_to_xn():
        def use(dve, n, j, c0):
            nc.vector.tensor_tensor(tile_of(xn, n), tile_of(xn, n), ps[0:P, j, 0:D], ALU.add).then_inc(g.chain.sem, 1)
        tiles([], None, [], turn_back(False), use, 1)

    def choose(tag, L, T, E, softmaxes, W, picks, iota_e, work, wT, load_scale=None, index_out=None):
        ch = g.chain
        marks = []
        t3 = lambda k: work[:, k, 0:T * E].rearrange("p (t e) -> p t e", e=E)
        v2 = lambda k: work[:, k, 0:T]
        bc = lambda ap: ap.unsqueeze(2).to_broadcast([P, T, E])
        ie = iota_e[:, 0:E].unsqueeze(1).to_broadcast([P, T, E])
        groups = [list(range(q, min(q + BT, NT))) for q in range(0, NT, BT)] if wT is not None else []
        with nc.Block() as block:
            count = [0]

            @block.vector
            def _(dve):
                def link(ins):
                    count[0] += 1
                    ins.then_inc(ch.sem, 1)
                    dve.wait_ge(ch.sem, ch.at(count[0]))

                def exp_of(ap):
                    marks.append((count[0], ap))
                    dve.wait_ge(g.act_step.sem, g.act_step.at(len(marks)))

                def softmax(a):
                    link(nc.vector.tensor_reduce(v2(6), a, X, ALU.max))
                    link(nc.vector.tensor_tensor(a, a, bc(v2(6)), ALU.subtract))
                    exp_of(a)
                    link(nc.vector.tensor_reduce(v2(6), a, X, ALU.add))
                    link(nc.vector.reciprocal(v2(7), v2(6)))
                    link(nc.vector.tensor_tensor(a, a, bc(v2(7)), ALU.mult))

                a = L
                if softmaxes >= 1:
                    softmax(a)
                if softmaxes == 2:
                    cap, per_load = load_scale
                    link(nc.vector.tensor_scalar(t3(0), a, per_load, None, ALU.mult))
                    link(nc.vector.reciprocal(t3(1), t3(0)))
                    link(nc.vector.tensor_scalar(t3(1), t3(1), cap, -1.0, ALU.mult, ALU.add))
                    link(nc.vector.tensor_scalar(t3(0), t3(0), cap, None, ALU.is_gt))
                    link(nc.vector.tensor_scalar(t3(1), t3(1), 3e38, None, ALU.min))
                    link(nc.vector.tensor_tensor(t3(1), t3(1), t3(0), ALU.mult))
                    link(nc.vector.tensor_scalar(t3(1), t3(1), 1.0, None, ALU.add))
                    link(nc.vector.tensor_tensor(a, a, t3(1), ALU.mult))
                    softmax(a)
                for k in range(picks):
                    link(nc.vector.tensor_reduce(v2(8 + k), a, X, ALU.max))
                    link(nc.vector.tensor_tensor(t3(0), a, bc(v2(8 + k)), ALU.not_equal))
                    link(nc.vector.scalar_tensor_tensor(t3(0), t3(0), 1024.0, ie, ALU.mult, ALU.add) if T == 1 else
                         nc.vector.tensor_scalar(t3(0), t3(0), 1024.0, None, ALU.mult))
                    if T > 1:
                        link(nc.vector.tensor_tensor(t3(0), t3(0), ie, ALU.add))
                    link(nc.vector.tensor_reduce(v2(6), t3(0), X, ALU.min))
                    if index_out is not None:
                        link(nc.vector.tensor_copy(index_out[0:1, k:k + 1], v2(6)[0:1, :]))
                    link(nc.vector.tensor_tensor(t3(2 + k), ie, bc(v2(6)), ALU.is_equal))
                    if k + 1 < picks:
                        link(nc.vector.tensor_scalar(t3(1), t3(2 + k), -3e38, None, ALU.mult))
                        link(nc.vector.tensor_tensor(t3(4), t3(2 + k), a, ALU.mult))
                        link(nc.vector.tensor_tensor(a, a, t3(4), ALU.subtract))
                        link(nc.vector.tensor_tensor(a, a, t3(1), ALU.add))
                if picks == 2:
                    link(nc.vector.tensor_tensor(v2(9), v2(9), v2(8), ALU.subtract))
                    exp_of(v2(9))
                    link(nc.vector.tensor_scalar(v2(6), v2(9), 1.0, None, ALU.add))
                    link(nc.vector.reciprocal(v2(6), v2(6)))
                    link(nc.vector.tensor_tensor(v2(7), v2(9), v2(6), ALU.mult))
                    if index_out is None:
                        link(nc.vector.tensor_tensor(t3(2), t3(2), bc(v2(6)), ALU.mult))
                        link(nc.vector.tensor_tensor(t3(3), t3(3), bc(v2(7)), ALU.mult))
                        link(nc.vector.tensor_tensor(W, t3(2), t3(3), ALU.add))
                    else:
                        for k in range(2):
                            link(nc.vector.tensor_copy(W[:, :, k], v2(6 + k).to_broadcast([P, NT])))
                else:
                    link(nc.vector.tensor_copy(W, t3(2)))
                for q, ts in enumerate(groups):
                    dve.wait_ge(g.turned.sem, g.turned.at(q + 1))
                    nc.vector.tensor_copy(wT[:, ts[0] * P:(ts[-1] + 1) * P], ps[0:wT.shape[0], q, 0:len(ts) * P]).then_inc(ch.sem, 1)

            @block.scalar
            def _(act):
                for at, ap in marks:
                    act.wait_ge(ch.sem, ch.at(at))
                    nc.scalar.activation(ap, ap, ACT.Exp).then_inc(g.act_step.sem, 1)

            @block.tensor
            def _(pe):
                if groups:
                    pe.wait_ge(ch.sem, ch.at(count[0]))
                for q, ts in enumerate(groups):
                    for s, t in enumerate(ts):
                        mm = nc.tensor.transpose(ps[0:wT.shape[0], q, s * P:(s + 1) * P], W[:, t, :], ident[0:P, 0:P])
                    mm.then_inc(g.turned.sem, 1)
        ch.passed(count[0] + len(groups)), g.act_step.passed(len(marks)), g.turned.passed(len(groups))

    def expert_index(iota_e):
        with nc.Block() as block:
            @block.gpsimd
            def _(pool):
                nc.gpsimd.iota(iota_e[:], [[1, 32]], base=0, channel_multiplier=0, allow_small_or_imprecise_dtypes=True)

    def experts(tag, E, load, first_layer, bias_ap, func, second, per_tile, wT, b2, w_ready=None, mask=None, mid=None, W=None, acc=None, late_bias=False):
        F = 4
        FB = F - 2 if mid is not None else 0
        EY = E + 1 if mask is None else 1
        ew_ = wT.shape[0]
        we = lambda e: e if mask is None else 0
        with ExitStack() as c:
            hid = sb(tag + "_hid", [128, 2, F, BT * P], F32, c)
            wts = sb(tag + "_wts", [ew_, BT * P], F32, c)
            with nc.Block() as block:
                @block.sync
                def _(sp):
                    load(sp)

                def counts(b, nt):
                    return b * F * E, b * EY * BT

                def blocks(eng, body):
                    body(0, BT, True)
                    with eng.Fori(1, NB) as b:
                        body(b, BT, False)
                    if NT % BT:
                        body(NB, NT % BT, False)

                @block.tensor
                def _(pe):
                    if late_bias:
                        pe.wait_ge(g.loaded.sem, g.loaded.at(16))

                    def body(b, nt, first):
                        h0, y0 = counts(b, nt)
                        cols = nt * P
                        tail = nt < BT
                        tok = lambda k: featT[:, k, bass.ds(b * BT * P, cols)]
                        pe.wait_ge(g.wt_staged.sem, g.wt_staged.at(b + 1))

                        def hidden(e, fs):
                            if first:
                                pe.wait_ge(wload[we(e)].sem, wload[we(e)].at(w_ready))
                            for f in fs:
                                n = h0 + e * F + f
                                if not (first and e == 0):
                                    hold_pe(g.hid_done, n - F + 1)
                                o = ps[:, f, 0:cols]
                                if mid is not None and f >= 2:
                                    if f == 2:
                                        pe.wait_ge(g.hid_done.sem, g.hid_done.at(h0 + e * F + 2))
                                    for k in range(KD):
                                        mm = nc.tensor.matmul(o, mid(e, f, k), hid[:, e % 2, k, 0:cols], start=(k == 0), stop=(k == KD - 1))
                                else:
                                    for k in range(KD):
                                        mm = nc.tensor.matmul(o, first_layer(e, f, k), tok(k), start=(k == 0), stop=(k == KD - 1 and mask is None))
                                    if mask is not None:
                                        mm = nc.tensor.matmul(o, mask[:, (e * F + f) * 128:(e * F + f + 1) * 128], wts[:, 0:cols], start=False, stop=True)
                                mm.then_inc(g.hid_ready.sem, 1)

                        def outputs(e):
                            if e < E:
                                pe.wait_ge(g.hid_done.sem, g.hid_done.at(h0 + (e + 1) * F))
                            for t in range(nt):
                                y = y0 + (e * nt + t if mask is None else t)
                                if e == 0 or mask is None:
                                    if tail:
                                        pe.wait_ge(g.y_done.sem, g.y_done.at(y))
                                    elif not (first and e == 0):
                                        hold_pe(g.y_done, y - BT + 1)
                                o = ps[0:P, F + t, 0:D]
                                if e < E:
                                    for f in range(FB, F):
                                        mm = nc.tensor.matmul(o, hid[:, e % 2, f, t * P:(t + 1) * P], second(e, f),
                                                              start=(f == FB and (mask is None or e == 0)), stop=(f == F - 1 and mask is None))
                                if (e == E and mask is None) or (mask is not None and e == E - 1):
                                    mm = nc.tensor.matmul(o, wts[:, t * P:(t + 1) * P], b2, start=mask is None, stop=True)
                                if mask is None or e == E - 1:
                                    mm.then_inc(g.y_ready.sem, 1)

                        if mid is None:
                            hidden(0, range(F))
                            for e in range(E):
                                if e + 1 < E:
                                    hidden(e + 1, range(F))
                                outputs(e)
                        else:
                            for s in range(E + 2):
                                if s < E:
                                    hidden(s, (0, 1))
                                if 1 <= s <= E:
                                    hidden(s - 1, (2, 3))
                                if s >= 2:
                                    outputs(s - 2)
                        if mask is None:
                            outputs(E)
                    blocks(pe, body)

                @block.scalar
                def _(act):
                    def body(b, nt, first):
                        h0, y0 = counts(b, nt)
                        cols = nt * P
                        if not first:
                            hold_act(g.y_ready, y0)
                        nc.scalar.copy(wts[:, 0:cols], wT[:, bass.ds(b * BT * P, cols)]).then_inc(g.wt_staged.sem, 1)

                        def chunk(e, f):
                            if first and f == 0 and bias_ap is not None:
                                act.wait_ge(wload[we(e)].sem, wload[we(e)].at(w_ready))
                            hold_act(g.hid_ready, h0 + e * F + f + 1)
                            if bias_ap is not None:
                                nc.scalar.activation(hid[:, e % 2, f, 0:cols], ps[:, f, 0:cols], func, bias=bias_ap(e, f)).then_inc(g.hid_done.sem, 1)
                            else:
                                nc.scalar.activation(hid[:, e % 2, f, 0:cols], ps[:, f, 0:cols], func).then_inc(g.hid_done.sem, 1)
                        if mid is None:
                            for e in range(E):
                                for f in range(F):
                                    chunk(e, f)
                        else:
                            for s in range(E + 1):
                                for f in (0, 1):
                                    if s < E:
                                        chunk(s, f)
                                for f in (2, 3):
                                    if s >= 1:
                                        chunk(s - 1, f)
                    blocks(act, body)

                @block.vector
                def _(dve):
                    def body(b, nt, first):
                        h0, y0 = counts(b, nt)
                        for e in range(EY):
                            for t in range(nt):
                                y = y0 + e * nt + t
                                n = BT * b + t
                                a = tile_of(acc, n)
                                dve.wait_ge(g.y_ready.sem, g.y_ready.at(y + 1))
                                if e > 0:
                                    dve.wait_ge(g.y_done.sem, g.y_done.at(y - nt + 1))
                                o = ps[0:P, F + t, 0:D]
                                if mask is not None:
                                    ins = nc.vector.scalar_tensor_tensor(a, o, 0.0, a, ALU.max, ALU.add)
                                elif e < E:
                                    ins = nc.vector.scalar_tensor_tensor(a, o, W[:, bass.ds(n, 1), e:e + 1].rearrange("p a e -> p (a e)"), a, ALU.mult, ALU.add)
                                else:
                                    ins = nc.vector.tensor_tensor(a, o, a, ALU.add)
                                ins.then_inc(g.y_done.sem, 1)
                    blocks(dve, body)
        tb = NT % BT
        g.hid_ready.passed(F * E * (NB + 1)), g.hid_done.passed(F * E * (NB + 1)), g.wt_staged.passed(NB + 1)
        g.y_ready.passed(EY * NT), g.y_done.passed(EY * NT)
        for e in range(E if mask is None else 1):
            wload[e].passed(w_ready)

    def ffn0():
        E = 8
        CAP = float(-((-N * 5) // (4 * E)))
        with ExitStack() as c:
            wr = sb("f0_wr", [128, KD, E], F32, c)
            br = sb("f0_br", [P, E], F32, c)
            mean = sb("f0_mean", [128, KD, P + 1], F32, c)
            L = sb("f0_L", [P, 1, E], F32, c)
            W = sb("f0_W", [P, NT, 2], F32, c)
            wT = sb("f0_wT", [2, N], F32, c)
            iota_e = sb("f0_iota", [P, 32], F32, c)
            work = sb("f0_work", [P, 10, NT], F32, c)
            pick = sb("f0_pick", [1, 2], I32, c)
            w1 = sb("f0_w1", [128, 2, KD, 512], F32, c)
            w2 = sb("f0_w2", [128, 2, 4, D], F32, c)
            b1 = sb("f0_b1", [128, 2, 4], F32, c)
            b2 = sb("f0_b2", [2, D], F32, c)
            b1rows = sb("f0_b1r", [4, 2, 128], F32, c)
            expert_index(iota_e)
            with nc.Block() as block:
                @block.sync
                def _(sp):
                    sp.dma_start(wr[:], halves(io["L0_ffn_Wr"])).then_inc(g.loaded.sem, 16)
                    sp.dma_start(br[:], io["L0_ffn_br"].partition_broadcast(P)).then_inc(g.loaded.sem, 16)

                @block.vector
                def _(dve):
                    nc.vector.tensor_reduce(mean[:, :, P:P + 1], featT[:, :, 0:N], X, ALU.add).then_inc(g.chain.sem, 1)
                    wait_chain(dve, 1)
                    nc.vector.tensor_scalar(mean[:, :, P:P + 1], mean[:, :, P:P + 1], 1.0 / N, None, ALU.mult).then_inc(g.chain.sem, 1)
                    wait_chain(dve, 2)
                    nc.vector.tensor_copy(mean[:, :, 0:P], mean[:, :, P:P + 1].to_broadcast([128, KD, P])).then_inc(g.chain.sem, 1)
                    dve.wait_ge(g.turned.sem, g.turned.at(1))
                    nc.vector.tensor_tensor(L[:, 0, :], ps[0:P, 0, 0:E], br[:], ALU.add).then_inc(g.chain.sem, 1)

                @block.tensor
                def _(pe):
                    pe.wait_ge(g.loaded.sem, g.loaded.at(32))
                    pe.wait_ge(g.chain.sem, g.chain.at(3))
                    for k in range(KD):
                        mm = nc.tensor.matmul(ps[0:P, 0, 0:E], mean[:, k, 0:P], wr[:, k, :], start=(k == 0), stop=(k == KD - 1))
                    mm.then_inc(g.turned.sem, 1)
            g.loaded.passed(32), g.chain.passed(4), g.turned.passed(1)
            choose("f0", L[:], 1, E, 2, W, 2, iota_e, work, wT, load_scale=(CAP, float(N)), index_out=pick)

            def load(sp):
                for j in range(2):
                    r = nc.sync.value_load(pick[0:1, j:j + 1], min_val=0, max_val=E - 1)
                    sp.dma_start(w1[:, j], io["L0_ffn_W1"][bass.ds(r, 1)].rearrange("e (k p) f -> p (e k) f", p=128)).then_inc(wload[j].sem, 16)
                    sp.dma_start(w2[:, j], io["L0_ffn_W2"][bass.ds(r, 1)].rearrange("e (k p) f -> p (e k) f", p=128)).then_inc(wload[j].sem, 16)
                    sp.dma_start(b1rows[:, j, :], io["L0_ffn_b1"][bass.ds(r, 1)].rearrange("e (f p) -> (e f) p", p=128)).then_inc(wload[j].sem, 16)
                    sp.dma_start(b2[j:j + 1, :], io["L0_ffn_b2"][bass.ds(r, 1)]).then_inc(wload[j].sem, 16)
            with nc.Block() as block:
                @block.sync
                def _(sp):
                    load(sp)

                @block.tensor
                def _(pe):
                    for j in range(2):
                        pe.wait_ge(wload[j].sem, wload[j].at(64))
                        mm = nc.tensor.transpose(ps[:, 0, 4 * j:4 * j + 4], b1rows[:, j, :], ident[0:4, 0:4])
                    mm.then_inc(g.turned.sem, 1)

                @block.vector
                def _(dve):
                    dve.wait_ge(g.turned.sem, g.turned.at(1))
                    nc.vector.tensor_copy(b1[:].rearrange("p e f -> p (e f)"), ps[:, 0, 0:8])
            g.turned.passed(1)
            experts("f0", 2, lambda sp: None, lambda e, f, k: w1[:, e, k, f * 128:(f + 1) * 128], lambda e, f: b1[:, e, f:f + 1],
                    ACT.Gelu, lambda e, f: w2[:, e, f, :], 2, wT, b2[:], w_ready=64, W=W, acc=xn)

    def biases(tag, b, rows, cols, dst):
        with ExitStack() as c:
            raw = sb(tag + "_bias_rows", [rows * cols, 128], F32, c)
            with nc.Block() as block:
                @block.sync
                def _(sp):
                    sp.dma_start(raw[:], b).then_inc(g.loaded.sem, 16)

                @block.tensor
                def _(pe):
                    pe.wait_ge(g.loaded.sem, g.loaded.at(16))
                    nc.tensor.transpose(ps[:, 0, 0:rows * cols], raw[:], ident[0:rows * cols, 0:rows * cols]).then_inc(g.turned.sem, 1)

                @block.vector
                def _(dve):
                    dve.wait_ge(g.turned.sem, g.turned.at(1))
                    nc.vector.tensor_copy(dst, ps[:, 0, 0:rows * cols])
            g.loaded.passed(16), g.turned.passed(1)

    def ffn1():
        E, RH = 6, 128
        with ExitStack() as c:
            W = sb("f1_W", [P, NT, E], F32, c)
            wT = sb("f1_wT", [E, N], F32, c)
            w = [sb(f"f1_w{i}", [128, E, KD, D], F32, c) for i in range(3)]
            b12 = sb("f1_b12", [128, 2, E, KD], F32, c)
            b3 = sb("f1_b3", [E, D], F32, c)
            for i in range(2):
                biases(f"f1_{i}", io[f"L1_ffn_expert_b{i + 1}"].rearrange("e (k p) -> (e k) p", p=128), E, KD, b12[:, i].rearrange("p e k -> p (e k)"))
            with ExitStack() as c2:
                rw1 = sb("f1_rw1", [128, KD, RH], F32, c2)
                rb1 = sb("f1_rb1", [RH, 1], F32, c2)
                rw2 = sb("f1_rw2", [RH, E], F32, c2)
                rb2 = sb("f1_rb2", [P, E], F32, c2)
                L = sb("f1_L", [P, NT, E], F32, c2)
                iota_e = sb("f1_iota", [P, 32], F32, c2)
                work = sb("f1_work", [P, 10, NT * E], F32, c2)
                rh = sb("f1_rh", [RH, RING, P], F32, c2)
                expert_index(iota_e)
                biases("f1_r", io["L1_ffn_router_b1"].rearrange("(a p) -> a p", a=1), 1, 1, rb1[:])
                with nc.Block() as block:
                    @block.sync
                    def _(sp):
                        sp.dma_start(rw1[:], halves(io["L1_ffn_router_w1"])).then_inc(g.loaded.sem, 16)
                        sp.dma_start(rw2[:], io["L1_ffn_router_w2"]).then_inc(g.loaded.sem, 16)
                        sp.dma_start(rb2[:], io["L1_ffn_router_b2"].partition_broadcast(P)).then_inc(g.loaded.sem, 16)

                    @block.tensor
                    def _(pe):
                        pe.wait_ge(g.loaded.sem, g.loaded.at(48))

                        def body(i, first):
                            for j in range(RING):
                                n = RING * i + j
                                if not first:
                                    hold_pe(g.staged, n - RING + 1)
                                    hold_pe(g.chain, n - RING + 1)
                                for k in range(KD):
                                    mm = nc.tensor.matmul(ps[:, j, 0:P], rw1[:, k, :], featT[:, k, bass.ds(P * n, P)], start=(k == 0), stop=(k == KD - 1))
                                mm.then_inc(g.hid_ready.sem, 1)
                                pe.wait_ge(g.staged.sem, g.staged.at(n + 1))
                                nc.tensor.matmul(ps[0:P, j, 256:256 + E], rh[:, j, :], rw2[:], start=True, stop=True).then_inc(g.tile_ready.sem, 1)
                        rounds(pe, NT // RING, body)

                    @block.scalar
                    def _(act):
                        def body(i, first):
                            for j in range(RING):
                                n = RING * i + j
                                hold_act(g.hid_ready, n + 1)
                                nc.scalar.activation(rh[:, j, :], ps[:, j, 0:P], ACT.Relu, bias=rb1[:]).then_inc(g.staged.sem, 1)
                        rounds(act, NT // RING, body)

                    @block.vector
                    def _(dve):
                        dve.wait_ge(g.loaded.sem, g.loaded.at(48))
                        def body(i, first):
                            for j in range(RING):
                                n = RING * i + j
                                dve.wait_ge(g.tile_ready.sem, g.tile_ready.at(n + 1))
                                nc.vector.tensor_tensor(tile_of(L, n), ps[0:P, j, 256:256 + E], rb2[:], ALU.add).then_inc(g.chain.sem, 1)
                        rounds(dve, NT // RING, body)
                g.loaded.passed(48)
                for s in (g.hid_ready, g.staged, g.tile_ready, g.chain):
                    s.passed(NT)
                choose("f1", L[:], NT, E, 1, W[:], 2, iota_e, work, wT)

            def load(sp):
                for e in range(E):
                    for i in range(3):
                        sp.dma_start(w[i][:, e], halves(io[f"L1_ffn_expert_w{i + 1}"][e])).then_inc(wload[e].sem, 16)
                    if e == 0:
                        sp.dma_start(b3[:], io["L1_ffn_expert_b3"]).then_inc(g.loaded.sem, 16)
            experts("f1", E, load, lambda e, f, k: w[0][:, e, k, f * 128:(f + 1) * 128], lambda e, f: b12[:, f // 2, e, f % 2:f % 2 + 1],
                    ACT.Relu, lambda e, f: w[2][:, e, f - 2, :], 2, wT, b3[:], w_ready=48, W=W, acc=xres, late_bias=True,
                    mid=lambda e, f, k: w[1][:, e, k, (f - 2) * 128:(f - 1) * 128])
            g.loaded.passed(16)

    def ffn2():
        E, H = 32, 64
        GRP = 4
        with ExitStack() as c:
            W = sb("f2_W", [P, NT, E], F32, c)
            wT = sb("f2_wT", [E, N], F32, c)
            w1 = sb("f2_w1", [128, KD, E, H], F32, c)
            w2 = sb("f2_w2", [128, E * H // 128, D], F32, c)
            b2 = sb("f2_b2", [E, D], F32, c)
            mask = sb("f2_mask", [E, E * H], F32, c)
            with ExitStack() as c2:
                raw = sb("f2_rw", [E, D], F32, c2)
                rw = sb("f2_rwT", [128, KD, E], F32, c2)
                rb = sb("f2_rb", [P, E], F32, c2)
                L = sb("f2_L", [P, NT, E], F32, c2)
                iota_e = sb("f2_iota", [P, 32], F32, c2)
                work = sb("f2_work", [P, 10, NT * E], F32, c2)
                b1row = sb("f2_b1", [E, E * H], F32, c2)
                expert_index(iota_e)

                def use(dve, n, j, c0):
                    nc.vector.tensor_tensor(tile_of(L, n), ps[0:P, j, 0:E], rb[:], ALU.add).then_inc(g.chain.sem, 1)
                tiles([(raw[:], io["L2_ffn_router_w"]), (rb[:], io["L2_ffn_router_b"].partition_broadcast(P)),
                       (b1row[:], io["L2_ffn_b1"].rearrange("e h -> (e h)").partition_broadcast(E))],
                      None, [(rw[:, k, :], raw[:, k * 128:(k + 1) * 128], E) for k in range(KD)], times(rw, E), use, 1)
                with nc.Block() as block:
                    @block.gpsimd
                    def _(pool):
                        nc.gpsimd.affine_select(out=mask[:], in_=b1row[:], pattern=[[1, E * H]], compare_op=ALU.is_ge, fill=MASKED,
                                                base=0, channel_multiplier=-H).then_inc(g.pool_step.sem, 1)
                        pool.wait_ge(g.pool_step.sem, g.pool_step.at(1))
                        nc.gpsimd.affine_select(out=mask[:], in_=mask[:], pattern=[[-1, E * H]], compare_op=ALU.is_ge, fill=MASKED,
                                                base=H - 1, channel_multiplier=H)
                g.pool_step.passed(1)
                choose("f2", L[:], NT, E, 0, W[:], 1, iota_e, work, wT)

            def load(sp):
                sp.dma_start(w1[:, 0], io["L2_ffn_W1"][:, 0:128, :].rearrange("e p h -> p e h")).then_inc(wload[0].sem, 16)
                sp.dma_start(w1[:, 1], io["L2_ffn_W1"][:, 128:256, :].rearrange("e p h -> p e h")).then_inc(wload[0].sem, 16)
                sp.dma_start(w2[:], io["L2_ffn_W2"].rearrange("e h d -> (e h) d").rearrange("(c p) d -> p c d", p=128)).then_inc(wload[0].sem, 16)
                sp.dma_start(b2[:], io["L2_ffn_b2"]).then_inc(wload[0].sem, 16)
            w1f = [w1[:, k].rearrange("p e h -> p (e h)") for k in range(KD)]
            experts("f2", GRP, load, lambda e, f, k: w1f[k][:, (e * 4 + f) * 128:(e * 4 + f + 1) * 128], None, ACT.Relu,
                    lambda e, f: w2[:, e * 4 + f, :], 1, wT, b2[:], w_ready=64, mask=mask, acc=xres)

    def ffn3():
        E = 8
        with ExitStack() as c:
            W = sb("f3_W", [P, NT, E], F32, c)
            wT = sb("f3_wT", [E, N], F32, c)
            b1 = sb("f3_b1", [128, E, 4], F32, c)
            b2 = sb("f3_b2", [E, D], F32, c)
            biases("f3", io["L3_ffn_b1"].rearrange("e (f p) -> (e f) p", p=128), E, 4, b1[:].rearrange("p e f -> p (e f)"))
            with ExitStack() as c2:
                wr = sb("f3_wr", [128, KD, E], F32, c2)
                br = sb("f3_br", [P, E], F32, c2)
                L = sb("f3_L", [P, NT, E], F32, c2)
                iota_e = sb("f3_iota", [P, 32], F32, c2)
                work = sb("f3_work", [P, 10, NT * E], F32, c2)
                expert_index(iota_e)

                def use(dve, n, j, c0):
                    nc.vector.tensor_tensor(tile_of(L, n), ps[0:P, j, 0:E], br[:], ALU.add).then_inc(g.chain.sem, 1)
                tiles([(wr[:], halves(io["L3_ffn_Wr"])), (br[:], io["L3_ffn_br"].partition_broadcast(P))], None, [], times(wr, E), use, 1)
                choose("f3", L[:], NT, E, 0, W[:], 2, iota_e, work, wT)
            w1 = sb("f3_w1", [128, E, KD, 512], F32, c)
            w2 = sb("f3_w2", [128, E, 4, D], F32, c)

            def load(sp):
                for e in range(E):
                    sp.dma_start(w1[:, e], halves(io["L3_ffn_W1"][e])).then_inc(wload[e].sem, 16)
                    sp.dma_start(w2[:, e], halves(io["L3_ffn_W2"][e])).then_inc(wload[e].sem, 16)
                    if e == 0:
                        sp.dma_start(b2[:], io["L3_ffn_b2"]).then_inc(g.loaded.sem, 16)
            experts("f3", E, load, lambda e, f, k: w1[:, e, k, f * 128:(f + 1) * 128], lambda e, f: b1[:, e, f:f + 1], ACT.Gelu,
                    lambda e, f: w2[:, e, f, :], 2, wT, b2[:], w_ready=32, W=W, acc=xres, late_bias=True)
            g.loaded.passed(16)

    def attention():
        with ExitStack() as c:
            ex = sb("ex", [P, NCH, HEADS], F32, c)
            extra = sb("extra", [EX, N + P], F32, c)
            own = sb("own", [P, NT, HEADS], F32, c)
            att_project(own)
            att_weights(ex, own)
            edge_pass("att", t_att, ex=ex, extra=extra)
            att_finish(extra, own)

    stages = [
        lambda: (prepare(), normalize("n0", xres, to_featT=True), attention()),
        lambda: (normalize("n1", xres, to_xn=True, to_featT=True), ffn0(),
                 normalize("n2", xn, gamma=io["L0_ffn_gamma"], beta=io["L0_ffn_beta"], add_to_x=True)),
        lambda: (normalize("n3", xres, table=t_row), edge_pass("sum", t_row, weight=ew), sum_finish()),
        lambda: (normalize("n4", xres, to_featT=True), ffn1()),
        lambda: (normalize("n5", xres, table=t_row, scale=dinv), edge_pass("c1", t_row, loops=True), conv_finish(1, t_row2),
                 edge_pass("c2", t_row2, loops=True), conv_finish(2, t_row), edge_pass("c3", t_row, loops=True), conv_finish(3, None)),
        lambda: (normalize("n6", xres, to_featT=True), ffn2()),
        lambda: (normalize("n7", xres, to_xn=True, to_featT=True), edge_project(), edge_gated(), sums_to_xn(),
                 normalize("n8", xn, gamma=io["L3_gnn_gamma"], beta=io["L3_gnn_beta"], add_to_x=True)),
        lambda: (normalize("n9", xres, to_xn=True),
                 normalize("n10", xn, gamma=io["L3_ffn_gamma"], beta=io["L3_ffn_beta"], to_featT=True), ffn3()),
    ]
    for s in stages[:stop]:
        s()
    with nc.Block() as block:
        @block.gpsimd
        def _(pool):
            pool.dma_start(out.rearrange("(t p) d -> p t d", p=P), xres[:]).then_inc(g.stored.sem, 16)
            pool.wait_ge(g.stored.sem, g.stored.at(16))


_INS = ["x", "src", "dst", "edge_attr_64", "edge_weight", "L0_gnn_W", "L0_gnn_b", "L0_gnn_a_src", "L0_gnn_a_trg", "L0_ffn_Wr",
        "L0_ffn_br", "L0_ffn_W1", "L0_ffn_b1", "L0_ffn_W2", "L0_ffn_b2", "L0_ffn_gamma", "L0_ffn_beta", "L1_gnn_weight",
        "L1_ffn_router_w1", "L1_ffn_router_b1", "L1_ffn_router_w2", "L1_ffn_router_b2", "L1_ffn_expert_w1", "L1_ffn_expert_b1",
        "L1_ffn_expert_w2", "L1_ffn_expert_b2", "L1_ffn_expert_w3", "L1_ffn_expert_b3", "L2_gnn_W1", "L2_gnn_b1", "L2_gnn_W2",
        "L2_gnn_b2", "L2_gnn_W3", "L2_gnn_b3", "L2_ffn_router_w", "L2_ffn_router_b", "L2_ffn_W1", "L2_ffn_b1", "L2_ffn_W2",
        "L2_ffn_b2", "L3_gnn_W1", "L3_gnn_b1", "L3_gnn_W2", "L3_gnn_b2", "L3_gnn_Wg", "L3_gnn_bg", "L3_gnn_gamma", "L3_gnn_beta",
        "L3_ffn_gamma", "L3_ffn_beta", "L3_ffn_Wr", "L3_ffn_br", "L3_ffn_W1", "L3_ffn_b1", "L3_ffn_W2", "L3_ffn_b2"]
STOP = 99


def kernel(**inputs):
    import numpy as _np
    import concourse.bacc as _bacc
    from concourse import mybir as _mybir
    from concourse.bass_utils import run_bass_kernel_spmd as _run

    nc = _bacc.Bacc("TRN2", target_bir_lowering=False, num_devices=1)
    arrays, io = {}, {}
    for name in _INS:
        a = _np.ascontiguousarray(inputs[name])
        arrays["in_" + name] = a
        io[name] = nc.dram_tensor("in_" + name, a.shape, _mybir.dt.from_np(a.dtype), kind="ExternalInput").ap()
    out = nc.dram_tensor("out_x", (N, D), F32, kind="ExternalOutput").ap()
    build(nc, io, out, STOP)
    r = _run(nc, [arrays], core_ids=[0])
    return r.results[0]["out_x"]
```

```python
from contextlib import ExitStack

import concourse.bass as bass
from concourse import mybir

F32 = mybir.dt.float32
I32 = mybir.dt.int32
ALU = mybir.AluOpType
ACT = mybir.ActivationFunctionType
X = mybir.AxisListType.X
RMAX = bass.bass_isa.ReduceOp.max

P = 125
NT = 25
N = P * NT
NCH = 425
D = 256
KD = D // 128
RING = 5
LOT = 8
GR = 15
HEADS, HF = 8, 32
AROW = D + HEADS
EPS = 1e-5
BT = 4
NB = NT // BT
EX = HEADS + 1
MASKED = -1e38


class Signal:

    def __init__(self, sem):
        self.sem = sem
        self.base = 0

    def at(self, n):
        return n + self.base

    def passed(self, n):
        self.base += n


class Signals:

    def __init__(self, sig):
        self.loaded = sig("loaded")
        self.chain = sig("chain")
        self.act_step = sig("act_step")
        self.pe_step = sig("pe_step")
        self.pool_step = sig("pool_step")
        self.gate_pool = sig("gate_pool")
        self.gate_act = sig("gate_act")
        self.gate_pe = sig("gate_pe")
        self.rows_ready = sig("rows_ready")
        self.turned = sig("turned")
        self.evicted = sig("evicted")
        self.xn_copied = sig("xn_copied")
        self.stored = sig("stored")
        self.used = sig("used")
        self.one_hot = sig("one_hot")
        self.agg_ready = sig("agg_ready")
        self.added = sig("added")
        self.staged = sig("staged")
        self.tile_ready = sig("tile_ready")
        self.hid_ready = sig("hid_ready")
        self.hid_done = sig("hid_done")
        self.y_ready = sig("y_ready")
        self.y_done = sig("y_done")
        self.wt_staged = sig("wt_staged")
        self.ea_turned = sig("ea_turned")
        self.eaT_ready = sig("eaT_ready")
        self.pre_ready = sig("pre_ready")
        self.relu_done = sig("relu_done")
        self.gpre_done = sig("gpre_done")
        self.gate_done = sig("gate_done")
        self.core_ready = sig("core_ready")
        self.msg_done = sig("msg_done")


class Carver:

    def __init__(self, flat):
        self.flat = flat
        self.used = 0

    def take(self, partitions, columns):
        self.used += columns
        return self.flat[0:partitions, self.used - columns:self.used]


def rounds(eng, count, body):
    body(0, True)
    with eng.Fori(1, count) as i:
        body(i, False)


def build(nc, io, out, stop=99):
    with ExitStack() as ctx:
        build_in(nc, io, out, ctx, stop)


def build_in(nc, io, out, ctx, stop):
    def sb(name, shape, dt=F32, c=ctx):
        return c.enter_context(nc.sbuf_tensor(name, shape, dt))

    def sig(name):
        return Signal(ctx.enter_context(nc.semaphore(name)))

    xres = sb("xres", [P, NT, D])
    xn = sb("xn", [P, NT, D])
    featT = sb("featT", [128, KD, N + P])
    stage = sb("stage", [128, RING, 512])
    ident = sb("ident", [128, 128])
    iota = sb("iota", [P, P])
    ones = sb("ones", [128, 128])
    row0 = sb("row0", [P, P])
    src_i = sb("src_i", [P, NCH], I32)
    dloc = sb("dloc", [P, NCH])
    ew = sb("ew", [P, NCH])
    base_i = sb("base_i", [1, NCH // RING, LOT], I32)
    dinv = sb("dinv", [P, NT])
    idx = sb("idx", [P, 4 * RING], I32)
    stats = sb("stats", [P, NT, 6])
    small = sb("small", [P, 8, NT])
    ps = ctx.enter_context(nc.psum_tensor("ps", [128, 8, 512], F32))

    g = Signals(sig)
    gath = [sig(f"gathered{j}") for j in range(4 * RING)]
    tgt_in = [sig(f"targets{h}") for h in range(4)]
    store = [sig(f"row_store{j}") for j in range(RING)]
    wload = [sig(f"weights{e}") for e in range(8)]

    def hold(eng, ns, gate, s, count):
        eng.wait_ge(s.sem, s.at(count))
        ns.sem_inc(gate.sem)

    def hold_act(s, count):
        hold(nc.scalar, nc.scalar, g.gate_act, s, count)

    def hold_pool(s, count):
        hold(nc.gpsimd, nc.gpsimd, g.gate_pool, s, count)

    def hold_pe(s, count):
        hold(nc.tensor, nc.tensor, g.gate_pe, s, count)

    reads = [0]

    def starts(eng, ns, m):
        reads[0] += 1
        regs = [eng.alloc_register(f"window{reads[0]}_{r}") for r in range(RING)]
        ns.load(regs, base_i[0:1, bass.ds(m, 1), 0:RING].rearrange("p a r -> p (a r)"))
        return [ns.snap(r, donate=True, min_val=0, max_val=N - 1) for r in regs]

    def dram(name, shape):
        return nc.dram_tensor(name, shape, F32).ap()

    t_att = dram("t_att", [N, AROW])
    t_tgt = dram("t_tgt", [N + P, 2 * HEADS])
    t_row = dram("t_row", [N, D])
    t_row2 = dram("t_row2", [N, D])
    t_edge = dram("t_edge", [N, 2 * D])
    TSMAX = max(2 * NT + 8, NT + 32)
    t_disp = dram("t_disp", [TSMAX * P, D])
    t_back = dram("t_back", [TSMAX * P, D])

    def prepare():
        with ExitStack() as c:
            rows = 85
            raw_i = sb("raw_i", [rows, 2, RING, P], I32, c)
            raw_f = sb("raw_f", [rows, 3, RING, P], F32, c)
            dst_f = sb("dst_f", [P, NCH], F32, c)
            with nc.Block() as block:
                @block.sync
                def _(sp):
                    for a, t in enumerate((io["src"], io["dst"])):
                        sp.dma_start(raw_i[:, a], t.rearrange("(r q p) -> q r p", q=rows, p=P)).then_inc(g.loaded.sem, 16)
                    sp.dma_start(raw_f[:, 2], io["edge_weight"].rearrange("(r q p) -> q r p", q=rows, p=P)).then_inc(g.loaded.sem, 16)

                @block.gpsimd
                def _(pool):
                    pool.dma_start(xres[:], io["x"].rearrange("(t p) d -> p t d", p=P)).then_inc(g.stored.sem, 16)
                    nc.gpsimd.iota(iota[:], [[1, P]], base=0, channel_multiplier=0,
                                   allow_small_or_imprecise_dtypes=True).then_inc(g.pool_step.sem, 1)
                    nc.gpsimd.memset(ones[:], 1.0).then_inc(g.pool_step.sem, 1)
                    pool.wait_ge(g.pool_step.sem, 2)
                    nc.gpsimd.affine_select(out=ident[:], in_=ones[:], pattern=[[-1, 128]], compare_op=ALU.is_equal,
                                            fill=0.0, base=0, channel_multiplier=1).then_inc(g.pool_step.sem, 1)
                    nc.gpsimd.affine_select(out=row0[:], in_=ones[0:P, 0:P], pattern=[[0, P]], compare_op=ALU.is_equal,
                                            fill=0.0, base=0, channel_multiplier=1).then_inc(g.pool_step.sem, 1)
                    pool.wait_ge(g.stored.sem, 16)

                @block.vector
                def _(dve):
                    dve.wait_ge(g.loaded.sem, 48)
                    nc.vector.tensor_copy(raw_f[:, 0:2], raw_i[:]).then_inc(g.chain.sem, 1)
                    for a in range(3):
                        dve.wait_ge(g.turned.sem, a + 1)
                        if a == 0:
                            nc.vector.tensor_copy(src_i[:], ps[0:P, 0, 0:NCH]).then_inc(g.chain.sem, 1)
                        elif a == 1:
                            nc.vector.tensor_copy(dst_f[:], ps[0:P, 1, 0:NCH]).then_inc(g.chain.sem, 1)
                            nc.vector.tensor_copy(base_i[:, :, 0:RING], ps[0:1, 1, 0:NCH].rearrange("p (l r) -> p l r", r=RING)).then_inc(g.chain.sem, 1)
                        else:
                            nc.vector.tensor_copy(ew[:], ps[0:P, 2, 0:NCH]).then_inc(g.chain.sem, 1)
                    dve.wait_ge(g.turned.sem, 4)
                    nc.vector.tensor_tensor(dloc[:], dst_f[:], ps[0:P, 3, 0:NCH], ALU.subtract).then_inc(g.chain.sem, 1)

                @block.tensor
                def _(pe):
                    pe.wait_ge(g.pool_step.sem, 4)
                    pe.wait_ge(g.chain.sem, 1)
                    for a in range(3):
                        for r in range(RING):
                            mm = nc.tensor.transpose(ps[0:P, a, r * rows:(r + 1) * rows], raw_f[:, a, r, :], ident[0:rows, 0:rows])
                        mm.then_inc(g.turned.sem, 1)
                    pe.wait_ge(g.chain.sem, 3)
                    nc.tensor.matmul(ps[0:P, 3, 0:NCH], row0[:], dst_f[:], start=True, stop=True).then_inc(g.turned.sem, 1)
        g.loaded.passed(48), g.stored.passed(16), g.pool_step.passed(4), g.chain.passed(6), g.turned.passed(4)

    def normalize(tag, src, gamma=None, beta=None, to_xn=False, to_featT=False, table=None, scale=None, add_to_x=False):
        with ExitStack() as c:
            gb = sb(tag + "_gb", [P, 2, D], F32, c) if gamma is not None else None
            nper = 1 + (2 if gamma is not None else 0) + (1 if scale is not None else 0)
            mean2, diff, m2, var, sd, rstd, mean = (small[:, k, :] for k in range(7))
            PRE = NT + 6
            PER = nper - 1
            LOT_STEPS = RING + 3
            with nc.Block() as block:
                @block.sync
                def _(sp):
                    if gamma is not None:
                        sp.dma_start(gb[:, 0, :], gamma.partition_broadcast(P)).then_inc(g.loaded.sem, 16)
                        sp.dma_start(gb[:, 1, :], beta.partition_broadcast(P)).then_inc(g.loaded.sem, 16)
                    if table is not None:
                        def body(i, first):
                            for j in range(RING):
                                sp.wait_ge(g.rows_ready.sem, g.rows_ready.at(RING * i + j + 1))
                                sp.dma_start(table[bass.ds(P * RING * i + P * j, P), :], stage[0:P, j, 0:D]).then_inc(store[j].sem, 16)
                        rounds(sp, NT // RING, body)
                        for j in range(RING):
                            sp.wait_ge(store[j].sem, store[j].at(16 * NT // RING))

                @block.vector
                def _(dve):
                    ch = g.chain
                    def stat(i, first):
                        for j in range(RING):
                            nc.vector.bn_stats(stats[:, bass.ds(RING * i + j, 1), :], src[:, bass.ds(RING * i + j, 1), :]).then_inc(ch.sem, 1)
                    rounds(dve, NT // RING, stat)
                    dve.wait_ge(ch.sem, ch.at(NT))
                    nc.vector.tensor_tensor(mean2, stats[:, :, 1], stats[:, :, 4], ALU.add).then_inc(ch.sem, 1)
                    nc.vector.tensor_tensor(diff, stats[:, :, 1], stats[:, :, 4], ALU.subtract).then_inc(ch.sem, 1)
                    nc.vector.tensor_tensor(m2, stats[:, :, 2], stats[:, :, 5], ALU.add).then_inc(ch.sem, 1)
                    dve.wait_ge(ch.sem, ch.at(NT + 3))
                    nc.vector.tensor_tensor(var, diff, diff, ALU.mult).then_inc(ch.sem, 1)
                    nc.vector.tensor_scalar(mean, mean2, 0.5, None, ALU.mult).then_inc(ch.sem, 1)
                    dve.wait_ge(ch.sem, ch.at(NT + 5))
                    nc.vector.scalar_tensor_tensor(var, var, D / 4.0, m2, ALU.mult, ALU.add).then_inc(g.pool_step.sem, 1)
                    dve.wait_ge(g.pool_step.sem, g.pool_step.at(1))
                    nc.vector.tensor_scalar(var, var, 1.0 / D, EPS, ALU.mult, ALU.add).then_inc(ch.sem, 1)
                    dve.wait_ge(g.act_step.sem, g.act_step.at(1))
                    nc.vector.reciprocal(rstd, sd).then_inc(g.pool_step.sem, 1)
                    dve.wait_ge(g.pool_step.sem, g.pool_step.at(2))
                    if gamma is not None:
                        dve.wait_ge(g.loaded.sem, g.loaded.at(32))

                    def body(i, first):
                        for j in range(RING):
                            n = RING * i + j
                            st = stage[0:P, j, 0:D]
                            if not first:
                                if to_xn:
                                    dve.wait_ge(g.xn_copied.sem, g.xn_copied.at(n - RING + 1))
                                if to_featT:
                                    dve.wait_ge(g.turned.sem, g.turned.at(n - RING + 1))
                                if table is not None:
                                    dve.wait_ge(store[j].sem, store[j].at(16 * i))
                            k = 0
                            last = nc.vector.tensor_scalar(st, src[:, bass.ds(n, 1), :].rearrange("p a d -> p (a d)"), mean[:, bass.ds(n, 1)],
                                                           rstd[:, bass.ds(n, 1)], ALU.subtract, ALU.mult)
                            if gamma is not None:
                                for q, op in ((0, ALU.mult), (1, ALU.add)):
                                    last.then_inc(ch.sem, 1)
                                    k += 1
                                    dve.wait_ge(ch.sem, ch.at(PRE + PER * n + k))
                                    last = nc.vector.tensor_tensor(st, st, gb[:, q, :], op)
                            if scale is not None:
                                last.then_inc(ch.sem, 1)
                                k += 1
                                dve.wait_ge(ch.sem, ch.at(PRE + PER * n + k))
                                last = nc.vector.tensor_scalar(st, st, scale[:, bass.ds(n, 1)], None, ALU.mult)
                            last.then_inc(g.rows_ready.sem, 1)

                    def add_lot(i, first):
                        c0 = PRE + LOT_STEPS * i
                        if not first:
                            dve.wait_ge(ch.sem, ch.at(c0))
                        for j in range(RING):
                            n = RING * i + j
                            nc.vector.tensor_scalar(stage[0:P, j, 0:D], src[:, bass.ds(n, 1), :].rearrange("p a d -> p (a d)"), mean[:, bass.ds(n, 1)],
                                                    rstd[:, bass.ds(n, 1)], ALU.subtract, ALU.mult).then_inc(ch.sem, 1)
                        lot = stage[0:P, :, 0:D]
                        for q, op in ((0, ALU.mult), (1, ALU.add)):
                            dve.wait_ge(ch.sem, ch.at(c0 + RING + q))
                            nc.vector.tensor_tensor(lot, lot, gb[:, q:q + 1, :].to_broadcast([P, RING, D]), op).then_inc(ch.sem, 1)
                        dve.wait_ge(ch.sem, ch.at(c0 + RING + 2))
                        x = xres[:, bass.ds(RING * i, RING), :]
                        nc.vector.tensor_tensor(x, x, lot, ALU.add).then_inc(ch.sem, 1)
                    rounds(dve, NT // RING, add_lot if add_to_x else body)

                @block.scalar
                def _(act):
                    act.wait_ge(g.chain.sem, g.chain.at(PRE))
                    nc.scalar.activation(sd, var, ACT.Sqrt).then_inc(g.act_step.sem, 1)

                    def body(i, first):
                        for j in range(RING):
                            n = RING * i + j
                            if to_xn:
                                hold_act(g.rows_ready, n + 1)
                                nc.scalar.copy(xn[:, bass.ds(n, 1), :].rearrange("p a d -> p (a d)"), stage[0:P, j, 0:D]).then_inc(g.xn_copied.sem, 1)
                            if to_featT:
                                hold_act(g.turned, n + 1)
                                nc.scalar.copy(featT[:, :, bass.ds(P * n, P)],
                                               ps[:, j, 0:KD * P].rearrange("p (k t) -> p k t", k=KD)).then_inc(g.evicted.sem, 1)
                    if to_xn or to_featT:
                        rounds(act, NT // RING, body)

                @block.tensor
                def _(pe):
                    def body(i, first):
                        for j in range(RING):
                            n = RING * i + j
                            pe.wait_ge(g.rows_ready.sem, g.rows_ready.at(n + 1))
                            if not first:
                                pe.wait_ge(g.evicted.sem, g.evicted.at(n - RING + 1))
                            for k in range(KD):
                                mm = nc.tensor.transpose(ps[:, j, k * P:(k + 1) * P], stage[0:P, j, k * 128:(k + 1) * 128], ident[0:P, 0:P])
                            mm.then_inc(g.turned.sem, 1)
                    if to_featT:
                        rounds(pe, NT // RING, body)
        g.chain.passed(PRE + (LOT_STEPS * NT // RING if add_to_x else PER * NT)), g.pool_step.passed(2), g.act_step.passed(1)
        if not add_to_x:
            g.rows_ready.passed(NT)
        if gamma is not None:
            g.loaded.passed(32)
        if to_xn:
            g.xn_copied.passed(NT)
        if to_featT:
            g.turned.passed(NT), g.evicted.passed(NT)
        if table is not None:
            for s in store:
                s.passed(16 * NT // RING)

    def tiles(load, weights_in, turn_weights, pe_ops, dve_ops, per, sp_rows=None, feat=featT, extra=False):
        NL = len(load)
        NW = len(turn_weights)
        ch = g.chain
        with nc.Block() as block:
            @block.sync
            def _(sp):
                for d, s in load:
                    sp.dma_start(d, s).then_inc(g.loaded.sem, 16)
                if sp_rows is not None:
                    def body(i, first):
                        for j in range(RING):
                            n = RING * i + j
                            sp.wait_ge(ch.sem, ch.at(per * (n + 1)))
                            for d, s in sp_rows(n, j):
                                sp.dma_start(d, s).then_inc(store[j].sem, 16)
                    rounds(sp, NT // RING, body)
                    k = len(sp_rows(0, 0))
                    for j in range(RING):
                        sp.wait_ge(store[j].sem, store[j].at(16 * k * NT // RING))

            @block.scalar
            def _(act):
                def body(i, first):
                    for j in range(RING):
                        n = RING * i + j
                        if not first:
                            hold_act(g.tile_ready, n - RING + 1)
                        last = nc.scalar.copy(stage[:, j, 0:KD * P].rearrange("p (k t) -> p k t", k=KD), feat[:, 0:KD, bass.ds(P * n, P)])
                        if extra:
                            last.then_inc(g.act_step.sem, 1)
                            last = nc.scalar.copy(stage[0:EX, j, KD * P:KD * P + P], feat[0:EX, KD:KD + 1, bass.ds(P * n, P)].rearrange("p a t -> p (a t)"))
                        last.then_inc(g.staged.sem, 1)
                rounds(act, NT // RING, body)

            @block.tensor
            def _(pe):
                if NL:
                    pe.wait_ge(g.loaded.sem, g.loaded.at(16 * NL))
                for w, (d, s, rows) in enumerate(turn_weights):
                    if w >= 2:
                        pe.wait_ge(g.pe_step.sem, g.pe_step.at(w - 1))
                    nc.tensor.transpose(ps[0:128, 6 + w % 2, 0:rows], s, ident[0:rows, 0:rows]).then_inc(g.turned.sem, 1)
                if NW:
                    pe.wait_ge(g.pe_step.sem, g.pe_step.at(NW))

                def body(i, first):
                    for j in range(RING):
                        n = RING * i + j
                        pe.wait_ge(g.staged.sem, g.staged.at(n + 1))
                        if extra:
                            pe.wait_ge(g.act_step.sem, g.act_step.at(n + 1))
                        if not first:
                            pe.wait_ge(ch.sem, ch.at(per * (n - RING + 1)))
                        pe_ops(j, stage[:, j, 0:KD * P].rearrange("p (k t) -> p k t", k=KD)).then_inc(g.tile_ready.sem, 1)
                rounds(pe, NT // RING, body)

            @block.vector
            def _(dve):
                if NL:
                    dve.wait_ge(g.loaded.sem, g.loaded.at(16 * NL))
                for w, (d, s, rows) in enumerate(turn_weights):
                    dve.wait_ge(g.turned.sem, g.turned.at(w + 1))
                    nc.vector.tensor_copy(d, ps[0:128, 6 + w % 2, 0:rows]).then_inc(g.pe_step.sem, 1)

                def body(i, first):
                    for j in range(RING):
                        n = RING * i + j
                        dve.wait_ge(g.tile_ready.sem, g.tile_ready.at(n + 1))
                        if sp_rows is not None and not first:
                            dve.wait_ge(store[j].sem, store[j].at(16 * len(sp_rows(0, 0)) * i))
                        dve_ops(dve, n, j, per * n)
                rounds(dve, NT // RING, body)
        g.loaded.passed(16 * NL), g.turned.passed(NW), g.pe_step.passed(NW)
        g.staged.passed(NT), g.tile_ready.passed(NT), ch.passed(per * NT)
        if extra:
            g.act_step.passed(NT)
        if sp_rows is not None:
            for s in store:
                s.passed(16 * len(sp_rows(0, 0)) * NT // RING)

    def tile_of(t, n):
        return t[:, bass.ds(n, 1), :].rearrange("p a d -> p (a d)")

    def times(w, width):
        def pe_ops(j, x):
            for k in range(KD):
                mm = nc.tensor.matmul(ps[0:P, j, 0:width], x[:, k, :], w[:, k, 0:width], start=(k == 0), stop=(k == KD - 1))
            return mm
        return pe_ops

    def halves(w):
        return w.rearrange("(k p) f -> p k f", p=128)

    def wait_chain(dve, count):
        dve.wait_ge(g.chain.sem, g.chain.at(count))

    def att_project(hst):
        with ExitStack() as c:
            w = sb("att_w", [128, KD, D], F32, c)
            b = sb("att_b", [P, D], F32, c)
            a = sb("att_a", [P, 2, D], F32, c)
            rows = sb("ap_rows", [P, RING, AROW], F32, c)
            prod = sb("att_prod", [P, 2, D], F32, c)
            both = sb("att_both", [P, 2 * HEADS], F32, c)

            def use(dve, n, j, c0):
                ch = g.chain.sem
                h = rows[:, j, 0:D].rearrange("p (f h) -> p h f", h=HEADS)
                nc.vector.tensor_tensor(h, ps[0:P, j, 0:D].rearrange("p (h f) -> p h f", h=HEADS),
                                        b[:].rearrange("p (h f) -> p h f", h=HEADS), ALU.add).then_inc(ch, 1)
                wait_chain(dve, c0 + 1)
                for s in range(2):
                    nc.vector.tensor_tensor(prod[:, s, :].rearrange("p (h f) -> p h f", h=HEADS), h,
                                            a[:, s, :].rearrange("p (h f) -> p h f", h=HEADS), ALU.mult).then_inc(ch, 1)
                nc.vector.tensor_copy(tile_of(xn, n), rows[:, j, 0:D]).then_inc(ch, 1)
                wait_chain(dve, c0 + 3)
                nc.vector.tensor_reduce(both[:].rearrange("p (s h) -> p s h", s=2),
                                        prod[:].rearrange("p s (h f) -> p s h f", h=HEADS), X, ALU.add).then_inc(ch, 1)
                wait_chain(dve, c0 + 5)
                nc.vector.tensor_copy(rows[:, j, D:AROW], both[:, 0:HEADS]).then_inc(ch, 1)
                nc.vector.tensor_copy(tile_of(hst, n), both[:]).then_inc(ch, 1)

            tiles([(w[:], halves(io["L0_gnn_W"])), (b[:], io["L0_gnn_b"].partition_broadcast(P)),
                   (a[:, 0, :], io["L0_gnn_a_src"].rearrange("a h f -> (a h f)").partition_broadcast(P)),
                   (a[:, 1, :], io["L0_gnn_a_trg"].rearrange("a h f -> (a h f)").partition_broadcast(P))],
                  None, [], times(w, D), use, 7,
                  sp_rows=lambda n, j: [(t_att[bass.ds(P * n, P), :], rows[:, j, :])])

    def att_shift(hst, own, shift, top):
        with ExitStack() as c:
            rows = sb("as_rows", [P, NT, 2 * HEADS], F32, c)
            zero = sb("as_zero", [P, 2 * HEADS], F32, c)
            hs, ht = hst[:, :, 0:HEADS], hst[:, :, HEADS:2 * HEADS]
            with nc.Block() as block:
                @block.vector
                def _(dve):
                    ch = g.chain.sem
                    nc.vector.tensor_reduce(top[:, 0, :], hs.rearrange("p t h -> p h t"), X, ALU.max).then_inc(ch, 1)
                    nc.vector.tensor_tensor(own[:], hs, ht, ALU.add).then_inc(ch, 1)
                    nc.vector.tensor_copy(rows[:, :, 0:HEADS], ht).then_inc(ch, 1)
                    nc.vector.memset(zero[:], 0.0).then_inc(ch, 1)
                    wait_chain(dve, 2)
                    nc.vector.scalar_tensor_tensor(own[:], own[:], 0.2, own[:], ALU.mult, ALU.max).then_inc(ch, 1)
                    dve.wait_ge(g.pe_step.sem, g.pe_step.at(1))
                    nc.vector.tensor_tensor(shift[:], ht, top[:, 1, :].unsqueeze(1).to_broadcast([P, NT, HEADS]), ALU.add).then_inc(ch, 1)
                    wait_chain(dve, 6)
                    nc.vector.scalar_tensor_tensor(shift[:], shift[:], 0.2, shift[:], ALU.mult, ALU.max).then_inc(ch, 1)
                    wait_chain(dve, 7)
                    nc.vector.tensor_copy(rows[:, :, HEADS:], shift[:]).then_inc(ch, 1)

                @block.gpsimd
                def _(pool):
                    pool.wait_ge(g.chain.sem, g.chain.at(1))
                    nc.gpsimd.partition_all_reduce(top[:, 1, :], top[:, 0, :], P, RMAX).then_inc(g.pe_step.sem, 1)

                @block.sync
                def _(sp):
                    sp.wait_ge(g.chain.sem, g.chain.at(8))
                    sp.dma_start(t_tgt[0:N, :].rearrange("(t p) k -> p t k", p=P), rows[:]).then_inc(g.loaded.sem, 16)
                    sp.dma_start(t_tgt[N:N + P, :], zero[:]).then_inc(g.loaded.sem, 16)
                    sp.wait_ge(g.loaded.sem, g.loaded.at(32))
        g.chain.passed(8), g.pe_step.passed(1), g.loaded.passed(32)

    def gathers(pool, table, free, rows, lots):
        def fill(i, h, first):
            n = RING * (lots * i + h)
            if not first:
                hold_pool(free, n - RING * (lots - 1))
            nc.gpsimd.tensor_copy(idx[:, RING * h:RING * h + RING], src_i[:, bass.ds(n, RING)]).then_inc(g.pool_step.sem, 1)
            hold_pool(g.pool_step, lots * i + h + 1)
            for j in range(RING * h, RING * h + RING):
                nc.gpsimd.indirect_dma_start(out=rows[:, j, :], out_offset=None, in_=table,
                                             in_offset=bass.IndirectOffsetOnAxis(ap=idx[:, j:j + 1], axis=0)).then_inc(gath[j].sem, 16)
        whole, rest = divmod(NCH // RING, lots)
        for h in range(lots):
            fill(0, h, True)
        with pool.Fori(1, whole) as i:
            for h in range(lots):
                fill(i, h, False)
        for h in range(rest):
            fill(whole, h, False)

    def gathers_passed(lots):
        g.pool_step.passed(NCH // RING)
        for j in range(RING * lots):
            gath[j].passed(16 * (NCH // RING // lots + (1 if j // RING < NCH // RING % lots else 0)))

    def steps(eng, count, ring, parts):
        top = max(l for l, _ in parts)
        whole = (count - top) // ring
        for n in range(-top, 0):
            for l, f in parts:
                if n + l >= 0:
                    f(n + l, (n + l) // ring, (n + l) % ring, n + l < ring)
        for j in range(ring):
            for l, f in parts:
                f(j + l, (j + l) // ring, (j + l) % ring, j + l < ring)
        with eng.Fori(1, whole) as i:
            for j in range(ring):
                for l, f in parts:
                    f(ring * i + j + l, i + (j + l) // ring, (j + l) % ring, False)
        for n in range(ring * whole, count):
            for l, f in parts:
                if n + l < count:
                    f(n + l, (n + l) // ring, (n + l) % ring, False)

    def att_pass(own, hst, shift, top, sums):
        LOTS = 4
        with ExitStack() as c:
            R = LOTS * RING
            rows = sb("ag_rows", [P, R, AROW], F32, c)
            msg = sb("ag_msg", [P, R, AROW + 1], F32, c)
            hot = sb("ag_hot", [P, R, P], F32, c)
            hotT = stage[0:P].rearrange("p r c -> p (r c)")[:, 0:LOTS * RING * P].rearrange("p (l r t) -> p l r t", l=LOTS, r=RING)
            tgt = sb("ag_tgt", [P, R, 2 * HEADS], F32, c)
            sc = sb("ag_sc", [P, 3, RING, HEADS], F32, c)
            high = sb("ag_high", [P, RING, HEADS], F32, c)
            NL = NCH // RING
            TB, EB, AB = 0, 2, 3
            with nc.Block() as block:
                @block.gpsimd
                def _(pool):
                    gathers(pool, t_att, g.msg_done, rows, LOTS)

                @block.sync
                def _(sp):
                    def body(m, i, h, first):
                        if not first:
                            sp.wait_ge(g.tile_ready.sem, g.tile_ready.at(m - LOTS + 1))
                        for j, b in enumerate(starts(sp, nc.sync, m), RING * h):
                            sp.dma_start(tgt[:, j, :], t_tgt[bass.ds(b, P), :]).then_inc(tgt_in[h].sem, 16)
                    steps(sp, NL, LOTS, [(0, body)])

                @block.vector
                def _(dve):
                    nc.vector.memset(sums[:], 0.0).then_inc(g.added.sem, 1)
                    nc.vector.memset(ps[:, AB:AB + RING, KD * P:(KD + 1) * P], 0.0).then_inc(g.added.sem, 1)
                    nc.vector.memset(msg[:], 1.0).then_inc(g.added.sem, 1)
                    nc.vector.memset(high[:], -3e38).then_inc(g.added.sem, 1)
                    dve.wait_ge(g.added.sem, g.added.at(4))

                    def scores(m, i, h, first):
                        lot = slice(RING * h, RING * h + RING)
                        e = ps[0:P, EB, 0:RING * 2 * HEADS].rearrange("p (c k) -> p c k", c=RING)
                        if not (first and h == 0):
                            dve.wait_ge(g.gate_done.sem, g.gate_done.at(m))
                        dve.wait_ge(g.tile_ready.sem, g.tile_ready.at(m + 1))
                        for j in range(RING * h, RING * h + RING):
                            dve.wait_ge(gath[j].sem, gath[j].at(16 * i + 16))
                        nc.vector.tensor_tensor(sc[:, 0], e[:, :, 0:HEADS], rows[:, lot, D:AROW], ALU.add).then_inc(g.chain.sem, 1)
                        wait_chain(dve, 4 * m + 1)
                        nc.vector.scalar_tensor_tensor(sc[:, 1], sc[:, 0], 0.2, sc[:, 0], ALU.mult, ALU.max).then_inc(g.chain.sem, 1)
                        wait_chain(dve, 4 * m + 2)
                        nc.vector.tensor_tensor(high[:], high[:], sc[:, 1], ALU.max).then_inc(g.chain.sem, 1)
                        nc.vector.tensor_tensor(sc[:, 2], sc[:, 1], e[:, :, HEADS:2 * HEADS], ALU.subtract).then_inc(g.chain.sem, 1)

                    def add(m, j, b):
                        n = RING * m + j
                        dve.wait_ge(g.agg_ready.sem, g.agg_ready.at(n + 1))
                        dve.wait_ge(g.added.sem, g.added.at(4 + n))
                        f = sums[:, :, bass.ds(b, P)]
                        nc.vector.tensor_tensor(f, f, ps[:, AB + j, 0:(KD + 1) * P].rearrange("p (k t) -> p k t", k=KD + 1), ALU.add).then_inc(g.added.sem, 1)

                    def messages_and_adds(m, i, h, first):
                        opening = first and h == 0
                        windows = None if opening else starts(dve, nc.vector, m - 1)
                        dve.wait_ge(g.gate_done.sem, g.gate_done.at(m + 1))
                        for j in range(RING):
                            if not opening:
                                add(m - 1, j, windows[j])
                            s = RING * h + j
                            nc.vector.tensor_tensor(msg[:, s, 0:D].rearrange("p (f h) -> p f h", h=HEADS),
                                                    rows[:, s, 0:D].rearrange("p (f h) -> p f h", h=HEADS),
                                                    msg[:, s, D:AROW].unsqueeze(1).to_broadcast([P, HF, HEADS]), ALU.mult).then_inc(g.msg_done.sem, 1)
                    steps(dve, NL, LOTS, [(1, messages_and_adds), (2, scores)])
                    for j, b in enumerate(starts(dve, nc.vector, NL - 1)):
                        add(NL - 1, j, b)
                    wait_chain(dve, 4 * NL)
                    nc.vector.tensor_reduce(sc[:, 0, 0, 0:1], high[:].rearrange("p c h -> p (c h)"), X, ALU.max).then_inc(g.chain.sem, 1)
                    nc.vector.tensor_reduce(sc[:, 0, 0, 1:2], own[:].rearrange("p t h -> p (t h)"), X, ALU.max).then_inc(g.chain.sem, 1)
                    wait_chain(dve, 4 * NL + 2)
                    nc.vector.tensor_tensor(top[:, 0, 0:1], sc[:, 0, 0, 0:1], sc[:, 0, 0, 1:2], ALU.max).then_inc(g.chain.sem, 1)

                @block.scalar
                def _(act):
                    def turned(m, i, h, first):
                        hold_act(g.turned, m + 1)
                        if not first:
                            hold_act(g.tile_ready, m - LOTS + 1)
                        for q, k in ((0, 3), (3, 2)):
                            last = nc.scalar.copy(hotT[:, h, q:q + k, :], ps[0:P, TB + q // 3, 0:k * P].rearrange("p (c t) -> p c t", c=k))
                            last.then_inc(g.evicted.sem, 1)

                    def weights(m, i, h, first):
                        hold_act(g.chain, 4 * m + 4)
                        if not first:
                            hold_act(g.agg_ready, RING * (m - LOTS + 1))
                        nc.scalar.activation(msg[:, RING * h:RING * h + RING, D:AROW], sc[:, 2], ACT.Exp).then_inc(g.gate_done.sem, 1)
                    def one_hots(m, i, h, first):
                        if not first:
                            hold_act(g.agg_ready, RING * (m - LOTS + 1))
                        lot = hot[:, RING * h:RING * h + RING, :]
                        for j in range(RING):
                            last = nc.scalar.activation(lot[:, j, :], iota[:], ACT.Square, bias=dloc[:, bass.ds(RING * m + j, 1)], scale=-1.0)
                        last.then_inc(g.act_step.sem, 1)
                        hold_act(g.act_step, m + 1)
                        nc.scalar.activation(lot, lot, ACT.Relu, bias=1.0, scale=-2.0).then_inc(g.one_hot.sem, 1)
                    steps(act, NL, LOTS, [(3, turned), (2, weights), (4, one_hots)])

                @block.tensor
                def _(pe):
                    def turn(m, i, h, first):
                        if not (first and h == 0):
                            hold_pe(g.evicted, 2 * m)
                        hold_pe(g.one_hot, m + 1)
                        for j in range(RING):
                            mm = nc.tensor.transpose(ps[0:P, TB + j // 3, (j % 3) * P:(j % 3 + 1) * P], hot[:, RING * h + j, :], ident[0:P, 0:P])
                        mm.then_inc(g.turned.sem, 1)

                    def spread(m, i, h, first):
                        hold_pe(g.evicted, 2 * m + 2)
                        hold_pe(tgt_in[h], 16 * RING * (i + 1))
                        if not (first and h == 0):
                            hold_pe(g.chain, 4 * m)
                        for j in range(RING):
                            mm = nc.tensor.matmul(ps[0:P, EB, 2 * HEADS * j:2 * HEADS * (j + 1)], hotT[:, h, j, :], tgt[:, RING * h + j, :], start=True, stop=True)
                        mm.then_inc(g.tile_ready.sem, 1)

                    def products(m, i, h, first):
                        for j in range(RING):
                            n = RING * m + j
                            s = RING * h + j
                            pe.wait_ge(g.msg_done.sem, g.msg_done.at(n + 1))
                            if first and h == 0:
                                pe.wait_ge(g.added.sem, g.added.at(4))
                            else:
                                pe.wait_ge(g.added.sem, g.added.at(4 + n - RING + 1))
                            for k in range(KD):
                                nc.tensor.matmul(ps[:, AB + j, k * P:(k + 1) * P], msg[:, s, k * 128:(k + 1) * 128], hot[:, s, :], start=True, stop=True)
                            nc.tensor.matmul(ps[0:EX, AB + j, KD * P:KD * P + P], msg[:, s, D:D + EX], hot[:, s, :], start=True, stop=True).then_inc(g.agg_ready.sem, 1)
                    steps(pe, NL, LOTS, [(0, products), (2, spread), (3, turn)])
        gathers_passed(LOTS)
        for h in range(LOTS):
            tgt_in[h].passed(16 * RING * (NL // LOTS + (1 if h < NL % LOTS else 0)))
        g.chain.passed(4 * NL + 3), g.added.passed(4 + NCH), g.evicted.passed(2 * NL)
        for s in (g.msg_done, g.agg_ready):
            s.passed(NCH)
        for s in (g.turned, g.tile_ready, g.gate_done, g.act_step, g.one_hot):
            s.passed(NL)

    def edge_pass(tag, table, weight=None, loops=False, clear=None):
        with ExitStack() as c:
            rows = sb(tag + "_rows", [P, GR, D], F32, c)
            hot = sb(tag + "_hot", [P, GR, P], F32, c)
            NL, LOTS = NCH // RING, GR // RING
            ZF = -(-TSMAX // (2 * RING))
            with nc.Block() as block:
                @block.gpsimd
                def _(pool):
                    gathers(pool, table, g.agg_ready, rows, GR // RING)

                @block.vector
                def _(dve):
                    if clear is not None:
                        nc.vector.memset(stage[:], 0.0).then_inc(g.act_step.sem, 1)
                    nc.vector.memset(featT[:, :, N:] if loops else featT[:], 0.0).then_inc(g.added.sem, 1)
                    if loops:
                        dve.wait_ge(g.evicted.sem, g.evicted.at(NT))
                    dve.wait_ge(g.added.sem, g.added.at(1))

                    def one_hots(m, i, h, first):
                        for j in range(RING):
                            nc.vector.tensor_scalar(hot[:, RING * h + j, :], iota[:], dloc[:, bass.ds(RING * m + j, 1)],
                                                    weight[:, bass.ds(RING * m + j, 1)] if weight is not None else None, ALU.is_equal,
                                                    ALU.mult if weight is not None else ALU.bypass).then_inc(g.one_hot.sem, 1)

                    def add(m, i, h, first):
                        for j, b in enumerate(starts(dve, nc.vector, m)):
                            n = RING * m + j
                            dve.wait_ge(g.agg_ready.sem, g.agg_ready.at(n + 1))
                            dve.wait_ge(g.added.sem, g.added.at(1 + n))
                            f = featT[:, :, bass.ds(b, P)]
                            nc.vector.tensor_tensor(f, f, ps[:, j, 0:KD * P].rearrange("p (k t) -> p k t", k=KD), ALU.add).then_inc(g.added.sem, 1)
                    steps(dve, NL, LOTS, [(LOTS - 1, one_hots), (0, add)])

                if clear is not None:
                    @block.sync
                    def _(sp):
                        sp.wait_ge(g.act_step.sem, g.act_step.at(1))
                        for t in range(0, TSMAX, 2 * RING):
                            k = min(2 * RING, TSMAX - t)
                            sp.dma_start(clear[t * P:(t + k) * P, :].rearrange("(k p) d -> p k d", p=P),
                                         stage[0:P].rearrange("p r (a d) -> p (r a) d", d=D)[:, 0:k, :]).then_inc(g.loaded.sem, 16)
                        sp.wait_ge(g.loaded.sem, g.loaded.at(16 * ZF))

                if loops:
                    @block.sync
                    def _(sp):
                        def body(i, first):
                            for j in range(RING):
                                if not first:
                                    sp.wait_ge(g.turned.sem, g.turned.at(RING * (i - 1) + j + 1))
                                sp.dma_start(stage[0:P, j, 0:D], table[bass.ds(P * RING * i + P * j, P), :]).then_inc(store[j].sem, 16)
                        rounds(sp, NT // RING, body)

                    @block.scalar
                    def _(act):
                        def body(i, first):
                            for j in range(RING):
                                n = RING * i + j
                                hold_act(g.turned, n + 1)
                                nc.scalar.copy(featT[:, :, bass.ds(P * n, P)],
                                               ps[:, j, 0:KD * P].rearrange("p (k t) -> p k t", k=KD)).then_inc(g.evicted.sem, 1)
                        rounds(act, NT // RING, body)

                @block.tensor
                def _(pe):
                    def turn(i, first):
                        for j in range(RING):
                            n = RING * i + j
                            pe.wait_ge(store[j].sem, store[j].at(16 * i + 16))
                            if not first:
                                pe.wait_ge(g.evicted.sem, g.evicted.at(n - RING + 1))
                            for k in range(KD):
                                mm = nc.tensor.transpose(ps[:, j, k * P:(k + 1) * P], stage[0:P, j, k * 128:(k + 1) * 128], ident[0:P, 0:P])
                            mm.then_inc(g.turned.sem, 1)
                    if loops:
                        rounds(pe, NT // RING, turn)
                        pe.wait_ge(g.evicted.sem, g.evicted.at(NT))

                    def body(n, i, j, first):
                        pe.wait_ge(gath[j].sem, gath[j].at(16 * i + 16))
                        pe.wait_ge(g.one_hot.sem, g.one_hot.at(n + 1))
                        if not (first and j < RING):
                            pe.wait_ge(g.added.sem, g.added.at(1 + n - RING + 1))
                        for k in range(KD):
                            lhs = rows[:, j, k * 128:(k + 1) * 128]
                            mm = nc.tensor.matmul(ps[:, j % RING, k * P:(k + 1) * P], lhs, hot[:, j, :], start=True, stop=True)
                        mm.then_inc(g.agg_ready.sem, 1)
                    for j in range(GR):
                        body(j, 0, j, True)
                    with pe.Fori(1, NCH // GR) as i:
                        for j in range(GR):
                            body(GR * i + j, i, j, False)
                    for j in range(NCH % GR):
                        body(NCH - NCH % GR + j, NCH // GR, j, False)
        gathers_passed(GR // RING)
        g.agg_ready.passed(NCH), g.one_hot.passed(NCH), g.added.passed(1 + NCH)
        if clear is not None:
            g.act_step.passed(1), g.loaded.passed(16 * ZF)
        if loops:
            g.turned.passed(NT), g.evicted.passed(NT)
            for s in store:
                s.passed(16 * NT // RING)

    def turn_back(extra_rows):
        def pe_ops(j, x):
            for k in range(KD):
                mm = nc.tensor.transpose(ps[0:P, j, k * 128:(k + 1) * 128], x[:, k, :], ident[:])
            if extra_rows:
                mm = nc.tensor.transpose(ps[0:P, j, D:D + EX], stage[0:EX, j, KD * P:KD * P + P], ident[0:EX, 0:EX])
            return mm
        return pe_ops

    def att_finish(sums, own, shift, top):
        with ExitStack() as c:
            den = sb("den", [P, 2, HEADS], F32, c)
            deg = sb("deg", [P, 2, NT], F32, c)
            o = sb("att_o", [P, 2, D], F32, c)

            def use(dve, n, j, c0):
                ch = g.chain.sem
                by_head = lambda ap: ap.rearrange("p (f h) -> p f h", h=HEADS)
                w = own[:, bass.ds(n, 1), :]
                nc.vector.tensor_tensor(den[:, 0, :], ps[0:P, j, D:D + HEADS], tile_of(shift, n), ALU.add).then_inc(ch, 1)
                nc.vector.tensor_copy(deg[:, 0, bass.ds(n, 1)], ps[0:P, j, D + HEADS:D + EX]).then_inc(ch, 1)
                nc.vector.tensor_tensor(by_head(o[:, 1, :]), by_head(tile_of(xn, n)), w.to_broadcast([P, HF, HEADS]), ALU.mult).then_inc(ch, 1)
                wait_chain(dve, c0 + 3)
                nc.vector.reciprocal(den[:, 1, :], den[:, 0, :]).then_inc(ch, 1)
                nc.vector.tensor_tensor(o[:, 1, :], o[:, 1, :], ps[0:P, j, 0:D], ALU.add).then_inc(ch, 1)
                wait_chain(dve, c0 + 5)
                nc.vector.tensor_tensor(o[:, 0, :].rearrange("p (h f) -> p f h", h=HEADS), by_head(o[:, 1, :]),
                                        den[:, 1, :].unsqueeze(1).to_broadcast([P, HF, HEADS]), ALU.mult).then_inc(ch, 1)
                wait_chain(dve, c0 + 6)
                nc.vector.tensor_tensor(tile_of(xres, n), tile_of(xres, n), o[:, 0, :], ALU.add).then_inc(ch, 1)

            flat = lambda t: t[:].rearrange("p t h -> p (t h)")
            with nc.Block() as block:
                @block.gpsimd
                def _(pool):
                    nc.gpsimd.partition_all_reduce(top[:, 1, 0:1], top[:, 0, 0:1], P, RMAX).then_inc(g.pool_step.sem, 1)

                @block.vector
                def _(dve):
                    nc.vector.tensor_tensor(flat(own), flat(own), flat(shift), ALU.subtract).then_inc(g.chain.sem, 1)

                @block.scalar
                def _(act):
                    act.wait_ge(g.chain.sem, g.chain.at(1))
                    nc.scalar.activation(flat(own), flat(own), ACT.Exp)
                    act.wait_ge(g.pool_step.sem, g.pool_step.at(1))
                    nc.scalar.activation(flat(shift), flat(shift), ACT.Exp, bias=top[:, 1, 0:1], scale=-1.0).then_inc(g.act_step.sem, 1)

                @block.vector
                def _(dve):
                    dve.wait_ge(g.act_step.sem, g.act_step.at(1))
                    nc.vector.scalar_tensor_tensor(flat(shift), flat(shift), 1e-10, flat(own), ALU.mult, ALU.add)
            g.chain.passed(1), g.pool_step.passed(1), g.act_step.passed(1)
            tiles([], None, [], turn_back(True), use, 7, feat=sums, extra=True)
            with nc.Block() as block:
                @block.vector
                def _(dve):
                    nc.vector.tensor_scalar(deg[:, 1, :], deg[:, 0, :], 1.0, None, ALU.add).then_inc(g.chain.sem, 1)
                    dve.wait_ge(g.act_step.sem, g.act_step.at(1))
                    nc.vector.reciprocal(dinv[:], deg[:, 0, :]).then_inc(g.chain.sem, 1)

                @block.scalar
                def _(act):
                    act.wait_ge(g.chain.sem, g.chain.at(1))
                    nc.scalar.activation(deg[:, 0, :], deg[:, 1, :], ACT.Sqrt).then_inc(g.act_step.sem, 1)
            g.chain.passed(2), g.act_step.passed(1)

    def sum_finish():
        with ExitStack() as c:
            w = sb("sum_w", [128, KD, D], F32, c)

            def use(dve, n, j, c0):
                nc.vector.tensor_tensor(tile_of(xres, n), tile_of(xres, n), ps[0:P, j, 0:D], ALU.add).then_inc(g.chain.sem, 1)
            tiles([(w[:], halves(io["L1_gnn_weight"]))], None, [], times(w, D), use, 1)

    def conv_finish(layer, table):
        with ExitStack() as c:
            raw = sb(f"conv_raw{layer}", [128, KD, D], F32, c)
            w = sb(f"conv_w{layer}", [128, KD, D], F32, c)
            b = sb(f"conv_b{layer}", [P, D], F32, c)
            h = sb(f"conv_h{layer}", [P, RING, D], F32, c)
            blocks = [(w[:, k, o * 128:(o + 1) * 128], raw[:, o, k * 128:(k + 1) * 128], 128) for o in range(KD) for k in range(KD)]

            def use(dve, n, j, c0):
                ch = g.chain.sem
                nc.vector.scalar_tensor_tensor(h[:, j, :], ps[0:P, j, 0:D], dinv[:, bass.ds(n, 1)], b[:], ALU.mult, ALU.add).then_inc(ch, 1)
                wait_chain(dve, c0 + 1)
                if table is not None:
                    nc.vector.tensor_scalar(h[:, j, :], h[:, j, :], 0.0, dinv[:, bass.ds(n, 1)], ALU.max, ALU.mult).then_inc(ch, 1)
                else:
                    nc.vector.tensor_tensor(tile_of(xres, n), tile_of(xres, n), h[:, j, :], ALU.add).then_inc(ch, 1)
            tiles([(raw[:], halves(io[f"L2_gnn_W{layer}"])), (b[:], io[f"L2_gnn_b{layer}"].partition_broadcast(P))],
                  None, blocks, times(w, D), use, 2,
                  sp_rows=(lambda n, j: [(table[bass.ds(P * n, P), :], h[:, j, :])]) if table is not None else None)

    def edge_project():
        with ExitStack() as c:
            w = sb("ep_w", [128, KD, 2 * D], F32, c)
            b = sb("ep_b", [P, 2 * D], F32, c)
            h = sb("ep_h", [P, RING, 2 * D], F32, c)

            def use(dve, n, j, c0):
                nc.vector.tensor_tensor(h[:, j, :], ps[0:P, j, :], b[:], ALU.add).then_inc(g.chain.sem, 1)
            tiles([(w[:, :, 0:D], halves(io["L3_gnn_W1"][0:D, :])), (w[:, :, D:2 * D], halves(io["L3_gnn_Wg"][0:D, :])),
                   (b[:, 0:D], io["L3_gnn_b1"].partition_broadcast(P)), (b[:, D:2 * D], io["L3_gnn_bg"].partition_broadcast(P))],
                  None, [], times(w, 2 * D), use, 1,
                  sp_rows=lambda n, j: [(t_edge[bass.ds(P * n, P), :], h[:, j, :])])

    def edge_gated():
        DE = 64
        GE = 2 * RING
        with ExitStack() as c:
            rows = sb("eg_rows", [P, GE, 2 * D], F32, c)
            hot = sb("eg_hot", [P, RING, P], F32, c)
            ea = sb("eg_ea", [P, RING, DE], F32, c)
            eaT = sb("eg_eaT", [DE, RING, P], F32, c)
            w1g = sb("eg_w1g", [DE, 2 * D], F32, c)
            w2 = sb("eg_w2", [128, KD, D], F32, c)
            b2 = sb("eg_b2", [P, D], F32, c)
            rT = sb("eg_rT", [128, RING, KD, P], F32, c)
            pre = sb("eg_pre", [P, RING, 2 * D], F32, c)
            msg = sb("eg_msg", [P, RING, D], F32, c)
            TB, PB, HB, CB, AB = 0, 1, 3, 5, 6
            NL = 4

            with nc.Block() as block:
                @block.gpsimd
                def _(pool):
                    gathers(pool, t_edge, g.gpre_done, rows, GE // RING)

                @block.sync
                def _(sp):
                    sp.dma_start(w1g[:, 0:D], io["L3_gnn_W1"][D:D + DE, :]).then_inc(g.loaded.sem, 16)
                    sp.dma_start(w1g[:, D:2 * D], io["L3_gnn_Wg"][D:D + DE, :]).then_inc(g.loaded.sem, 16)
                    sp.dma_start(w2[:], halves(io["L3_gnn_W2"])).then_inc(g.loaded.sem, 16)
                    sp.dma_start(b2[:], io["L3_gnn_b2"].partition_broadcast(P)).then_inc(g.loaded.sem, 16)

                    def body(i, first):
                        for j in range(RING):
                            n = RING * i + j
                            if not first:
                                sp.wait_ge(g.ea_turned.sem, g.ea_turned.at(n - RING + 1))
                            sp.dma_start(ea[:, j, :], io["edge_attr_64"][bass.ds(P * RING * i + P * j, P), :]).then_inc(store[j].sem, 16)
                    rounds(sp, NCH // RING, body)

                @block.tensor
                def _(pe):
                    pe.wait_ge(g.loaded.sem, g.loaded.at(16 * NL))

                    def turn(n, i, j, first):
                        s = j % RING
                        i5 = 2 * i + (j // RING)
                        if not (first and j < 1):
                            pe.wait_ge(g.eaT_ready.sem, g.eaT_ready.at(n))
                        hold_pe(store[s], 16 * i5 + 16)
                        nc.tensor.transpose(ps[0:DE, TB, 0:P], ea[:, s, :], ident[0:P, 0:P]).then_inc(g.ea_turned.sem, 1)

                    def attr_products(n, i, j, first):
                        s = j % RING
                        pe.wait_ge(g.eaT_ready.sem, g.eaT_ready.at(n + 1))
                        if not (first and j < 2):
                            pe.wait_ge(g.gpre_done.sem, g.gpre_done.at(n - 1))
                        nc.tensor.matmul(ps[0:P, PB + j % 2, :], eaT[:, s, :], w1g[:], start=True, stop=True).then_inc(g.pre_ready.sem, 1)

                    def turn_pre(n, i, j, first):
                        hold_pe(g.gpre_done, n + 1)
                        if not (first and j < 2):
                            hold_pe(g.relu_done, n - 1)
                        for k in range(KD):
                            mm = nc.tensor.transpose(ps[:, HB + j % 2, k * P:(k + 1) * P], pre[:, j % RING, k * 128:(k + 1) * 128], ident[0:P, 0:P])
                        mm.then_inc(g.tile_ready.sem, 1)

                    def core(n, i, j, first):
                        pe.wait_ge(g.relu_done.sem, g.relu_done.at(n + 1))
                        if not (first and j < 1):
                            pe.wait_ge(g.msg_done.sem, g.msg_done.at(2 * n))
                        for k in range(KD):
                            mm = nc.tensor.matmul(ps[0:P, CB, 0:D], rT[:, j % RING, k, :], w2[:, k, :], start=(k == 0), stop=(k == KD - 1))
                        mm.then_inc(g.core_ready.sem, 1)

                    def agg(n, i, j, first):
                        pe.wait_ge(g.msg_done.sem, g.msg_done.at(2 * n + 2))
                        pe.wait_ge(g.one_hot.sem, g.one_hot.at(n + 1))
                        if not (first and j < 2):
                            pe.wait_ge(g.added.sem, g.added.at(n))
                        for k in range(KD):
                            mm = nc.tensor.matmul(ps[:, AB + j % 2, k * P:(k + 1) * P], msg[:, j % RING, k * 128:(k + 1) * 128], hot[:, j % RING, :], start=True, stop=True)
                        mm.then_inc(g.agg_ready.sem, 1)
                    steps(pe, NCH, GE, [(5, turn), (4, attr_products), (2, turn_pre), (1, core), (0, agg)])

                @block.scalar
                def _(act):
                    def attr(n, i, j, first):
                        hold_act(g.ea_turned, n + 1)
                        if not (first and j < RING):
                            hold_act(g.pre_ready, n - RING + 1)
                        nc.scalar.copy(eaT[:, j % RING, :], ps[0:DE, TB, 0:P]).then_inc(g.eaT_ready.sem, 1)

                    def relu(n, i, j, first):
                        hold_act(g.tile_ready, n + 1)
                        if not (first and j < RING):
                            hold_act(g.core_ready, n - RING + 1)
                        nc.scalar.activation(rT[:, j % RING], ps[:, HB + j % 2, 0:KD * P].rearrange("p (k t) -> p k t", k=KD), ACT.Relu).then_inc(g.relu_done.sem, 1)

                    def gate(n, i, j, first):
                        hold_act(g.gpre_done, n + 1)
                        nc.scalar.activation(pre[:, j % RING, D:2 * D], pre[:, j % RING, D:2 * D], ACT.Sigmoid).then_inc(g.gate_done.sem, 1)
                    steps(act, NCH, GE, [(4, attr), (1, relu), (1, gate)])

                @block.vector
                def _(dve):
                    nc.vector.memset(featT[:], 0.0).then_inc(g.added.sem, 1)
                    dve.wait_ge(g.loaded.sem, g.loaded.at(16 * NL))
                    windows = []

                    def gpre(n, i, j, first):
                        s = j % RING
                        dve.wait_ge(g.pre_ready.sem, g.pre_ready.at(n + 1))
                        if not (first and j < RING):
                            dve.wait_ge(g.msg_done.sem, g.msg_done.at(2 * (n - RING + 1)))
                        dve.wait_ge(gath[j].sem, gath[j].at(16 * i + 16))
                        nc.vector.tensor_tensor(pre[:, s, :], ps[0:P, PB + j % 2, :], rows[:, j, :], ALU.add).then_inc(g.gpre_done.sem, 1)
                        if not (first and j < RING):
                            dve.wait_ge(g.agg_ready.sem, g.agg_ready.at(n - RING + 1))
                        nc.vector.tensor_scalar(hot[:, s, :], iota[:], dloc[:, bass.ds(n, 1)], None, ALU.is_equal).then_inc(g.one_hot.sem, 1)

                    def message(n, i, j, first):
                        s = j % RING
                        dve.wait_ge(g.core_ready.sem, g.core_ready.at(n + 1))
                        if not (first and j < RING):
                            dve.wait_ge(g.agg_ready.sem, g.agg_ready.at(n - RING + 1))
                        nc.vector.tensor_tensor(msg[:, s, :], ps[0:P, CB, 0:D], b2[:], ALU.add).then_inc(g.msg_done.sem, 1)
                        dve.wait_ge(g.msg_done.sem, g.msg_done.at(2 * n + 1))
                        dve.wait_ge(g.gate_done.sem, g.gate_done.at(n + 1))
                        nc.vector.tensor_tensor(msg[:, s, :], msg[:, s, :], pre[:, s, D:2 * D], ALU.mult).then_inc(g.msg_done.sem, 1)

                    def add(n, i, j, first):
                        if j % RING == 0:
                            windows[:] = starts(dve, nc.vector, (GE // RING) * i + j // RING)
                        b = windows[j % RING]
                        dve.wait_ge(g.agg_ready.sem, g.agg_ready.at(n + 1))
                        dve.wait_ge(g.added.sem, g.added.at(n + 1))
                        f = featT[:, :, bass.ds(b, P)]
                        nc.vector.tensor_tensor(f, f, ps[:, AB + j % 2, 0:KD * P].rearrange("p (k t) -> p k t", k=KD), ALU.add).then_inc(g.added.sem, 1)
                    steps(dve, NCH, GE, [(3, gpre), (1, message), (0, add)])
        gathers_passed(GE // RING)
        for s in store:
            s.passed(16 * NCH // RING)
        g.loaded.passed(16 * NL), g.added.passed(1 + NCH), g.msg_done.passed(2 * NCH)
        for s in (g.ea_turned, g.eaT_ready, g.pre_ready, g.tile_ready, g.relu_done, g.gpre_done, g.gate_done, g.core_ready, g.one_hot, g.agg_ready):
            s.passed(NCH)

    def sums_to_xn():
        def use(dve, n, j, c0):
            nc.vector.tensor_tensor(tile_of(xn, n), tile_of(xn, n), ps[0:P, j, 0:D], ALU.add).then_inc(g.chain.sem, 1)
        tiles([], None, [], turn_back(False), use, 1)

    def choose(tag, L, T, E, softmaxes, W, picks, iota_e, work, wT, load_scale=None, index_out=None, pw=None):
        ch = g.chain
        marks = []
        t3 = lambda k: work[:, k * T * E:(k + 1) * T * E].rearrange("p (t e) -> p t e", e=E)
        v2 = lambda k: work[:, 6 * T * E + (k - 6) * T:6 * T * E + (k - 5) * T]
        bc = lambda ap: ap.unsqueeze(2).to_broadcast([P, T, E])
        ie = iota_e[:, 0:E].unsqueeze(1).to_broadcast([P, T, E])
        groups = [list(range(q, min(q + BT, NT))) for q in range(0, NT, BT)] if wT is not None else []
        with nc.Block() as block:
            count = [0]

            @block.vector
            def _(dve):
                def link(ins):
                    count[0] += 1
                    ins.then_inc(ch.sem, 1)
                    dve.wait_ge(ch.sem, ch.at(count[0]))

                def exp_of(ap):
                    marks.append((count[0], ap))
                    dve.wait_ge(g.act_step.sem, g.act_step.at(len(marks)))

                def softmax(a):
                    link(nc.vector.tensor_reduce(v2(6), a, X, ALU.max))
                    link(nc.vector.tensor_tensor(a, a, bc(v2(6)), ALU.subtract))
                    exp_of(a)
                    link(nc.vector.tensor_reduce(v2(6), a, X, ALU.add))
                    link(nc.vector.reciprocal(v2(7), v2(6)))
                    link(nc.vector.tensor_tensor(a, a, bc(v2(7)), ALU.mult))

                a = L
                if softmaxes >= 1:
                    softmax(a)
                if softmaxes == 2:
                    cap, per_load = load_scale
                    link(nc.vector.tensor_scalar(t3(0), a, per_load, None, ALU.mult))
                    link(nc.vector.reciprocal(t3(1), t3(0)))
                    link(nc.vector.tensor_scalar(t3(1), t3(1), cap, -1.0, ALU.mult, ALU.add))
                    link(nc.vector.tensor_scalar(t3(0), t3(0), cap, None, ALU.is_gt))
                    link(nc.vector.tensor_scalar(t3(1), t3(1), 3e38, None, ALU.min))
                    link(nc.vector.tensor_tensor(t3(1), t3(1), t3(0), ALU.mult))
                    link(nc.vector.tensor_scalar(t3(1), t3(1), 1.0, None, ALU.add))
                    link(nc.vector.tensor_tensor(a, a, t3(1), ALU.mult))
                    softmax(a)
                for k in range(picks):
                    link(nc.vector.tensor_reduce(v2(8 + k), a, X, ALU.max))
                    link(nc.vector.tensor_tensor(t3(0), a, bc(v2(8 + k)), ALU.not_equal))
                    link(nc.vector.scalar_tensor_tensor(t3(0), t3(0), 1024.0, ie, ALU.mult, ALU.add) if T == 1 else
                         nc.vector.tensor_scalar(t3(0), t3(0), 1024.0, None, ALU.mult))
                    if T > 1:
                        link(nc.vector.tensor_tensor(t3(0), t3(0), ie, ALU.add))
                    link(nc.vector.tensor_reduce(v2(6), t3(0), X, ALU.min))
                    if index_out is not None:
                        link(nc.vector.tensor_copy(index_out[0:1, k:k + 1], v2(6)[0:1, :]))
                    link(nc.vector.tensor_tensor(t3(2 + k), ie, bc(v2(6)), ALU.is_equal))
                    if k + 1 < picks:
                        link(nc.vector.tensor_scalar(t3(1), t3(2 + k), -3e38, None, ALU.mult))
                        link(nc.vector.tensor_tensor(t3(4), t3(2 + k), a, ALU.mult))
                        link(nc.vector.tensor_tensor(a, a, t3(4), ALU.subtract))
                        link(nc.vector.tensor_tensor(a, a, t3(1), ALU.add))
                if picks == 2:
                    link(nc.vector.tensor_tensor(v2(9), v2(9), v2(8), ALU.subtract))
                    exp_of(v2(9))
                    link(nc.vector.tensor_scalar(v2(6), v2(9), 1.0, None, ALU.add))
                    link(nc.vector.reciprocal(v2(6), v2(6)))
                    link(nc.vector.tensor_tensor(v2(7), v2(9), v2(6), ALU.mult))
                    if pw is not None:
                        for k in range(2):
                            link(nc.vector.tensor_copy(pw[:, k, :], v2(6 + k)))
                    elif index_out is None:
                        link(nc.vector.tensor_tensor(t3(2), t3(2), bc(v2(6)), ALU.mult))
                        link(nc.vector.tensor_tensor(t3(3), t3(3), bc(v2(7)), ALU.mult))
                        link(nc.vector.tensor_tensor(W, t3(2), t3(3), ALU.add))
                    else:
                        for k in range(2):
                            link(nc.vector.tensor_copy(W[:, :, k], v2(6 + k).to_broadcast([P, NT])))
                for q, ts in enumerate(groups):
                    dve.wait_ge(g.turned.sem, g.turned.at(q + 1))
                    nc.vector.tensor_copy(wT[:, ts[0] * P:(ts[-1] + 1) * P], ps[0:wT.shape[0], q, 0:len(ts) * P]).then_inc(ch.sem, 1)

            @block.scalar
            def _(act):
                for at, ap in marks:
                    act.wait_ge(ch.sem, ch.at(at))
                    nc.scalar.activation(ap, ap, ACT.Exp).then_inc(g.act_step.sem, 1)

            @block.tensor
            def _(pe):
                if groups:
                    pe.wait_ge(ch.sem, ch.at(count[0]))
                for q, ts in enumerate(groups):
                    for s, t in enumerate(ts):
                        mm = nc.tensor.transpose(ps[0:wT.shape[0], q, s * P:(s + 1) * P], W[:, t, :], ident[0:P, 0:P])
                    mm.then_inc(g.turned.sem, 1)
        ch.passed(count[0] + len(groups)), g.act_step.passed(len(marks)), g.turned.passed(len(groups))

    def expert_index(iota_e):
        with nc.Block() as block:
            @block.gpsimd
            def _(pool):
                nc.gpsimd.iota(iota_e[:], [[1, 32]], base=0, channel_multiplier=0, allow_small_or_imprecise_dtypes=True)

    def route(load, turn, w, bias, L, E):
        per_bank = 512 // E
        banks = -(-NT // per_bank)
        with nc.Block() as block:
            @block.sync
            def _(sp):
                for d, src in load:
                    sp.dma_start(d, src).then_inc(g.loaded.sem, 16)

            @block.tensor
            def _(pe):
                pe.wait_ge(g.loaded.sem, g.loaded.at(16 * len(load)))
                if turn is not None:
                    for k in range(KD):
                        mm = nc.tensor.transpose(ps[0:128, 7, k * E:(k + 1) * E], turn[:, k * 128:(k + 1) * 128], ident[0:E, 0:E])
                    mm.then_inc(g.turned.sem, 1)
                    pe.wait_ge(g.staged.sem, g.staged.at(1))
                for t in range(NT):
                    for k in range(KD):
                        mm = nc.tensor.matmul(ps[0:P, t // per_bank, t % per_bank * E:(t % per_bank + 1) * E], featT[:, k, t * P:(t + 1) * P], w[:, k, :],
                                              start=(k == 0), stop=(k == KD - 1))
                mm.then_inc(g.tile_ready.sem, 1)

            @block.vector
            def _(dve):
                dve.wait_ge(g.loaded.sem, g.loaded.at(16 * len(load)))
                if turn is not None:
                    dve.wait_ge(g.turned.sem, g.turned.at(1))
                    nc.vector.tensor_copy(w.rearrange("p k e -> p (k e)"), ps[0:128, 7, 0:KD * E]).then_inc(g.staged.sem, 1)
                dve.wait_ge(g.tile_ready.sem, g.tile_ready.at(1))
                for b in range(banks):
                    ts = slice(b * per_bank, min(NT, (b + 1) * per_bank))
                    n = ts.stop - ts.start
                    nc.vector.tensor_tensor(L[:, ts, :], ps[0:P, b, 0:n * E].rearrange("p (t e) -> p t e", e=E),
                                            bias.unsqueeze(1).to_broadcast([P, n, E]), ALU.add)
        g.loaded.passed(16 * len(load)), g.tile_ready.passed(1)
        if turn is not None:
            g.turned.passed(1), g.staged.passed(1)

    def experts(tag, E, load, first_layer, bias_ap, func, second, per_tile, wT, b2, w_ready=None, mask=None, mid=None, W=None, acc=None, late_bias=False):
        F = 4
        FB = F - 2 if mid is not None else 0
        EY = E + 1 if mask is None else 1
        ew_ = wT.shape[0]
        we = lambda e: e if mask is None else 0
        with ExitStack() as c:
            hid = sb(tag + "_hid", [128, 2, F, BT * P], F32, c)
            wts = sb(tag + "_wts", [ew_, BT * P], F32, c)
            with nc.Block() as block:
                @block.sync
                def _(sp):
                    load(sp)

                def counts(b, nt):
                    return b * F * E, b * EY * BT

                def blocks(eng, body):
                    body(0, BT, True)
                    with eng.Fori(1, NB) as b:
                        body(b, BT, False)
                    if NT % BT:
                        body(NB, NT % BT, False)

                @block.tensor
                def _(pe):
                    if late_bias:
                        pe.wait_ge(g.loaded.sem, g.loaded.at(16))

                    def body(b, nt, first):
                        h0, y0 = counts(b, nt)
                        cols = nt * P
                        tail = nt < BT
                        tok = lambda k: featT[:, k, bass.ds(b * BT * P, cols)]
                        pe.wait_ge(g.wt_staged.sem, g.wt_staged.at(b + 1))

                        def hidden(e, fs):
                            if first:
                                pe.wait_ge(wload[we(e)].sem, wload[we(e)].at(w_ready))
                            for f in fs:
                                n = h0 + e * F + f
                                if not (first and e == 0):
                                    hold_pe(g.hid_done, n - F + 1)
                                o = ps[:, f, 0:cols]
                                if mid is not None and f >= 2:
                                    if f == 2:
                                        pe.wait_ge(g.hid_done.sem, g.hid_done.at(h0 + e * F + 2))
                                    for k in range(KD):
                                        mm = nc.tensor.matmul(o, mid(e, f, k), hid[:, e % 2, k, 0:cols], start=(k == 0), stop=(k == KD - 1))
                                else:
                                    for k in range(KD):
                                        mm = nc.tensor.matmul(o, first_layer(e, f, k), tok(k), start=(k == 0), stop=(k == KD - 1 and mask is None))
                                    if mask is not None:
                                        mm = nc.tensor.matmul(o, mask[:, (e * F + f) * 128:(e * F + f + 1) * 128], wts[:, 0:cols], start=False, stop=True)
                                mm.then_inc(g.hid_ready.sem, 1)

                        def outputs(e):
                            if e < E:
                                pe.wait_ge(g.hid_done.sem, g.hid_done.at(h0 + (e + 1) * F))
                            for t in range(nt):
                                y = y0 + (e * nt + t if mask is None else t)
                                if e == 0 or mask is None:
                                    if tail:
                                        pe.wait_ge(g.y_done.sem, g.y_done.at(y))
                                    elif not (first and e == 0):
                                        hold_pe(g.y_done, y - BT + 1)
                                o = ps[0:P, F + t, 0:D]
                                if e < E:
                                    for f in range(FB, F):
                                        mm = nc.tensor.matmul(o, hid[:, e % 2, f, t * P:(t + 1) * P], second(e, f),
                                                              start=(f == FB and (mask is None or e == 0)), stop=(f == F - 1 and mask is None))
                                if (e == E and mask is None) or (mask is not None and e == E - 1):
                                    mm = nc.tensor.matmul(o, wts[:, t * P:(t + 1) * P], b2, start=mask is None, stop=True)
                                if mask is None or e == E - 1:
                                    mm.then_inc(g.y_ready.sem, 1)

                        if mid is None:
                            hidden(0, range(F))
                            for e in range(E):
                                if e + 1 < E:
                                    hidden(e + 1, range(F))
                                outputs(e)
                        else:
                            for s in range(E + 2):
                                if s < E:
                                    hidden(s, (0, 1))
                                if 1 <= s <= E:
                                    hidden(s - 1, (2, 3))
                                if s >= 2:
                                    outputs(s - 2)
                        if mask is None:
                            outputs(E)
                    blocks(pe, body)

                @block.scalar
                def _(act):
                    def body(b, nt, first):
                        h0, y0 = counts(b, nt)
                        cols = nt * P
                        if not first:
                            hold_act(g.y_ready, y0)
                        nc.scalar.copy(wts[:, 0:cols], wT[:, bass.ds(b * BT * P, cols)]).then_inc(g.wt_staged.sem, 1)

                        def chunk(e, f):
                            if first and f == 0 and bias_ap is not None:
                                act.wait_ge(wload[we(e)].sem, wload[we(e)].at(w_ready))
                            hold_act(g.hid_ready, h0 + e * F + f + 1)
                            if bias_ap is not None:
                                nc.scalar.activation(hid[:, e % 2, f, 0:cols], ps[:, f, 0:cols], func, bias=bias_ap(e, f)).then_inc(g.hid_done.sem, 1)
                            else:
                                nc.scalar.activation(hid[:, e % 2, f, 0:cols], ps[:, f, 0:cols], func).then_inc(g.hid_done.sem, 1)
                        if mid is None:
                            for e in range(E):
                                for f in range(F):
                                    chunk(e, f)
                        else:
                            for s in range(E + 1):
                                for f in (0, 1):
                                    if s < E:
                                        chunk(s, f)
                                for f in (2, 3):
                                    if s >= 1:
                                        chunk(s - 1, f)
                    blocks(act, body)

                @block.vector
                def _(dve):
                    def body(b, nt, first):
                        h0, y0 = counts(b, nt)
                        for e in range(EY):
                            for t in range(nt):
                                y = y0 + e * nt + t
                                n = BT * b + t
                                a = tile_of(acc, n)
                                dve.wait_ge(g.y_ready.sem, g.y_ready.at(y + 1))
                                if e > 0:
                                    dve.wait_ge(g.y_done.sem, g.y_done.at(y - nt + 1))
                                o = ps[0:P, F + t, 0:D]
                                if mask is not None:
                                    ins = nc.vector.scalar_tensor_tensor(a, o, 0.0, a, ALU.max, ALU.add)
                                elif e < E:
                                    ins = nc.vector.scalar_tensor_tensor(a, o, W[:, bass.ds(n, 1), e:e + 1].rearrange("p a e -> p (a e)"), a, ALU.mult, ALU.add)
                                else:
                                    ins = nc.vector.tensor_tensor(a, o, a, ALU.add)
                                ins.then_inc(g.y_done.sem, 1)
                    blocks(dve, body)
        tb = NT % BT
        g.hid_ready.passed(F * E * (NB + 1)), g.hid_done.passed(F * E * (NB + 1)), g.wt_staged.passed(NB + 1)
        g.y_ready.passed(EY * NT), g.y_done.passed(EY * NT)
        for e in range(E if mask is None else 1):
            wload[e].passed(w_ready)

    def dispatch(tag, E, picks, work, slot, expert, leads, TS, loads):
        halves_ = ((0, 13), (13, NT))
        with ExitStack() as c:
            upper = sb(tag + "_upper", [P, P], F32, c)
            by_tile = lambda k: work[:, k * NT * E:(k + 1) * NT * E].rearrange("p (t e) -> p t e", e=E)
            hot = lambda k: by_tile(2 + k)
            run = [by_tile(0), by_tile(1)]
            a = by_tile(4)
            cmp = work[:, 5 * NT * E:6 * NT * E].rearrange("p (e t) -> p e t", t=NT)
            step = sb(tag + "_step", [P, NT], F32, c)
            ends = [sb(f"{tag}_ends{q}", [P, E], F32, c) for q in range(2)]
            te = sb(tag + "_te", [P, E], F32, c)
            pos = sb(tag + "_pos", [P, picks, NT], F32, c)
            ecmp = stage[0:1].rearrange("p r c -> p (r c)")[:, 0:TS * E].rearrange("p (s e) -> p s e", e=E)
            ef = sb(tag + "_ef", [1, TS], F32, c)
            count = [0]
            with nc.Block() as block:
                @block.sync
                def _(sp):
                    for d, s in loads:
                        sp.dma_start(d, s).then_inc(g.loaded.sem, 16)

                @block.gpsimd
                def _(pool):
                    nc.gpsimd.affine_select(out=upper[:], in_=ones[0:P, 0:P], pattern=[[1, P]], compare_op=ALU.is_gt, fill=0.0,
                                            base=0, channel_multiplier=-1).then_inc(g.pool_step.sem, 1)
                    pool.wait_ge(g.turned.sem, g.turned.at(2))
                    for t in range(NT):
                        for k in range(picks):
                            nc.gpsimd.indirect_dma_start(out=t_disp[0:TS * P, :], out_offset=bass.IndirectOffsetOnAxis(ap=slot[:, k, t:t + 1], axis=0),
                                                         in_=xn[:, t, :], in_offset=None).then_inc(g.stored.sem, 16)
                    pool.wait_ge(g.stored.sem, g.stored.at(16 * NT * picks))

                @block.tensor
                def _(pe):
                    pe.wait_ge(g.chain.sem, g.chain.at(1))
                    pe.wait_ge(g.pool_step.sem, g.pool_step.at(1))
                    for q, (t0, t1) in enumerate(halves_):
                        nc.tensor.matmul(ps[0:P, q, 0:(t1 - t0) * E], upper[:], a[:, t0:t1, :].rearrange("p t e -> p (t e)"), start=True, stop=True)
                        mm = nc.tensor.matmul(ps[0:P, 2 + q, 0:(t1 - t0) * E], ones[0:P, 0:P], a[:, t0:t1, :].rearrange("p t e -> p (t e)"), start=True, stop=True)
                    mm.then_inc(g.turned.sem, 1)

                @block.vector
                def _(dve):
                    def link(ins):
                        count[0] += 1
                        ins.then_inc(g.chain.sem, 1)
                        dve.wait_ge(g.chain.sem, g.chain.at(count[0]))

                    def from_psum(b, t0, t1):
                        return ps[0:P, b, 0:(t1 - t0) * E].rearrange("p (t e) -> p t e", e=E)

                    def running(bufs, length, at):
                        q, d = 0, 1
                        while d < length:
                            link(nc.vector.tensor_copy(at(bufs[1 - q], 0, d), at(bufs[q], 0, d)))
                            link(nc.vector.tensor_tensor(at(bufs[1 - q], d, length), at(bufs[q], d, length), at(bufs[q], 0, length - d), ALU.add))
                            q, d = 1 - q, 2 * d
                        return q

                    if picks == 2:
                        link(nc.vector.tensor_tensor(a, hot(0), hot(1), ALU.add))
                    else:
                        link(nc.vector.tensor_copy(a, hot(0)))
                    link(nc.vector.tensor_scalar(step[:], iota[:, 0:NT], float(P), None, ALU.mult))
                    dve.wait_ge(g.turned.sem, g.turned.at(1))
                    for q, (t0, t1) in enumerate(halves_):
                        link(nc.vector.tensor_copy(run[0][:, t0:t1, :], from_psum(2 + q, t0, t1)))
                    r = running(run, NT, lambda b, u, v: b[:, u:v, :])
                    total = run[r][:, NT - 1:NT, :].rearrange("p a e -> p (a e)")
                    link(nc.vector.tensor_tensor(cmp, total.unsqueeze(2).to_broadcast([P, E, NT]), step[:].unsqueeze(1).to_broadcast([P, E, NT]), ALU.is_gt))
                    link(nc.vector.tensor_reduce(te[:], cmp, X, ALU.add))
                    link(nc.vector.tensor_copy(ends[0][:], te[:]))
                    z = running(ends, E, lambda b, u, v: b[:, u:v])
                    link(nc.vector.tensor_tensor(ecmp, iota[0:1, 0:TS].unsqueeze(2).to_broadcast([1, TS, E]), ends[z][0:1, :].unsqueeze(1).to_broadcast([1, TS, E]), ALU.is_ge))
                    link(nc.vector.tensor_reduce(ef[:], ecmp, X, ALU.add))
                    link(nc.vector.tensor_scalar(ef[:], ef[:], float(E - 1), None, ALU.min))
                    link(nc.vector.memset(expert[:], 0))
                    for l, lead in enumerate(leads):
                        link(nc.vector.tensor_copy(expert[:, l, 0:TS - lead], ef[:, lead:TS]))
                    link(nc.vector.tensor_tensor(te[:], ends[z][:], te[:], ALU.subtract))
                    link(nc.vector.tensor_scalar(te[:], te[:], float(P), None, ALU.mult))
                    for q, (t0, t1) in enumerate(halves_):
                        link(nc.vector.tensor_tensor(run[r][:, t0:t1, :], run[r][:, t0:t1, :], from_psum(2 + q, t0, t1), ALU.subtract))
                        link(nc.vector.tensor_tensor(run[r][:, t0:t1, :], run[r][:, t0:t1, :], from_psum(q, t0, t1), ALU.add))
                    link(nc.vector.tensor_tensor(run[r], run[r], te[:].unsqueeze(1).to_broadcast([P, NT, E]), ALU.add))
                    for k in range(picks):
                        link(nc.vector.tensor_tensor(run[1 - r], run[r], hot(k), ALU.mult))
                        link(nc.vector.tensor_reduce(pos[:, k, :], run[1 - r], X, ALU.add))
                    nc.vector.tensor_copy(slot[:], pos[:]).then_inc(g.turned.sem, 1)
            g.chain.passed(count[0]), g.turned.passed(2), g.pool_step.passed(1), g.stored.passed(16 * NT * picks)

    def expert_tiles(E, TS, expert, leads, LD, layers):
        NLAY = len(layers)
        R = 4
        RI = LOT
        cut = Carver(featT[:].rearrange("p k n -> p (k n)"))
        xd = stage[0:P].rearrange("p r c -> p (r c)")[:, 0:RI * D].rearrange("p (r d) -> p r d", r=RI)
        inT = [cut.take(128, R * P * ((w[0] + 127) // 128)).rearrange("p (r k t) -> p r k t", r=R, t=P) for w in layers]
        pre = [cut.take(P, R * w[1]).rearrange("p (r d) -> p r d", r=R) for w in layers]

        def tile_experts(eng, ns, l):
            held = []

            def of(n, j):
                if j == leads[l]:
                    reads[0] += 1
                    regs = [eng.alloc_register(f"expert{reads[0]}_{r}") for r in range(LOT)]
                    ns.load(regs, expert[0:1, l, bass.ds(n - leads[l], LOT)])
                    held[:] = [ns.snap(r, donate=True, min_val=0, max_val=E - 1) for r in regs]
                return held[(j - leads[l]) % LOT] if held else ns.value_load(expert[0:1, NLAY - 1, n:n + 1], min_val=0, max_val=E - 1)
            return of

        TB = lambda l: 2 * l
        MB = lambda l: 2 * l + 1
        turned = [g.turned, g.pre_ready, g.hid_ready]
        in_ready = [g.evicted, g.relu_done, g.hid_done]
        product = [g.tile_ready, g.core_ready, g.y_ready]
        biased = [g.staged, g.msg_done, g.y_done]
        with nc.Block() as block:
            @block.sync
            def _(sp):
                def rows_in(n, i, j, first):
                    if not first:
                        sp.wait_ge(turned[0].sem, turned[0].at(n - RI + 1))
                    sp.dma_start(xd[:, j, :], t_disp[bass.ds(P * n, P), :]).then_inc(wload[j].sem, 16)
                steps(sp, TS, RI, [(0, rows_in)])

            @block.gpsimd
            def _(pool):
                def rows_out(n, i, j, first):
                    hold_pool(biased[NLAY - 1], n + 1)
                    pool.dma_start(t_back[bass.ds(P * n, P), :], pre[-1][:, j, :]).then_inc(gath[j].sem, 16)
                steps(pool, TS, R, [(0, rows_out)])
                for j in range(R):
                    pool.wait_ge(gath[j].sem, gath[j].at(16 * ((TS - j + R - 1) // R)))

            @block.tensor
            def _(pe):
                pe.wait_ge(g.loaded.sem, g.loaded.at(16 * LD))

                def turn(l):
                    wide = layers[l][0]

                    def f(n, i, j, first):
                        if l == 0:
                            hold_pe(wload[j], 16 * (i + 1))
                        else:
                            hold_pe(biased[l - 1], n + 1)
                        if not (first and j == 0):
                            hold_pe(in_ready[l], n)
                        src = xd[:, j, :] if l == 0 else pre[l - 1][:, j % R, :]
                        for k in range((wide + 127) // 128):
                            w = min(128, wide - 128 * k)
                            mm = nc.tensor.transpose(ps[0:w, TB(l), k * P:(k + 1) * P], src[:, 128 * k:128 * k + w], ident[0:P, 0:P])
                        mm.then_inc(turned[l].sem, 1)
                    return f

                def multiply(l):
                    wide, out_w, weights = layers[l][0:3]

                    expert_of = tile_experts(pe, nc.tensor, l)

                    def f(n, i, j, first):
                        e = expert_of(n, j)
                        hold_pe(in_ready[l], n + 1)
                        if not (first and j == 0):
                            hold_pe(biased[l], n)
                        kk = (wide + 127) // 128
                        for k in range(kk):
                            w = min(128, wide - 128 * k)
                            mm = nc.tensor.matmul(ps[0:P, MB(l), 0:out_w], inT[l][0:w, j % R, k, :], weights(e, k), start=(k == 0), stop=(k == kk - 1))
                        mm.then_inc(product[l].sem, 1)
                    return f
                parts = []
                for l in range(NLAY):
                    parts += [(leads[l] + 1, turn(l)), (leads[l], multiply(l))]
                steps(pe, TS, RI, parts)

            @block.scalar
            def _(act):
                def copy_in(l):
                    wide, func = layers[l][0], layers[l][4]

                    def f(n, i, j, first):
                        hold_act(turned[l], n + 1)
                        if not first:
                            hold_act(product[l], n - R + 1)
                        w = min(128, wide)
                        nc.scalar.activation(inT[l][0:w, j], ps[0:w, TB(l), 0:((wide + 127) // 128) * P].rearrange("p (k t) -> p k t", t=P), func).then_inc(in_ready[l].sem, 1)
                    return f
                steps(act, TS, R, [(leads[l] + 1, copy_in(l)) for l in range(NLAY)])

            @block.vector
            def _(dve):
                dve.wait_ge(g.loaded.sem, g.loaded.at(16 * LD))

                def add_bias(l):
                    out_w, bias = layers[l][1], layers[l][3]

                    expert_of = tile_experts(dve, nc.vector, l)

                    def f(n, i, j, first):
                        e = expert_of(n, j)
                        if not (first and j < R):
                            if l + 1 < NLAY:
                                dve.wait_ge(turned[l + 1].sem, turned[l + 1].at(n - R + 1))
                            else:
                                dve.wait_ge(gath[j % R].sem, gath[j % R].at(16 * ((RI // R) * i + j // R)))
                        dve.wait_ge(product[l].sem, product[l].at(n + 1))
                        nc.vector.tensor_tensor(pre[l][:, j % R, :], ps[0:P, MB(l), 0:out_w], bias(e), ALU.add).then_inc(biased[l].sem, 1)
                    return f
                steps(dve, TS, RI, [(leads[l], add_bias(l)) for l in range(NLAY)])
        g.loaded.passed(16 * LD)
        for q in (turned, in_ready, product, biased):
            for l in range(NLAY):
                q[l].passed(TS)
        for j in range(R):
            gath[j].passed(16 * ((TS - j + R - 1) // R))
        for j in range(RI):
            wload[j].passed(16 * ((TS - j + RI - 1) // RI))

    def collect(tag, picks, slot, pw, TS):
        with ExitStack() as c:
            y = sb(tag + "_y", [P, GR, D], F32, c)
            total = NT * picks
            with nc.Block() as block:
                @block.gpsimd
                def _(pool):
                    for n in range(total):
                        t, k, j = n // picks, n % picks, n % GR
                        if n >= GR:
                            pool.wait_ge(g.used.sem, g.used.at(n - GR + 1))
                        nc.gpsimd.indirect_dma_start(out=y[:, j, :], out_offset=None, in_=t_back[0:TS * P, :],
                                                     in_offset=bass.IndirectOffsetOnAxis(ap=slot[:, k, t:t + 1], axis=0)).then_inc(gath[j].sem, 16)

                @block.vector
                def _(dve):
                    for n in range(total):
                        t, k, j = n // picks, n % picks, n % GR
                        dve.wait_ge(gath[j].sem, gath[j].at(16 * (n // GR + 1)))
                        if k > 0:
                            dve.wait_ge(g.used.sem, g.used.at(n))
                        if pw is not None:
                            ins = nc.vector.scalar_tensor_tensor(xres[:, t, :], y[:, j, :], pw[:, k, t:t + 1], xres[:, t, :], ALU.mult, ALU.add)
                        else:
                            ins = nc.vector.scalar_tensor_tensor(xres[:, t, :], y[:, j, :], 0.0, xres[:, t, :], ALU.max, ALU.add)
                        ins.then_inc(g.used.sem, 1)
        g.used.passed(total)
        for j in range(GR):
            gath[j].passed(16 * ((total - j + GR - 1) // GR))

    def ffn0():
        E = 8
        CAP = float(-((-N * 5) // (4 * E)))
        with ExitStack() as c:
            wr = sb("f0_wr", [128, KD, E], F32, c)
            br = sb("f0_br", [P, E], F32, c)
            mean = sb("f0_mean", [128, KD, P + 1], F32, c)
            L = sb("f0_L", [P, 1, E], F32, c)
            W = sb("f0_W", [P, NT, 2], F32, c)
            wT = sb("f0_wT", [2, N], F32, c)
            iota_e = sb("f0_iota", [P, 32], F32, c)
            work = sb("f0_work", [P, 6 * E + 4], F32, c)
            pick = sb("f0_pick", [1, 2], I32, c)
            w1 = sb("f0_w1", [128, 2, KD, 512], F32, c)
            w2 = sb("f0_w2", [128, 2, 4, D], F32, c)
            b1 = sb("f0_b1", [128, 2, 4], F32, c)
            b2 = sb("f0_b2", [2, D], F32, c)
            b1rows = sb("f0_b1r", [4, 2, 128], F32, c)
            expert_index(iota_e)
            with nc.Block() as block:
                @block.sync
                def _(sp):
                    sp.dma_start(wr[:], halves(io["L0_ffn_Wr"])).then_inc(g.loaded.sem, 16)
                    sp.dma_start(br[:], io["L0_ffn_br"].partition_broadcast(P)).then_inc(g.loaded.sem, 16)

                @block.vector
                def _(dve):
                    nc.vector.tensor_reduce(mean[:, :, P:P + 1], featT[:, :, 0:N], X, ALU.add).then_inc(g.chain.sem, 1)
                    wait_chain(dve, 1)
                    nc.vector.tensor_scalar(mean[:, :, P:P + 1], mean[:, :, P:P + 1], 1.0 / N, None, ALU.mult).then_inc(g.chain.sem, 1)
                    wait_chain(dve, 2)
                    nc.vector.tensor_copy(mean[:, :, 0:P], mean[:, :, P:P + 1].to_broadcast([128, KD, P])).then_inc(g.chain.sem, 1)
                    dve.wait_ge(g.turned.sem, g.turned.at(1))
                    nc.vector.tensor_tensor(L[:, 0, :], ps[0:P, 0, 0:E], br[:], ALU.add).then_inc(g.chain.sem, 1)

                @block.tensor
                def _(pe):
                    pe.wait_ge(g.loaded.sem, g.loaded.at(32))
                    pe.wait_ge(g.chain.sem, g.chain.at(3))
                    for k in range(KD):
                        mm = nc.tensor.matmul(ps[0:P, 0, 0:E], mean[:, k, 0:P], wr[:, k, :], start=(k == 0), stop=(k == KD - 1))
                    mm.then_inc(g.turned.sem, 1)
            g.loaded.passed(32), g.chain.passed(4), g.turned.passed(1)
            choose("f0", L[:], 1, E, 2, W, 2, iota_e, work[:], wT, load_scale=(CAP, float(N)), index_out=pick)

            def load(sp):
                for j in range(2):
                    r = nc.sync.value_load(pick[0:1, j:j + 1], min_val=0, max_val=E - 1)
                    sp.dma_start(w1[:, j], io["L0_ffn_W1"][bass.ds(r, 1)].rearrange("e (k p) f -> p (e k) f", p=128)).then_inc(wload[j].sem, 16)
                    sp.dma_start(w2[:, j], io["L0_ffn_W2"][bass.ds(r, 1)].rearrange("e (k p) f -> p (e k) f", p=128)).then_inc(wload[j].sem, 16)
                    sp.dma_start(b1rows[:, j, :], io["L0_ffn_b1"][bass.ds(r, 1)].rearrange("e (f p) -> (e f) p", p=128)).then_inc(wload[j].sem, 16)
                    sp.dma_start(b2[j:j + 1, :], io["L0_ffn_b2"][bass.ds(r, 1)]).then_inc(wload[j].sem, 16)
            with nc.Block() as block:
                @block.sync
                def _(sp):
                    load(sp)

                @block.tensor
                def _(pe):
                    for j in range(2):
                        pe.wait_ge(wload[j].sem, wload[j].at(64))
                        mm = nc.tensor.transpose(ps[:, 0, 4 * j:4 * j + 4], b1rows[:, j, :], ident[0:4, 0:4])
                    mm.then_inc(g.turned.sem, 1)

                @block.vector
                def _(dve):
                    dve.wait_ge(g.turned.sem, g.turned.at(1))
                    nc.vector.tensor_copy(b1[:].rearrange("p e f -> p (e f)"), ps[:, 0, 0:8])
            g.turned.passed(1)
            experts("f0", 2, lambda sp: None, lambda e, f, k: w1[:, e, k, f * 128:(f + 1) * 128], lambda e, f: b1[:, e, f:f + 1],
                    ACT.Gelu, lambda e, f: w2[:, e, f, :], 2, wT, b2[:], w_ready=64, W=W, acc=xn)

    def biases(tag, b, rows, cols, dst):
        with ExitStack() as c:
            raw = sb(tag + "_bias_rows", [rows * cols, 128], F32, c)
            with nc.Block() as block:
                @block.sync
                def _(sp):
                    sp.dma_start(raw[:], b).then_inc(g.loaded.sem, 16)

                @block.tensor
                def _(pe):
                    pe.wait_ge(g.loaded.sem, g.loaded.at(16))
                    nc.tensor.transpose(ps[:, 0, 0:rows * cols], raw[:], ident[0:rows * cols, 0:rows * cols]).then_inc(g.turned.sem, 1)

                @block.vector
                def _(dve):
                    dve.wait_ge(g.turned.sem, g.turned.at(1))
                    nc.vector.tensor_copy(dst, ps[:, 0, 0:rows * cols])
            g.loaded.passed(16), g.turned.passed(1)

    def one_row(ap, e):
        return ap[0:P, bass.ds(e, 1), :].rearrange("p a d -> p (a d)")

    def ffn1():
        E, RH = 6, 128
        TS = 2 * NT + E
        with ExitStack() as c:
            pw = sb("f1_pw", [P, 2, NT], F32, c)
            slot = sb("f1_slot", [P, 2, NT], I32, c)
            leads = [2 * l for l in reversed(range(3))]
            expert = sb("f1_expert", [1, 3, -(-TS // LOT) * LOT], I32, c)
            with ExitStack() as c2:
                rw1 = sb("f1_rw1", [128, KD, RH], F32, c2)
                rb1 = sb("f1_rb1", [RH, 1], F32, c2)
                rw2 = sb("f1_rw2", [RH, E], F32, c2)
                rb2 = sb("f1_rb2", [P, E], F32, c2)
                L = sb("f1_L", [P, NT, E], F32, c2)
                iota_e = sb("f1_iota", [P, 32], F32, c2)
                work = featT[0:P].rearrange("p k n -> p (k n)")
                rh = sb("f1_rh", [RH, RING, P], F32, c2)
                expert_index(iota_e)
                biases("f1_r", io["L1_ffn_router_b1"].rearrange("(a p) -> a p", a=1), 1, 1, rb1[:])
                with nc.Block() as block:
                    @block.sync
                    def _(sp):
                        sp.dma_start(rw1[:], halves(io["L1_ffn_router_w1"])).then_inc(g.loaded.sem, 16)
                        sp.dma_start(rw2[:], io["L1_ffn_router_w2"]).then_inc(g.loaded.sem, 16)
                        sp.dma_start(rb2[:], io["L1_ffn_router_b2"].partition_broadcast(P)).then_inc(g.loaded.sem, 16)

                    @block.tensor
                    def _(pe):
                        pe.wait_ge(g.loaded.sem, g.loaded.at(48))

                        def hidden(n, i, j, first):
                            if not first:
                                hold_pe(g.chain, n - RING + 1)
                            for k in range(KD):
                                mm = nc.tensor.matmul(ps[:, j, 0:P], rw1[:, k, :], featT[:, k, bass.ds(P * n, P)], start=(k == 0), stop=(k == KD - 1))
                            mm.then_inc(g.hid_ready.sem, 1)

                        def logits(n, i, j, first):
                            hold_pe(g.staged, n + 1)
                            nc.tensor.matmul(ps[0:P, j, 256:256 + E], rh[:, j, :], rw2[:], start=True, stop=True).then_inc(g.tile_ready.sem, 1)
                        steps(pe, NT, RING, [(3, hidden), (0, logits)])

                    @block.scalar
                    def _(act):
                        def body(i, first):
                            for j in range(RING):
                                n = RING * i + j
                                hold_act(g.hid_ready, n + 1)
                                nc.scalar.activation(rh[:, j, :], ps[:, j, 0:P], ACT.Relu, bias=rb1[:]).then_inc(g.staged.sem, 1)
                        rounds(act, NT // RING, body)

                    @block.vector
                    def _(dve):
                        dve.wait_ge(g.loaded.sem, g.loaded.at(48))
                        def body(i, first):
                            for j in range(RING):
                                n = RING * i + j
                                dve.wait_ge(g.tile_ready.sem, g.tile_ready.at(n + 1))
                                nc.vector.tensor_tensor(tile_of(L, n), ps[0:P, j, 256:256 + E], rb2[:], ALU.add).then_inc(g.chain.sem, 1)
                        rounds(dve, NT // RING, body)
                g.loaded.passed(48)
                for s in (g.hid_ready, g.staged, g.tile_ready, g.chain):
                    s.passed(NT)
                choose("f1", L[:], NT, E, 1, None, 2, iota_e, work, None, pw=pw)
            w = [sb(f"f1_w{i}", [128, E, KD, D], F32, c) for i in range(3)]
            b = [sb(f"f1_b{i}", [128, E, D], F32, c) for i in range(3)]
            loads = []
            for i in range(3):
                loads.append((w[i][:].rearrange("p e k f -> p (e k) f"), io[f"L1_ffn_expert_w{i + 1}"].rearrange("e (k p) f -> p (e k) f", p=128)))
                loads.append((b[i][:].rearrange("p e f -> p (e f)"), io[f"L1_ffn_expert_b{i + 1}"].rearrange("e f -> (e f)").partition_broadcast(128)))
            dispatch("f1d", E, 2, work, slot, expert, leads, TS, loads)
            expert_tiles(E, TS, expert, leads, len(loads),
                         [(D, D, (lambda i: lambda e, k: w[i][:, bass.ds(e, 1), k, :].rearrange("p a f -> p (a f)"))(i),
                           (lambda i: lambda e: one_row(b[i], e))(i), ACT.Copy if i == 0 else ACT.Relu) for i in range(3)])
            collect("f1c", 2, slot, pw, TS)

    def ffn2():
        E, H = 32, 64
        TS = NT + E
        with ExitStack() as c:
            slot = sb("f2_slot", [P, 1, NT], I32, c)
            leads = [2 * l for l in reversed(range(2))]
            expert = sb("f2_expert", [1, 2, -(-TS // LOT) * LOT], I32, c)
            with ExitStack() as c2:
                raw = sb("f2_rw", [E, D], F32, c2)
                rw = sb("f2_rwT", [128, KD, E], F32, c2)
                rb = sb("f2_rb", [P, E], F32, c2)
                L = sb("f2_L", [P, NT, E], F32, c2)
                iota_e = sb("f2_iota", [P, 32], F32, c2)
                work = featT[0:P].rearrange("p k n -> p (k n)")
                expert_index(iota_e)

                route([(raw[:], io["L2_ffn_router_w"]), (rb[:], io["L2_ffn_router_b"].partition_broadcast(P))], raw[:], rw[:], rb[:], L[:], E)
                choose("f2", L[:], NT, E, 0, None, 1, iota_e, work, None)
            w1 = sb("f2_w1", [128, E, KD, H], F32, c)
            w2 = sb("f2_w2", [H, E, D], F32, c)
            b1 = sb("f2_b1", [128, E, H], F32, c)
            b2 = sb("f2_b2", [128, E, D], F32, c)
            loads = [(w1[:].rearrange("p e k h -> p (e k) h"), io["L2_ffn_W1"].rearrange("e (k p) h -> p (e k) h", p=128)),
                     (w2[:], io["L2_ffn_W2"].rearrange("e h d -> h e d")),
                     (b1[:].rearrange("p e h -> p (e h)"), io["L2_ffn_b1"].rearrange("e h -> (e h)").partition_broadcast(128)),
                     (b2[:].rearrange("p e d -> p (e d)"), io["L2_ffn_b2"].rearrange("e d -> (e d)").partition_broadcast(128))]
            dispatch("f2d", E, 1, work, slot, expert, leads, TS, loads)
            expert_tiles(E, TS, expert, leads, len(loads),
                         [(D, H, lambda e, k: w1[:, bass.ds(e, 1), k, :].rearrange("p a h -> p (a h)"), lambda e: one_row(b1, e), ACT.Copy),
                          (H, D, lambda e, k: w2[:, bass.ds(e, 1), :].rearrange("p a d -> p (a d)"), lambda e: one_row(b2, e), ACT.Relu)])
            collect("f2c", 1, slot, None, TS)

    def ffn3():
        E, H = 8, 512
        TS = 2 * NT + E
        with ExitStack() as c:
            pw = sb("f3_pw", [P, 2, NT], F32, c)
            slot = sb("f3_slot", [P, 2, NT], I32, c)
            leads = [2 * l for l in reversed(range(2))]
            expert = sb("f3_expert", [1, 2, -(-TS // LOT) * LOT], I32, c)
            with ExitStack() as c2:
                wr = sb("f3_wr", [128, KD, E], F32, c2)
                br = sb("f3_br", [P, E], F32, c2)
                L = sb("f3_L", [P, NT, E], F32, c2)
                iota_e = sb("f3_iota", [P, 32], F32, c2)
                work = featT[0:P].rearrange("p k n -> p (k n)")
                expert_index(iota_e)

                route([(wr[:], halves(io["L3_ffn_Wr"])), (br[:], io["L3_ffn_br"].partition_broadcast(P))], None, wr[:], br[:], L[:], E)
                choose("f3", L[:], NT, E, 0, None, 2, iota_e, work, None, pw=pw)
            w1 = sb("f3_w1", [128, E, KD, H], F32, c)
            w2 = sb("f3_w2", [128, E, H // 128, D], F32, c)
            b1 = sb("f3_b1", [128, E, H], F32, c)
            b2 = sb("f3_b2", [128, E, D], F32, c)
            loads = [(w1[:].rearrange("p e k f -> p (e k) f"), io["L3_ffn_W1"].rearrange("e (k p) f -> p (e k) f", p=128)),
                     (w2[:].rearrange("p e k f -> p (e k) f"), io["L3_ffn_W2"].rearrange("e (k p) f -> p (e k) f", p=128)),
                     (b1[:].rearrange("p e f -> p (e f)"), io["L3_ffn_b1"].rearrange("e f -> (e f)").partition_broadcast(128)),
                     (b2[:].rearrange("p e f -> p (e f)"), io["L3_ffn_b2"].rearrange("e f -> (e f)").partition_broadcast(128))]
            dispatch("f3d", E, 2, work, slot, expert, leads, TS, loads)
            expert_tiles(E, TS, expert, leads, len(loads),
                         [(D, H, lambda e, k: w1[:, bass.ds(e, 1), k, :].rearrange("p a f -> p (a f)"), lambda e: one_row(b1, e), ACT.Copy),
                          (H, D, lambda e, k: w2[:, bass.ds(e, 1), k, :].rearrange("p a f -> p (a f)"), lambda e: one_row(b2, e), ACT.Gelu)])
            collect("f3c", 2, slot, pw, TS)

    def attention():
        with ExitStack() as c:
            hst = sb("hst", [P, NT, 2 * HEADS], F32, c)
            own = sb("own", [P, NT, HEADS], F32, c)
            shift = sb("shift", [P, NT, HEADS], F32, c)
            top = sb("top", [P, 2, HEADS], F32, c)
            sums = sb("att_sums", [128, KD + 1, N + P], F32, c)
            att_project(hst)
            att_shift(hst, own, shift, top)
            att_pass(own, hst, shift, top, sums)
            att_finish(sums, own, shift, top)

    stages = [
        lambda: (prepare(), normalize("n0", xres, to_featT=True), attention()),
        lambda: (normalize("n1", xres, to_xn=True, to_featT=True), ffn0(),
                 normalize("n2", xn, gamma=io["L0_ffn_gamma"], beta=io["L0_ffn_beta"], add_to_x=True)),
        lambda: (normalize("n3", xres, table=t_row), edge_pass("sum", t_row, weight=ew, clear=t_disp), sum_finish()),
        lambda: (normalize("n4", xres, to_xn=True, to_featT=True), ffn1()),
        lambda: (normalize("n5", xres, table=t_row, scale=dinv), edge_pass("c1", t_row, loops=True), conv_finish(1, t_row2),
                 edge_pass("c2", t_row2, loops=True), conv_finish(2, t_row), edge_pass("c3", t_row, loops=True), conv_finish(3, None)),
        lambda: (normalize("n6", xres, to_xn=True, to_featT=True), ffn2()),
        lambda: (normalize("n7", xres, to_xn=True, to_featT=True), edge_project(), edge_gated(), sums_to_xn(),
                 normalize("n8", xn, gamma=io["L3_gnn_gamma"], beta=io["L3_gnn_beta"], add_to_x=True)),
        lambda: (normalize("n9", xres, to_xn=True),
                 normalize("n10", xn, gamma=io["L3_ffn_gamma"], beta=io["L3_ffn_beta"], to_xn=True, to_featT=True), ffn3()),
    ]
    for s in stages[:stop]:
        s()
    with nc.Block() as block:
        @block.gpsimd
        def _(pool):
            pool.dma_start(out.rearrange("(t p) d -> p t d", p=P), xres[:]).then_inc(g.stored.sem, 16)
            pool.wait_ge(g.stored.sem, g.stored.at(16))


_INS = ["x", "src", "dst", "edge_attr_64", "edge_weight", "L0_gnn_W", "L0_gnn_b", "L0_gnn_a_src", "L0_gnn_a_trg", "L0_ffn_Wr",
        "L0_ffn_br", "L0_ffn_W1", "L0_ffn_b1", "L0_ffn_W2", "L0_ffn_b2", "L0_ffn_gamma", "L0_ffn_beta", "L1_gnn_weight",
        "L1_ffn_router_w1", "L1_ffn_router_b1", "L1_ffn_router_w2", "L1_ffn_router_b2", "L1_ffn_expert_w1", "L1_ffn_expert_b1",
        "L1_ffn_expert_w2", "L1_ffn_expert_b2", "L1_ffn_expert_w3", "L1_ffn_expert_b3", "L2_gnn_W1", "L2_gnn_b1", "L2_gnn_W2",
        "L2_gnn_b2", "L2_gnn_W3", "L2_gnn_b3", "L2_ffn_router_w", "L2_ffn_router_b", "L2_ffn_W1", "L2_ffn_b1", "L2_ffn_W2",
        "L2_ffn_b2", "L3_gnn_W1", "L3_gnn_b1", "L3_gnn_W2", "L3_gnn_b2", "L3_gnn_Wg", "L3_gnn_bg", "L3_gnn_gamma", "L3_gnn_beta",
        "L3_ffn_gamma", "L3_ffn_beta", "L3_ffn_Wr", "L3_ffn_br", "L3_ffn_W1", "L3_ffn_b1", "L3_ffn_W2", "L3_ffn_b2"]
STOP = 99


def kernel(**inputs):
    import numpy as _np
    import concourse.bacc as _bacc
    from concourse import mybir as _mybir
    from concourse.bass_utils import run_bass_kernel_spmd as _run

    nc = _bacc.Bacc("TRN2", target_bir_lowering=False, num_devices=1)
    arrays, io = {}, {}
    for name in _INS:
        a = _np.ascontiguousarray(inputs[name])
        arrays["in_" + name] = a
        io[name] = nc.dram_tensor("in_" + name, a.shape, _mybir.dt.from_np(a.dtype), kind="ExternalInput").ap()
    out = nc.dram_tensor("out_x", (N, D), F32, kind="ExternalOutput").ap()
    build(nc, io, out, STOP)
    r = _run(nc, [arrays], core_ids=[0])
    return r.results[0]["out_x"]
```

```python
from contextlib import ExitStack

import concourse.bass as bass
from concourse import mybir

F32 = mybir.dt.float32
I32 = mybir.dt.int32
ALU = mybir.AluOpType
ACT = mybir.ActivationFunctionType
X = mybir.AxisListType.X
RMAX = bass.bass_isa.ReduceOp.max

P = 125
NT = 25
N = P * NT
NCH = 425
D = 256
KD = D // 128
RING = 5
LOT = 8
GR = 15
HEADS, HF = 8, 32
AROW = D + HEADS
EPS = 1e-5
BT = 4
NB = NT // BT
EX = HEADS + 1


class Signal:

    def __init__(self, sem):
        self.sem = sem
        self.base = 0

    def at(self, n):
        return n + self.base

    def passed(self, n):
        self.base += n


class Signals:

    def __init__(self, sig):
        self.loaded = sig("loaded")
        self.chain = sig("chain")
        self.act_step = sig("act_step")
        self.pe_step = sig("pe_step")
        self.pool_step = sig("pool_step")
        self.gate_pool = sig("gate_pool")
        self.gate_act = sig("gate_act")
        self.gate_pe = sig("gate_pe")
        self.rows_ready = sig("rows_ready")
        self.turned = sig("turned")
        self.evicted = sig("evicted")
        self.xn_copied = sig("xn_copied")
        self.stored = sig("stored")
        self.used = sig("used")
        self.one_hot = sig("one_hot")
        self.agg_ready = sig("agg_ready")
        self.added = sig("added")
        self.staged = sig("staged")
        self.tile_ready = sig("tile_ready")
        self.hid_ready = sig("hid_ready")
        self.hid_done = sig("hid_done")
        self.y_ready = sig("y_ready")
        self.y_done = sig("y_done")
        self.ea_turned = sig("ea_turned")
        self.eaT_ready = sig("eaT_ready")
        self.pre_ready = sig("pre_ready")
        self.relu_done = sig("relu_done")
        self.gpre_done = sig("gpre_done")
        self.gate_done = sig("gate_done")
        self.core_ready = sig("core_ready")
        self.msg_done = sig("msg_done")


class Carver:

    def __init__(self, flat):
        self.flat = flat
        self.used = 0

    def take(self, partitions, columns):
        self.used += columns
        return self.flat[0:partitions, self.used - columns:self.used]


def rounds(eng, count, body):
    body(0, True)
    with eng.Fori(1, count) as i:
        body(i, False)


def build(nc, io, out):
    with ExitStack() as ctx:
        build_in(nc, io, out, ctx)


def build_in(nc, io, out, ctx):
    def sb(name, shape, dt=F32, c=ctx):
        return c.enter_context(nc.sbuf_tensor(name, shape, dt))

    def sig(name):
        return Signal(ctx.enter_context(nc.semaphore(name)))

    xres = sb("xres", [P, NT, D])
    xn = sb("xn", [P, NT, D])
    featT = sb("featT", [128, KD, N + P])
    stage = sb("stage", [128, RING, 512])
    ident = sb("ident", [128, 128])
    iota = sb("iota", [P, P])
    ones = sb("ones", [128, 128])
    row0 = sb("row0", [P, P])
    src_i = sb("src_i", [P, NCH], I32)
    dloc = sb("dloc", [P, NCH])
    ew = sb("ew", [P, NCH])
    base_i = sb("base_i", [1, NCH // RING, LOT], I32)
    dinv = sb("dinv", [P, NT])
    idx = sb("idx", [P, 4 * RING], I32)
    stats = sb("stats", [P, NT, 6])
    small = sb("small", [P, 8, NT])
    ps = ctx.enter_context(nc.psum_tensor("ps", [128, 8, 512], F32))

    g = Signals(sig)
    gath = [sig(f"gathered{j}") for j in range(4 * RING)]
    tgt_in = [sig(f"targets{h}") for h in range(4)]
    store = [sig(f"row_store{j}") for j in range(RING)]
    wload = [sig(f"weights_or_tiles{e}") for e in range(LOT)]

    def hold(eng, ns, gate, s, count):
        eng.wait_ge(s.sem, s.at(count))
        ns.sem_inc(gate.sem)

    def hold_act(s, count):
        hold(nc.scalar, nc.scalar, g.gate_act, s, count)

    def hold_pool(s, count):
        hold(nc.gpsimd, nc.gpsimd, g.gate_pool, s, count)

    def hold_pe(s, count):
        hold(nc.tensor, nc.tensor, g.gate_pe, s, count)

    reads = [0]

    def starts(eng, ns, m):
        reads[0] += 1
        regs = [eng.alloc_register(f"window{reads[0]}_{r}") for r in range(RING)]
        ns.load(regs, base_i[0:1, bass.ds(m, 1), 0:RING].rearrange("p a r -> p (a r)"))
        return [ns.snap(r, donate=True, min_val=0, max_val=N - 1) for r in regs]

    def dram(name, shape):
        return nc.dram_tensor(name, shape, F32).ap()

    t_att = dram("t_att", [N, AROW])
    t_tgt = dram("t_tgt", [N + P, 2 * HEADS])
    t_row = dram("t_row", [N, D])
    t_row2 = dram("t_row2", [N, D])
    t_edge = dram("t_edge", [N, 2 * D])
    TSMAX = max(2 * NT + 8, NT + 32)
    t_disp = dram("t_disp", [TSMAX * P, D])
    t_back = dram("t_back", [TSMAX * P, D])

    def prepare():
        with ExitStack() as c:
            rows = 85
            raw_i = sb("raw_i", [rows, 2, RING, P], I32, c)
            raw_f = sb("raw_f", [rows, 3, RING, P], F32, c)
            dst_f = sb("dst_f", [P, NCH], F32, c)
            with nc.Block() as block:
                @block.sync
                def _(sp):
                    for a, t in enumerate((io["src"], io["dst"])):
                        sp.dma_start(raw_i[:, a], t.rearrange("(r q p) -> q r p", q=rows, p=P)).then_inc(g.loaded.sem, 16)
                    sp.dma_start(raw_f[:, 2], io["edge_weight"].rearrange("(r q p) -> q r p", q=rows, p=P)).then_inc(g.loaded.sem, 16)

                @block.gpsimd
                def _(pool):
                    pool.dma_start(xres[:], io["x"].rearrange("(t p) d -> p t d", p=P)).then_inc(g.stored.sem, 16)
                    nc.gpsimd.iota(iota[:], [[1, P]], base=0, channel_multiplier=0,
                                   allow_small_or_imprecise_dtypes=True).then_inc(g.pool_step.sem, 1)
                    nc.gpsimd.memset(ones[:], 1.0).then_inc(g.pool_step.sem, 1)
                    pool.wait_ge(g.pool_step.sem, 2)
                    nc.gpsimd.affine_select(out=ident[:], in_=ones[:], pattern=[[-1, 128]], compare_op=ALU.is_equal,
                                            fill=0.0, base=0, channel_multiplier=1).then_inc(g.pool_step.sem, 1)
                    nc.gpsimd.affine_select(out=row0[:], in_=ones[0:P, 0:P], pattern=[[0, P]], compare_op=ALU.is_equal,
                                            fill=0.0, base=0, channel_multiplier=1).then_inc(g.pool_step.sem, 1)
                    pool.wait_ge(g.stored.sem, 16)

                @block.vector
                def _(dve):
                    dve.wait_ge(g.loaded.sem, 48)
                    nc.vector.tensor_copy(raw_f[:, 0:2], raw_i[:]).then_inc(g.chain.sem, 1)
                    for a in range(3):
                        dve.wait_ge(g.turned.sem, a + 1)
                        if a == 0:
                            nc.vector.tensor_copy(src_i[:], ps[0:P, 0, 0:NCH]).then_inc(g.chain.sem, 1)
                        elif a == 1:
                            nc.vector.tensor_copy(dst_f[:], ps[0:P, 1, 0:NCH]).then_inc(g.chain.sem, 1)
                            nc.vector.tensor_copy(base_i[:, :, 0:RING], ps[0:1, 1, 0:NCH].rearrange("p (l r) -> p l r", r=RING)).then_inc(g.chain.sem, 1)
                        else:
                            nc.vector.tensor_copy(ew[:], ps[0:P, 2, 0:NCH]).then_inc(g.chain.sem, 1)
                    dve.wait_ge(g.turned.sem, 4)
                    nc.vector.tensor_tensor(dloc[:], dst_f[:], ps[0:P, 3, 0:NCH], ALU.subtract).then_inc(g.chain.sem, 1)

                @block.tensor
                def _(pe):
                    pe.wait_ge(g.pool_step.sem, 4)
                    pe.wait_ge(g.chain.sem, 1)
                    for a in range(3):
                        for r in range(RING):
                            mm = nc.tensor.transpose(ps[0:P, a, r * rows:(r + 1) * rows], raw_f[:, a, r, :], ident[0:rows, 0:rows])
                        mm.then_inc(g.turned.sem, 1)
                    pe.wait_ge(g.chain.sem, 3)
                    nc.tensor.matmul(ps[0:P, 3, 0:NCH], row0[:], dst_f[:], start=True, stop=True).then_inc(g.turned.sem, 1)
        g.loaded.passed(48), g.stored.passed(16), g.pool_step.passed(4), g.chain.passed(6), g.turned.passed(4)

    def normalize(tag, src, gamma=None, beta=None, to_xn=False, to_featT=False, table=None, scale=None, add_to_x=False):
        with ExitStack() as c:
            gb = sb(tag + "_gb", [P, 2, D], F32, c) if gamma is not None else None
            mean2, diff, m2, var, sd, rstd, mean = (small[:, k, :] for k in range(7))
            PRE = NT + 6
            PER = 2 if gamma is not None else 0
            LOT_STEPS = RING + 3
            with nc.Block() as block:
                @block.sync
                def _(sp):
                    if gamma is not None:
                        sp.dma_start(gb[:, 0, :], gamma.partition_broadcast(P)).then_inc(g.loaded.sem, 16)
                        sp.dma_start(gb[:, 1, :], beta.partition_broadcast(P)).then_inc(g.loaded.sem, 16)
                    if table is not None:
                        def body(i, first):
                            for j in range(RING):
                                sp.wait_ge(g.rows_ready.sem, g.rows_ready.at(RING * i + j + 1))
                                sp.dma_start(table[bass.ds(P * RING * i + P * j, P), :], stage[0:P, j, 0:D]).then_inc(store[j].sem, 16)
                        rounds(sp, NT // RING, body)
                        for j in range(RING):
                            sp.wait_ge(store[j].sem, store[j].at(16 * NT // RING))

                @block.vector
                def _(dve):
                    ch = g.chain
                    def stat(i, first):
                        for j in range(RING):
                            nc.vector.bn_stats(stats[:, bass.ds(RING * i + j, 1), :], src[:, bass.ds(RING * i + j, 1), :]).then_inc(ch.sem, 1)
                    rounds(dve, NT // RING, stat)
                    dve.wait_ge(ch.sem, ch.at(NT))
                    nc.vector.tensor_tensor(mean2, stats[:, :, 1], stats[:, :, 4], ALU.add).then_inc(ch.sem, 1)
                    nc.vector.tensor_tensor(diff, stats[:, :, 1], stats[:, :, 4], ALU.subtract).then_inc(ch.sem, 1)
                    nc.vector.tensor_tensor(m2, stats[:, :, 2], stats[:, :, 5], ALU.add).then_inc(ch.sem, 1)
                    dve.wait_ge(ch.sem, ch.at(NT + 3))
                    nc.vector.tensor_tensor(var, diff, diff, ALU.mult).then_inc(ch.sem, 1)
                    nc.vector.tensor_scalar(mean, mean2, 0.5, None, ALU.mult).then_inc(ch.sem, 1)
                    dve.wait_ge(ch.sem, ch.at(NT + 5))
                    nc.vector.scalar_tensor_tensor(var, var, D / 4.0, m2, ALU.mult, ALU.add).then_inc(g.pool_step.sem, 1)
                    dve.wait_ge(g.pool_step.sem, g.pool_step.at(1))
                    nc.vector.tensor_scalar(var, var, 1.0 / D, EPS, ALU.mult, ALU.add).then_inc(ch.sem, 1)
                    dve.wait_ge(g.act_step.sem, g.act_step.at(1))
                    nc.vector.reciprocal(rstd, sd).then_inc(g.pool_step.sem, 1)
                    dve.wait_ge(g.pool_step.sem, g.pool_step.at(2))
                    if scale is not None:
                        nc.vector.tensor_tensor(rstd, rstd, scale[:], ALU.mult).then_inc(g.pool_step.sem, 1)
                        dve.wait_ge(g.pool_step.sem, g.pool_step.at(3))
                    if gamma is not None:
                        dve.wait_ge(g.loaded.sem, g.loaded.at(32))

                    def body(i, first):
                        for j in range(RING):
                            n = RING * i + j
                            st = stage[0:P, j, 0:D]
                            if not first:
                                if to_xn:
                                    dve.wait_ge(g.xn_copied.sem, g.xn_copied.at(n - RING + 1))
                                if to_featT:
                                    dve.wait_ge(g.turned.sem, g.turned.at(n - RING + 1))
                                if table is not None:
                                    dve.wait_ge(store[j].sem, store[j].at(16 * i))
                            last = nc.vector.tensor_scalar(st, src[:, bass.ds(n, 1), :].rearrange("p a d -> p (a d)"), mean[:, bass.ds(n, 1)],
                                                           rstd[:, bass.ds(n, 1)], ALU.subtract, ALU.mult)
                            if gamma is not None:
                                for q, op in ((0, ALU.mult), (1, ALU.add)):
                                    last.then_inc(ch.sem, 1)
                                    dve.wait_ge(ch.sem, ch.at(PRE + PER * n + q + 1))
                                    last = nc.vector.tensor_tensor(st, st, gb[:, q, :], op)
                            last.then_inc(g.rows_ready.sem, 1)

                    def add_lot(i, first):
                        c0 = PRE + LOT_STEPS * i
                        if not first:
                            dve.wait_ge(ch.sem, ch.at(c0))
                        for j in range(RING):
                            n = RING * i + j
                            nc.vector.tensor_scalar(stage[0:P, j, 0:D], src[:, bass.ds(n, 1), :].rearrange("p a d -> p (a d)"), mean[:, bass.ds(n, 1)],
                                                    rstd[:, bass.ds(n, 1)], ALU.subtract, ALU.mult).then_inc(ch.sem, 1)
                        lot = stage[0:P, :, 0:D]
                        for q, op in ((0, ALU.mult), (1, ALU.add)):
                            dve.wait_ge(ch.sem, ch.at(c0 + RING + q))
                            nc.vector.tensor_tensor(lot, lot, gb[:, q:q + 1, :].to_broadcast([P, RING, D]), op).then_inc(ch.sem, 1)
                        dve.wait_ge(ch.sem, ch.at(c0 + RING + 2))
                        x = xres[:, bass.ds(RING * i, RING), :]
                        nc.vector.tensor_tensor(x, x, lot, ALU.add).then_inc(ch.sem, 1)
                    rounds(dve, NT // RING, add_lot if add_to_x else body)

                @block.scalar
                def _(act):
                    act.wait_ge(g.chain.sem, g.chain.at(PRE))
                    nc.scalar.activation(sd, var, ACT.Sqrt).then_inc(g.act_step.sem, 1)

                    def body(i, first):
                        for j in range(RING):
                            n = RING * i + j
                            if to_xn:
                                hold_act(g.rows_ready, n + 1)
                                nc.scalar.copy(xn[:, bass.ds(n, 1), :].rearrange("p a d -> p (a d)"), stage[0:P, j, 0:D]).then_inc(g.xn_copied.sem, 1)
                            if to_featT:
                                hold_act(g.turned, n + 1)
                                nc.scalar.copy(featT[:, :, bass.ds(P * n, P)],
                                               ps[:, j, 0:KD * P].rearrange("p (k t) -> p k t", k=KD)).then_inc(g.evicted.sem, 1)
                    if to_xn or to_featT:
                        rounds(act, NT // RING, body)

                @block.tensor
                def _(pe):
                    def body(i, first):
                        for j in range(RING):
                            n = RING * i + j
                            pe.wait_ge(g.rows_ready.sem, g.rows_ready.at(n + 1))
                            if not first:
                                pe.wait_ge(g.evicted.sem, g.evicted.at(n - RING + 1))
                            for k in range(KD):
                                mm = nc.tensor.transpose(ps[:, j, k * P:(k + 1) * P], stage[0:P, j, k * 128:(k + 1) * 128], ident[0:P, 0:P])
                            mm.then_inc(g.turned.sem, 1)
                    if to_featT:
                        rounds(pe, NT // RING, body)
        g.chain.passed(PRE + (LOT_STEPS * NT // RING if add_to_x else PER * NT)), g.pool_step.passed(2 + (1 if scale is not None else 0)), g.act_step.passed(1)
        if not add_to_x:
            g.rows_ready.passed(NT)
        if gamma is not None:
            g.loaded.passed(32)
        if to_xn:
            g.xn_copied.passed(NT)
        if to_featT:
            g.turned.passed(NT), g.evicted.passed(NT)
        if table is not None:
            for s in store:
                s.passed(16 * NT // RING)

    def tiles(load, turn_weights, pe_ops, dve_ops, per, sp_rows=None, feat=featT, extra=False):
        NL = len(load)
        NW = len(turn_weights)
        ch = g.chain
        with nc.Block() as block:
            @block.sync
            def _(sp):
                for d, s in load:
                    sp.dma_start(d, s).then_inc(g.loaded.sem, 16)
                if sp_rows is not None:
                    def body(i, first):
                        for j in range(RING):
                            n = RING * i + j
                            sp.wait_ge(ch.sem, ch.at(per * (n + 1)))
                            for d, s in sp_rows(n, j):
                                sp.dma_start(d, s).then_inc(store[j].sem, 16)
                    rounds(sp, NT // RING, body)
                    k = len(sp_rows(0, 0))
                    for j in range(RING):
                        sp.wait_ge(store[j].sem, store[j].at(16 * k * NT // RING))

            @block.scalar
            def _(act):
                def body(i, first):
                    for j in range(RING):
                        n = RING * i + j
                        if not first:
                            hold_act(g.tile_ready, n - RING + 1)
                        last = nc.scalar.copy(stage[:, j, 0:KD * P].rearrange("p (k t) -> p k t", k=KD), feat[:, 0:KD, bass.ds(P * n, P)])
                        if extra:
                            last.then_inc(g.act_step.sem, 1)
                            last = nc.scalar.copy(stage[0:EX, j, KD * P:KD * P + P], feat[0:EX, KD:KD + 1, bass.ds(P * n, P)].rearrange("p a t -> p (a t)"))
                        last.then_inc(g.staged.sem, 1)
                rounds(act, NT // RING, body)

            @block.tensor
            def _(pe):
                if NL:
                    pe.wait_ge(g.loaded.sem, g.loaded.at(16 * NL))
                for w, (d, s, rows) in enumerate(turn_weights):
                    if w >= 2:
                        pe.wait_ge(g.pe_step.sem, g.pe_step.at(w - 1))
                    nc.tensor.transpose(ps[0:128, 6 + w % 2, 0:rows], s, ident[0:rows, 0:rows]).then_inc(g.turned.sem, 1)
                if NW:
                    pe.wait_ge(g.pe_step.sem, g.pe_step.at(NW))

                def body(i, first):
                    for j in range(RING):
                        n = RING * i + j
                        pe.wait_ge(g.staged.sem, g.staged.at(n + 1))
                        if extra:
                            pe.wait_ge(g.act_step.sem, g.act_step.at(n + 1))
                        if not first:
                            pe.wait_ge(ch.sem, ch.at(per * (n - RING + 1)))
                        pe_ops(j, stage[:, j, 0:KD * P].rearrange("p (k t) -> p k t", k=KD)).then_inc(g.tile_ready.sem, 1)
                rounds(pe, NT // RING, body)

            @block.vector
            def _(dve):
                if NL:
                    dve.wait_ge(g.loaded.sem, g.loaded.at(16 * NL))
                for w, (d, s, rows) in enumerate(turn_weights):
                    dve.wait_ge(g.turned.sem, g.turned.at(w + 1))
                    nc.vector.tensor_copy(d, ps[0:128, 6 + w % 2, 0:rows]).then_inc(g.pe_step.sem, 1)

                def body(i, first):
                    for j in range(RING):
                        n = RING * i + j
                        dve.wait_ge(g.tile_ready.sem, g.tile_ready.at(n + 1))
                        if sp_rows is not None and not first:
                            dve.wait_ge(store[j].sem, store[j].at(16 * len(sp_rows(0, 0)) * i))
                        dve_ops(dve, n, j, per * n)
                rounds(dve, NT // RING, body)
        g.loaded.passed(16 * NL), g.turned.passed(NW), g.pe_step.passed(NW)
        g.staged.passed(NT), g.tile_ready.passed(NT), ch.passed(per * NT)
        if extra:
            g.act_step.passed(NT)
        if sp_rows is not None:
            for s in store:
                s.passed(16 * len(sp_rows(0, 0)) * NT // RING)

    def tile_of(t, n):
        return t[:, bass.ds(n, 1), :].rearrange("p a d -> p (a d)")

    def times(w, width):
        def pe_ops(j, x):
            for k in range(KD):
                mm = nc.tensor.matmul(ps[0:P, j, 0:width], x[:, k, :], w[:, k, 0:width], start=(k == 0), stop=(k == KD - 1))
            return mm
        return pe_ops

    def halves(w):
        return w.rearrange("(k p) f -> p k f", p=128)

    def wait_chain(dve, count):
        dve.wait_ge(g.chain.sem, g.chain.at(count))

    def att_project(hst):
        with ExitStack() as c:
            w = sb("att_w", [128, KD, D], F32, c)
            b = sb("att_b", [P, D], F32, c)
            a = sb("att_a", [P, 2, D], F32, c)
            rows = sb("ap_rows", [P, RING, AROW], F32, c)
            prod = sb("att_prod", [P, 2, D], F32, c)
            both = sb("att_both", [P, 2 * HEADS], F32, c)

            def use(dve, n, j, c0):
                ch = g.chain.sem
                h = rows[:, j, 0:D].rearrange("p (f h) -> p h f", h=HEADS)
                nc.vector.tensor_tensor(h, ps[0:P, j, 0:D].rearrange("p (h f) -> p h f", h=HEADS),
                                        b[:].rearrange("p (h f) -> p h f", h=HEADS), ALU.add).then_inc(ch, 1)
                wait_chain(dve, c0 + 1)
                for s in range(2):
                    nc.vector.tensor_tensor(prod[:, s, :].rearrange("p (h f) -> p h f", h=HEADS), h,
                                            a[:, s, :].rearrange("p (h f) -> p h f", h=HEADS), ALU.mult).then_inc(ch, 1)
                nc.vector.tensor_copy(tile_of(xn, n), rows[:, j, 0:D]).then_inc(ch, 1)
                wait_chain(dve, c0 + 3)
                nc.vector.tensor_reduce(both[:].rearrange("p (s h) -> p s h", s=2),
                                        prod[:].rearrange("p s (h f) -> p s h f", h=HEADS), X, ALU.add).then_inc(ch, 1)
                wait_chain(dve, c0 + 5)
                nc.vector.tensor_copy(rows[:, j, D:AROW], both[:, 0:HEADS]).then_inc(ch, 1)
                nc.vector.tensor_copy(tile_of(hst, n), both[:]).then_inc(ch, 1)

            tiles([(w[:], halves(io["L0_gnn_W"])), (b[:], io["L0_gnn_b"].partition_broadcast(P)),
                   (a[:, 0, :], io["L0_gnn_a_src"].rearrange("a h f -> (a h f)").partition_broadcast(P)),
                   (a[:, 1, :], io["L0_gnn_a_trg"].rearrange("a h f -> (a h f)").partition_broadcast(P))],
                  [], times(w, D), use, 7,
                  sp_rows=lambda n, j: [(t_att[bass.ds(P * n, P), :], rows[:, j, :])])

    def att_shift(hst, own, shift, top):
        with ExitStack() as c:
            rows = sb("as_rows", [P, NT, 2 * HEADS], F32, c)
            zero = sb("as_zero", [P, 2 * HEADS], F32, c)
            hs, ht = hst[:, :, 0:HEADS], hst[:, :, HEADS:2 * HEADS]
            with nc.Block() as block:
                @block.vector
                def _(dve):
                    ch = g.chain.sem
                    nc.vector.tensor_reduce(top[:, 0, :], hs.rearrange("p t h -> p h t"), X, ALU.max).then_inc(ch, 1)
                    nc.vector.tensor_tensor(own[:], hs, ht, ALU.add).then_inc(ch, 1)
                    nc.vector.tensor_copy(rows[:, :, 0:HEADS], ht).then_inc(ch, 1)
                    nc.vector.memset(zero[:], 0.0).then_inc(ch, 1)
                    wait_chain(dve, 2)
                    nc.vector.scalar_tensor_tensor(own[:], own[:], 0.2, own[:], ALU.mult, ALU.max).then_inc(ch, 1)
                    dve.wait_ge(g.pe_step.sem, g.pe_step.at(1))
                    nc.vector.tensor_tensor(shift[:], ht, top[:, 1, :].unsqueeze(1).to_broadcast([P, NT, HEADS]), ALU.add).then_inc(ch, 1)
                    wait_chain(dve, 6)
                    nc.vector.scalar_tensor_tensor(shift[:], shift[:], 0.2, shift[:], ALU.mult, ALU.max).then_inc(ch, 1)
                    wait_chain(dve, 7)
                    nc.vector.tensor_copy(rows[:, :, HEADS:], shift[:]).then_inc(ch, 1)

                @block.gpsimd
                def _(pool):
                    pool.wait_ge(g.chain.sem, g.chain.at(1))
                    nc.gpsimd.partition_all_reduce(top[:, 1, :], top[:, 0, :], P, RMAX).then_inc(g.pe_step.sem, 1)

                @block.sync
                def _(sp):
                    sp.wait_ge(g.chain.sem, g.chain.at(8))
                    sp.dma_start(t_tgt[0:N, :].rearrange("(t p) k -> p t k", p=P), rows[:]).then_inc(g.loaded.sem, 16)
                    sp.dma_start(t_tgt[N:N + P, :], zero[:]).then_inc(g.loaded.sem, 16)
                    sp.wait_ge(g.loaded.sem, g.loaded.at(32))
        g.chain.passed(8), g.pe_step.passed(1), g.loaded.passed(32)

    def by_lots(eng, lots, fill, between=None):
        whole, rest = divmod(NCH // RING, lots)
        for h in range(lots):
            fill(h, h, True)
        if between is not None:
            between()
        with eng.Fori(1, whole) as i:
            for h in range(lots):
                fill(lots * i + h, h, False)
        for h in range(rest):
            fill(lots * whole + h, h, False)

    def index_slots(h):
        return idx[:, RING * h:RING * h + RING]

    def indices_by_act(act, free, lots, between=None):
        def fill(m, h, first):
            if not first:
                hold_act(free, RING * (m - lots + 1))
            nc.scalar.copy(index_slots(h), src_i[:, bass.ds(RING * m, RING)]).then_inc(g.pool_step.sem, 1)
        by_lots(act, lots, fill, between)

    def gathers(pool, table, rows, lots, free=None):
        def fill(m, h, first):
            if free is not None:
                if not first:
                    hold_pool(free, RING * (m - lots + 1))
                nc.gpsimd.tensor_copy(index_slots(h), src_i[:, bass.ds(RING * m, RING)]).then_inc(g.pool_step.sem, 1)
            hold_pool(g.pool_step, m + 1)
            for j in range(RING * h, RING * h + RING):
                nc.gpsimd.indirect_dma_start(out=rows[:, j, :], out_offset=None, in_=table,
                                             in_offset=bass.IndirectOffsetOnAxis(ap=idx[:, j:j + 1], axis=0)).then_inc(gath[j].sem, 16)
        by_lots(pool, lots, fill)

    def gathers_passed(lots):
        g.pool_step.passed(NCH // RING)
        for j in range(RING * lots):
            gath[j].passed(16 * (NCH // RING // lots + (1 if j // RING < NCH // RING % lots else 0)))

    def steps(eng, count, ring, parts):
        top = max(l for l, _ in parts)
        whole = (count - top) // ring
        for n in range(-top, 0):
            for l, f in parts:
                if n + l >= 0:
                    f(n + l, (n + l) // ring, (n + l) % ring, n + l < ring)
        for j in range(ring):
            for l, f in parts:
                f(j + l, (j + l) // ring, (j + l) % ring, j + l < ring)
        with eng.Fori(1, whole) as i:
            for j in range(ring):
                for l, f in parts:
                    f(ring * i + j + l, i + (j + l) // ring, (j + l) % ring, False)
        for n in range(ring * whole, count):
            for l, f in parts:
                if n + l < count:
                    f(n + l, (n + l) // ring, (n + l) % ring, False)

    def att_pass(own, top, sums):
        LOTS = 4
        with ExitStack() as c:
            R = LOTS * RING
            rows = sb("ag_rows", [P, R, AROW], F32, c)
            msg = sb("ag_msg", [P, R, AROW + 1], F32, c)
            hot = sb("ag_hot", [P, R, P], F32, c)
            hotT = stage[0:P].rearrange("p r c -> p (r c)")[:, 0:LOTS * RING * P].rearrange("p (l r t) -> p l r t", l=LOTS, r=RING)
            tgt = sb("ag_tgt", [P, R, 2 * HEADS], F32, c)
            sc = sb("ag_sc", [P, 3, RING, HEADS], F32, c)
            high = sb("ag_high", [P, RING, HEADS], F32, c)
            NL = NCH // RING
            TB, EB, AB = 0, 2, 3
            with nc.Block() as block:
                @block.gpsimd
                def _(pool):
                    gathers(pool, t_att, rows, LOTS, free=g.msg_done)

                @block.sync
                def _(sp):
                    def body(m, i, h, first):
                        if not first:
                            sp.wait_ge(g.tile_ready.sem, g.tile_ready.at(m - LOTS + 1))
                        for j, b in enumerate(starts(sp, nc.sync, m), RING * h):
                            sp.dma_start(tgt[:, j, :], t_tgt[bass.ds(b, P), :]).then_inc(tgt_in[h].sem, 16)
                    steps(sp, NL, LOTS, [(0, body)])

                @block.vector
                def _(dve):
                    nc.vector.memset(sums[:], 0.0).then_inc(g.added.sem, 1)
                    nc.vector.memset(ps[:, AB:AB + RING, KD * P:(KD + 1) * P], 0.0).then_inc(g.added.sem, 1)
                    nc.vector.memset(msg[:], 1.0).then_inc(g.added.sem, 1)
                    nc.vector.memset(high[:], -3e38).then_inc(g.added.sem, 1)
                    dve.wait_ge(g.added.sem, g.added.at(4))

                    def scores(m, i, h, first):
                        lot = slice(RING * h, RING * h + RING)
                        e = ps[0:P, EB, 0:RING * 2 * HEADS].rearrange("p (c k) -> p c k", c=RING)
                        if not (first and h == 0):
                            dve.wait_ge(g.gate_done.sem, g.gate_done.at(m))
                        dve.wait_ge(g.tile_ready.sem, g.tile_ready.at(m + 1))
                        for j in range(RING * h, RING * h + RING):
                            dve.wait_ge(gath[j].sem, gath[j].at(16 * i + 16))
                        nc.vector.tensor_tensor(sc[:, 0], e[:, :, 0:HEADS], rows[:, lot, D:AROW], ALU.add).then_inc(g.chain.sem, 1)
                        wait_chain(dve, 4 * m + 1)
                        nc.vector.scalar_tensor_tensor(sc[:, 1], sc[:, 0], 0.2, sc[:, 0], ALU.mult, ALU.max).then_inc(g.chain.sem, 1)
                        wait_chain(dve, 4 * m + 2)
                        nc.vector.tensor_tensor(high[:], high[:], sc[:, 1], ALU.max).then_inc(g.chain.sem, 1)
                        nc.vector.tensor_tensor(sc[:, 2], sc[:, 1], e[:, :, HEADS:2 * HEADS], ALU.subtract).then_inc(g.chain.sem, 1)

                    def add(m, j, b):
                        n = RING * m + j
                        dve.wait_ge(g.agg_ready.sem, g.agg_ready.at(n + 1))
                        dve.wait_ge(g.added.sem, g.added.at(4 + n))
                        f = sums[:, :, bass.ds(b, P)]
                        nc.vector.tensor_tensor(f, f, ps[:, AB + j, 0:(KD + 1) * P].rearrange("p (k t) -> p k t", k=KD + 1), ALU.add).then_inc(g.added.sem, 1)

                    def messages_and_adds(m, i, h, first):
                        opening = first and h == 0
                        windows = None if opening else starts(dve, nc.vector, m - 1)
                        dve.wait_ge(g.gate_done.sem, g.gate_done.at(m + 1))
                        for j in range(RING):
                            if not opening:
                                add(m - 1, j, windows[j])
                            s = RING * h + j
                            nc.vector.tensor_tensor(msg[:, s, 0:D].rearrange("p (f h) -> p f h", h=HEADS),
                                                    rows[:, s, 0:D].rearrange("p (f h) -> p f h", h=HEADS),
                                                    msg[:, s, D:AROW].unsqueeze(1).to_broadcast([P, HF, HEADS]), ALU.mult).then_inc(g.msg_done.sem, 1)
                    steps(dve, NL, LOTS, [(1, messages_and_adds), (2, scores)])
                    for j, b in enumerate(starts(dve, nc.vector, NL - 1)):
                        add(NL - 1, j, b)
                    wait_chain(dve, 4 * NL)
                    nc.vector.tensor_reduce(sc[:, 0, 0, 0:1], high[:].rearrange("p c h -> p (c h)"), X, ALU.max).then_inc(g.chain.sem, 1)
                    nc.vector.tensor_reduce(sc[:, 0, 0, 1:2], own[:].rearrange("p t h -> p (t h)"), X, ALU.max).then_inc(g.chain.sem, 1)
                    wait_chain(dve, 4 * NL + 2)
                    nc.vector.tensor_tensor(top[:, 0, 0:1], sc[:, 0, 0, 0:1], sc[:, 0, 0, 1:2], ALU.max).then_inc(g.chain.sem, 1)

                @block.scalar
                def _(act):
                    def turned(m, i, h, first):
                        hold_act(g.turned, m + 1)
                        if not first:
                            hold_act(g.tile_ready, m - LOTS + 1)
                        for q, k in ((0, 3), (3, 2)):
                            last = nc.scalar.copy(hotT[:, h, q:q + k, :], ps[0:P, TB + q // 3, 0:k * P].rearrange("p (c t) -> p c t", c=k))
                            last.then_inc(g.evicted.sem, 1)

                    def weights(m, i, h, first):
                        hold_act(g.chain, 4 * m + 4)
                        if not first:
                            hold_act(g.agg_ready, RING * (m - LOTS + 1))
                        nc.scalar.activation(msg[:, RING * h:RING * h + RING, D:AROW], sc[:, 2], ACT.Exp).then_inc(g.gate_done.sem, 1)
                    def one_hots(m, i, h, first):
                        if not first:
                            hold_act(g.agg_ready, RING * (m - LOTS + 1))
                        lot = hot[:, RING * h:RING * h + RING, :]
                        for j in range(RING):
                            last = nc.scalar.activation(lot[:, j, :], iota[:], ACT.Square, bias=dloc[:, bass.ds(RING * m + j, 1)], scale=-1.0)
                        last.then_inc(g.act_step.sem, 1)
                        hold_act(g.act_step, m + 1)
                        nc.scalar.activation(lot, lot, ACT.Relu, bias=1.0, scale=-2.0).then_inc(g.one_hot.sem, 1)
                    steps(act, NL, LOTS, [(3, turned), (2, weights), (4, one_hots)])

                @block.tensor
                def _(pe):
                    def turn(m, i, h, first):
                        if not (first and h == 0):
                            hold_pe(g.evicted, 2 * m)
                        hold_pe(g.one_hot, m + 1)
                        for j in range(RING):
                            mm = nc.tensor.transpose(ps[0:P, TB + j // 3, (j % 3) * P:(j % 3 + 1) * P], hot[:, RING * h + j, :], ident[0:P, 0:P])
                        mm.then_inc(g.turned.sem, 1)

                    def spread(m, i, h, first):
                        hold_pe(g.evicted, 2 * m + 2)
                        hold_pe(tgt_in[h], 16 * RING * (i + 1))
                        if not (first and h == 0):
                            hold_pe(g.chain, 4 * m)
                        for j in range(RING):
                            mm = nc.tensor.matmul(ps[0:P, EB, 2 * HEADS * j:2 * HEADS * (j + 1)], hotT[:, h, j, :], tgt[:, RING * h + j, :], start=True, stop=True)
                        mm.then_inc(g.tile_ready.sem, 1)

                    def products(m, i, h, first):
                        for j in range(RING):
                            n = RING * m + j
                            s = RING * h + j
                            pe.wait_ge(g.msg_done.sem, g.msg_done.at(n + 1))
                            if first and h == 0:
                                pe.wait_ge(g.added.sem, g.added.at(4))
                            else:
                                pe.wait_ge(g.added.sem, g.added.at(4 + n - RING + 1))
                            for k in range(KD):
                                nc.tensor.matmul(ps[:, AB + j, k * P:(k + 1) * P], msg[:, s, k * 128:(k + 1) * 128], hot[:, s, :], start=True, stop=True)
                            nc.tensor.matmul(ps[0:EX, AB + j, KD * P:KD * P + P], msg[:, s, D:D + EX], hot[:, s, :], start=True, stop=True).then_inc(g.agg_ready.sem, 1)
                    steps(pe, NL, LOTS, [(0, products), (2, spread), (3, turn)])
        gathers_passed(LOTS)
        for h in range(LOTS):
            tgt_in[h].passed(16 * RING * (NL // LOTS + (1 if h < NL % LOTS else 0)))
        g.chain.passed(4 * NL + 3), g.added.passed(4 + NCH), g.evicted.passed(2 * NL)
        for s in (g.msg_done, g.agg_ready):
            s.passed(NCH)
        for s in (g.turned, g.tile_ready, g.gate_done, g.act_step, g.one_hot):
            s.passed(NL)

    def edge_pass(tag, table, weight=None, loops=False, clear=None):
        with ExitStack() as c:
            rows = sb(tag + "_rows", [P, GR, D], F32, c)
            hot = sb(tag + "_hot", [P, GR, P], F32, c)
            NL, LOTS = NCH // RING, GR // RING
            ZF = -(-TSMAX // (2 * RING))
            with nc.Block() as block:
                @block.gpsimd
                def _(pool):
                    gathers(pool, table, rows, LOTS)

                @block.vector
                def _(dve):
                    if clear is not None:
                        nc.vector.memset(stage[:], 0.0).then_inc(g.act_step.sem, 1)
                    nc.vector.memset(featT[:, :, N:] if loops else featT[:], 0.0).then_inc(g.added.sem, 1)
                    if loops:
                        dve.wait_ge(g.evicted.sem, g.evicted.at(NT))
                    dve.wait_ge(g.added.sem, g.added.at(1))

                    def one_hots(m, i, h, first):
                        for j in range(RING):
                            nc.vector.tensor_scalar(hot[:, RING * h + j, :], iota[:], dloc[:, bass.ds(RING * m + j, 1)],
                                                    weight[:, bass.ds(RING * m + j, 1)] if weight is not None else None, ALU.is_equal,
                                                    ALU.mult if weight is not None else ALU.bypass).then_inc(g.one_hot.sem, 1)

                    def add(m, i, h, first):
                        for j, b in enumerate(starts(dve, nc.vector, m)):
                            n = RING * m + j
                            dve.wait_ge(g.agg_ready.sem, g.agg_ready.at(n + 1))
                            dve.wait_ge(g.added.sem, g.added.at(1 + n))
                            f = featT[:, :, bass.ds(b, P)]
                            nc.vector.tensor_tensor(f, f, ps[:, j, 0:KD * P].rearrange("p (k t) -> p k t", k=KD), ALU.add).then_inc(g.added.sem, 1)
                    steps(dve, NL, LOTS, [(LOTS - 1, one_hots), (0, add)])

                if clear is not None:
                    @block.sync
                    def _(sp):
                        sp.wait_ge(g.act_step.sem, g.act_step.at(1))
                        for t in range(0, TSMAX, 2 * RING):
                            k = min(2 * RING, TSMAX - t)
                            sp.dma_start(clear[t * P:(t + k) * P, :].rearrange("(k p) d -> p k d", p=P),
                                         stage[0:P].rearrange("p r (a d) -> p (r a) d", d=D)[:, 0:k, :]).then_inc(g.loaded.sem, 16)
                        sp.wait_ge(g.loaded.sem, g.loaded.at(16 * ZF))

                if loops:
                    @block.sync
                    def _(sp):
                        def body(i, first):
                            for j in range(RING):
                                if not first:
                                    sp.wait_ge(g.turned.sem, g.turned.at(RING * (i - 1) + j + 1))
                                sp.dma_start(stage[0:P, j, 0:D], table[bass.ds(P * RING * i + P * j, P), :]).then_inc(store[j].sem, 16)
                        rounds(sp, NT // RING, body)

                @block.scalar
                def _(act):
                    def body(i, first):
                        for j in range(RING):
                            n = RING * i + j
                            hold_act(g.turned, n + 1)
                            nc.scalar.copy(featT[:, :, bass.ds(P * n, P)],
                                           ps[:, j, 0:KD * P].rearrange("p (k t) -> p k t", k=KD)).then_inc(g.evicted.sem, 1)
                    indices_by_act(act, g.agg_ready, LOTS, between=(lambda: rounds(act, NT // RING, body)) if loops else None)

                @block.tensor
                def _(pe):
                    def turn(i, first):
                        for j in range(RING):
                            n = RING * i + j
                            pe.wait_ge(store[j].sem, store[j].at(16 * i + 16))
                            if not first:
                                pe.wait_ge(g.evicted.sem, g.evicted.at(n - RING + 1))
                            for k in range(KD):
                                mm = nc.tensor.transpose(ps[:, j, k * P:(k + 1) * P], stage[0:P, j, k * 128:(k + 1) * 128], ident[0:P, 0:P])
                            mm.then_inc(g.turned.sem, 1)
                    if loops:
                        rounds(pe, NT // RING, turn)
                        pe.wait_ge(g.evicted.sem, g.evicted.at(NT))

                    def body(n, i, j, first):
                        pe.wait_ge(gath[j].sem, gath[j].at(16 * i + 16))
                        pe.wait_ge(g.one_hot.sem, g.one_hot.at(n + 1))
                        if not (first and j < RING):
                            pe.wait_ge(g.added.sem, g.added.at(1 + n - RING + 1))
                        for k in range(KD):
                            lhs = rows[:, j, k * 128:(k + 1) * 128]
                            mm = nc.tensor.matmul(ps[:, j % RING, k * P:(k + 1) * P], lhs, hot[:, j, :], start=True, stop=True)
                        mm.then_inc(g.agg_ready.sem, 1)
                    for j in range(GR):
                        body(j, 0, j, True)
                    with pe.Fori(1, NCH // GR) as i:
                        for j in range(GR):
                            body(GR * i + j, i, j, False)
                    for j in range(NCH % GR):
                        body(NCH - NCH % GR + j, NCH // GR, j, False)
        gathers_passed(GR // RING)
        g.agg_ready.passed(NCH), g.one_hot.passed(NCH), g.added.passed(1 + NCH)
        if clear is not None:
            g.act_step.passed(1), g.loaded.passed(16 * ZF)
        if loops:
            g.turned.passed(NT), g.evicted.passed(NT)
            for s in store:
                s.passed(16 * NT // RING)

    def turn_back(extra_rows):
        def pe_ops(j, x):
            for k in range(KD):
                mm = nc.tensor.transpose(ps[0:P, j, k * 128:(k + 1) * 128], x[:, k, :], ident[:])
            if extra_rows:
                mm = nc.tensor.transpose(ps[0:P, j, D:D + EX], stage[0:EX, j, KD * P:KD * P + P], ident[0:EX, 0:EX])
            return mm
        return pe_ops

    def att_finish(sums, own, shift, top):
        with ExitStack() as c:
            den = sb("den", [P, 2, HEADS], F32, c)
            deg = sb("deg", [P, 2, NT], F32, c)
            o = sb("att_o", [P, 2, D], F32, c)

            def use(dve, n, j, c0):
                ch = g.chain.sem
                by_head = lambda ap: ap.rearrange("p (f h) -> p f h", h=HEADS)
                w = own[:, bass.ds(n, 1), :]
                nc.vector.tensor_tensor(den[:, 0, :], ps[0:P, j, D:D + HEADS], tile_of(shift, n), ALU.add).then_inc(ch, 1)
                nc.vector.tensor_copy(deg[:, 0, bass.ds(n, 1)], ps[0:P, j, D + HEADS:D + EX]).then_inc(ch, 1)
                nc.vector.tensor_tensor(by_head(o[:, 1, :]), by_head(tile_of(xn, n)), w.to_broadcast([P, HF, HEADS]), ALU.mult).then_inc(ch, 1)
                wait_chain(dve, c0 + 3)
                nc.vector.reciprocal(den[:, 1, :], den[:, 0, :]).then_inc(ch, 1)
                nc.vector.tensor_tensor(o[:, 1, :], o[:, 1, :], ps[0:P, j, 0:D], ALU.add).then_inc(ch, 1)
                wait_chain(dve, c0 + 5)
                nc.vector.tensor_tensor(o[:, 0, :].rearrange("p (h f) -> p f h", h=HEADS), by_head(o[:, 1, :]),
                                        den[:, 1, :].unsqueeze(1).to_broadcast([P, HF, HEADS]), ALU.mult).then_inc(ch, 1)
                wait_chain(dve, c0 + 6)
                nc.vector.tensor_tensor(tile_of(xres, n), tile_of(xres, n), o[:, 0, :], ALU.add).then_inc(ch, 1)

            flat = lambda t: t[:].rearrange("p t h -> p (t h)")
            with nc.Block() as block:
                @block.gpsimd
                def _(pool):
                    nc.gpsimd.partition_all_reduce(top[:, 1, 0:1], top[:, 0, 0:1], P, RMAX).then_inc(g.pool_step.sem, 1)

                @block.vector
                def _(dve):
                    nc.vector.tensor_tensor(flat(own), flat(own), flat(shift), ALU.subtract).then_inc(g.chain.sem, 1)

                @block.scalar
                def _(act):
                    act.wait_ge(g.chain.sem, g.chain.at(1))
                    nc.scalar.activation(flat(own), flat(own), ACT.Exp)
                    act.wait_ge(g.pool_step.sem, g.pool_step.at(1))
                    nc.scalar.activation(flat(shift), flat(shift), ACT.Exp, bias=top[:, 1, 0:1], scale=-1.0).then_inc(g.act_step.sem, 1)

                @block.vector
                def _(dve):
                    dve.wait_ge(g.act_step.sem, g.act_step.at(1))
                    nc.vector.scalar_tensor_tensor(flat(shift), flat(shift), 1e-10, flat(own), ALU.mult, ALU.add)
            g.chain.passed(1), g.pool_step.passed(1), g.act_step.passed(1)
            tiles([], [], turn_back(True), use, 7, feat=sums, extra=True)
            with nc.Block() as block:
                @block.vector
                def _(dve):
                    nc.vector.tensor_scalar(deg[:, 1, :], deg[:, 0, :], 1.0, None, ALU.add).then_inc(g.chain.sem, 1)
                    dve.wait_ge(g.act_step.sem, g.act_step.at(1))
                    nc.vector.reciprocal(dinv[:], deg[:, 0, :]).then_inc(g.chain.sem, 1)

                @block.scalar
                def _(act):
                    act.wait_ge(g.chain.sem, g.chain.at(1))
                    nc.scalar.activation(deg[:, 0, :], deg[:, 1, :], ACT.Sqrt).then_inc(g.act_step.sem, 1)
            g.chain.passed(2), g.act_step.passed(1)

    def sum_finish():
        with ExitStack() as c:
            w = sb("sum_w", [128, KD, D], F32, c)

            def use(dve, n, j, c0):
                nc.vector.tensor_tensor(tile_of(xres, n), tile_of(xres, n), ps[0:P, j, 0:D], ALU.add).then_inc(g.chain.sem, 1)
            tiles([(w[:], halves(io["L1_gnn_weight"]))], [], times(w, D), use, 1)

    def conv_finish(layer, table):
        with ExitStack() as c:
            raw = sb(f"conv_raw{layer}", [128, KD, D], F32, c)
            w = sb(f"conv_w{layer}", [128, KD, D], F32, c)
            b = sb(f"conv_b{layer}", [P, D], F32, c)
            h = sb(f"conv_h{layer}", [P, RING, D], F32, c)
            blocks = [(w[:, k, o * 128:(o + 1) * 128], raw[:, o, k * 128:(k + 1) * 128], 128) for o in range(KD) for k in range(KD)]

            def use(dve, n, j, c0):
                ch = g.chain.sem
                nc.vector.scalar_tensor_tensor(h[:, j, :], ps[0:P, j, 0:D], dinv[:, bass.ds(n, 1)], b[:], ALU.mult, ALU.add).then_inc(ch, 1)
                wait_chain(dve, c0 + 1)
                if table is not None:
                    nc.vector.tensor_scalar(h[:, j, :], h[:, j, :], 0.0, dinv[:, bass.ds(n, 1)], ALU.max, ALU.mult).then_inc(ch, 1)
                else:
                    nc.vector.tensor_tensor(tile_of(xres, n), tile_of(xres, n), h[:, j, :], ALU.add).then_inc(ch, 1)
            tiles([(raw[:], halves(io[f"L2_gnn_W{layer}"])), (b[:], io[f"L2_gnn_b{layer}"].partition_broadcast(P))],
                  blocks, times(w, D), use, 2,
                  sp_rows=(lambda n, j: [(table[bass.ds(P * n, P), :], h[:, j, :])]) if table is not None else None)

    def edge_project():
        with ExitStack() as c:
            w = sb("ep_w", [128, KD, 2 * D], F32, c)
            b = sb("ep_b", [P, 2 * D], F32, c)
            h = sb("ep_h", [P, RING, 2 * D], F32, c)

            def use(dve, n, j, c0):
                nc.vector.tensor_tensor(h[:, j, :], ps[0:P, j, :], b[:], ALU.add).then_inc(g.chain.sem, 1)
            tiles([(w[:, :, 0:D], halves(io["L3_gnn_W1"][0:D, :])), (w[:, :, D:2 * D], halves(io["L3_gnn_Wg"][0:D, :])),
                   (b[:, 0:D], io["L3_gnn_b1"].partition_broadcast(P)), (b[:, D:2 * D], io["L3_gnn_bg"].partition_broadcast(P))],
                  [], times(w, 2 * D), use, 1,
                  sp_rows=lambda n, j: [(t_edge[bass.ds(P * n, P), :], h[:, j, :])])

    def edge_gated():
        DE = 64
        GE = 2 * RING
        with ExitStack() as c:
            rows = sb("eg_rows", [P, GE, 2 * D], F32, c)
            hot = sb("eg_hot", [P, RING, P], F32, c)
            ea = sb("eg_ea", [P, RING, 2, DE], F32, c)
            eaT = sb("eg_eaT", [2 * DE, RING, P], F32, c)
            w1g = sb("eg_w1g", [2 * DE, 2 * D], F32, c)
            w2 = sb("eg_w2", [128, KD, D], F32, c)
            b2 = sb("eg_b2", [P, D], F32, c)
            rT = sb("eg_rT", [128, RING, KD, P], F32, c)
            pre = sb("eg_pre", [P, RING, 2 * D], F32, c)
            msg = sb("eg_msg", [P, RING, D], F32, c)
            TB, PB, HB, CB, AB = 0, 1, 3, 5, 6
            NL = 6
            PAIRS, last_chunk = (NCH + 1) // 2, NCH - 1
            chunks_from = lambda n: 1 if isinstance(n, int) and n == last_chunk else 2
            pair = lambda i, j: (GE // 2) * i + j // 2

            with nc.Block() as block:
                @block.gpsimd
                def _(pool):
                    gathers(pool, t_edge, rows, GE // RING, free=g.gpre_done)

                @block.sync
                def _(sp):
                    for h in range(2):
                        sp.dma_start(w1g[h * DE:(h + 1) * DE, 0:D], io["L3_gnn_W1"][D:D + DE, :]).then_inc(g.loaded.sem, 16)
                        sp.dma_start(w1g[h * DE:(h + 1) * DE, D:2 * D], io["L3_gnn_Wg"][D:D + DE, :]).then_inc(g.loaded.sem, 16)
                    sp.dma_start(w2[:], halves(io["L3_gnn_W2"])).then_inc(g.loaded.sem, 16)
                    sp.dma_start(b2[:], io["L3_gnn_b2"].partition_broadcast(P)).then_inc(g.loaded.sem, 16)

                    def attributes(m, j, first, chunks=2):
                        if not first:
                            sp.wait_ge(g.ea_turned.sem, g.ea_turned.at(m - RING + 1))
                        sp.dma_start(ea[:, j, 0:chunks, :], io["edge_attr_64"][bass.ds(2 * P * m, chunks * P), :].rearrange("(h p) d -> p h d", p=P)).then_inc(store[j].sem, 16)

                    def body(i, first):
                        for j in range(RING):
                            attributes(RING * i + j, j, first)
                    rounds(sp, PAIRS // RING, body)
                    for m in range(PAIRS // RING * RING, PAIRS):
                        attributes(m, m % RING, False, chunks=min(2, NCH - 2 * m))

                @block.tensor
                def _(pe):
                    pe.wait_ge(g.loaded.sem, g.loaded.at(16 * NL))

                    def turn(n, i, j, first):
                        if j % 2 == 0:
                            s = j // 2
                            rows_out = chunks_from(n) * DE
                            if not (first and j < 2):
                                pe.wait_ge(g.eaT_ready.sem, g.eaT_ready.at(pair(i, j)))
                            hold_pe(store[s], 16 * i + 16)
                            nc.tensor.transpose(ps[0:rows_out, TB, 0:P], ea[:, s].rearrange("p h d -> p (h d)")[:, 0:rows_out], ident[0:P, 0:P]).then_inc(g.ea_turned.sem, 1)

                    def attr_products(n, i, j, first):
                        half = slice(j % 2 * DE, (j % 2 + 1) * DE)
                        pe.wait_ge(g.eaT_ready.sem, g.eaT_ready.at(pair(i, j) + 1))
                        if not (first and j < 2):
                            pe.wait_ge(g.gpre_done.sem, g.gpre_done.at(n - 1))
                        nc.tensor.matmul(ps[0:P, PB + j % 2, :], eaT[half, j // 2, :], w1g[half, :], start=True, stop=True).then_inc(g.pre_ready.sem, 1)

                    def turn_pre(n, i, j, first):
                        hold_pe(g.gpre_done, n + 1)
                        if not (first and j < 2):
                            hold_pe(g.relu_done, n - 1)
                        for k in range(KD):
                            mm = nc.tensor.transpose(ps[:, HB + j % 2, k * P:(k + 1) * P], pre[:, j % RING, k * 128:(k + 1) * 128], ident[0:P, 0:P])
                        mm.then_inc(g.tile_ready.sem, 1)

                    def core(n, i, j, first):
                        pe.wait_ge(g.relu_done.sem, g.relu_done.at(n + 1))
                        if not (first and j < 1):
                            pe.wait_ge(g.msg_done.sem, g.msg_done.at(2 * n))
                        for k in range(KD):
                            mm = nc.tensor.matmul(ps[0:P, CB, 0:D], rT[:, j % RING, k, :], w2[:, k, :], start=(k == 0), stop=(k == KD - 1))
                        mm.then_inc(g.core_ready.sem, 1)

                    def agg(n, i, j, first):
                        pe.wait_ge(g.msg_done.sem, g.msg_done.at(2 * n + 2))
                        pe.wait_ge(g.one_hot.sem, g.one_hot.at(n + 1))
                        if not (first and j < 2):
                            pe.wait_ge(g.added.sem, g.added.at(n))
                        for k in range(KD):
                            mm = nc.tensor.matmul(ps[:, AB + j % 2, k * P:(k + 1) * P], msg[:, j % RING, k * 128:(k + 1) * 128], hot[:, j % RING, :], start=True, stop=True)
                        mm.then_inc(g.agg_ready.sem, 1)
                    steps(pe, NCH, GE, [(8, turn), (4, attr_products), (2, turn_pre), (1, core), (0, agg)])

                @block.scalar
                def _(act):
                    def attr(n, i, j, first):
                        if j % 2 == 0:
                            rows_out = chunks_from(n) * DE
                            hold_act(g.ea_turned, pair(i, j) + 1)
                            if not first:
                                hold_act(g.pre_ready, n - GE + 2)
                            nc.scalar.copy(eaT[0:rows_out, j // 2, :], ps[0:rows_out, TB, 0:P]).then_inc(g.eaT_ready.sem, 1)

                    def relu(n, i, j, first):
                        hold_act(g.tile_ready, n + 1)
                        if not (first and j < RING):
                            hold_act(g.core_ready, n - RING + 1)
                        nc.scalar.activation(rT[:, j % RING], ps[:, HB + j % 2, 0:KD * P].rearrange("p (k t) -> p k t", k=KD), ACT.Relu).then_inc(g.relu_done.sem, 1)

                    def gate(n, i, j, first):
                        hold_act(g.gpre_done, n + 1)
                        nc.scalar.activation(pre[:, j % RING, D:2 * D], pre[:, j % RING, D:2 * D], ACT.Sigmoid).then_inc(g.gate_done.sem, 1)
                    steps(act, NCH, GE, [(6, attr), (1, relu), (1, gate)])

                @block.vector
                def _(dve):
                    nc.vector.memset(featT[:], 0.0).then_inc(g.added.sem, 1)
                    dve.wait_ge(g.loaded.sem, g.loaded.at(16 * NL))
                    windows = []

                    def gpre(n, i, j, first):
                        s = j % RING
                        dve.wait_ge(g.pre_ready.sem, g.pre_ready.at(n + 1))
                        if not (first and j < RING):
                            dve.wait_ge(g.msg_done.sem, g.msg_done.at(2 * (n - RING + 1)))
                        dve.wait_ge(gath[j].sem, gath[j].at(16 * i + 16))
                        nc.vector.tensor_tensor(pre[:, s, :], ps[0:P, PB + j % 2, :], rows[:, j, :], ALU.add).then_inc(g.gpre_done.sem, 1)
                        if not (first and j < RING):
                            dve.wait_ge(g.agg_ready.sem, g.agg_ready.at(n - RING + 1))
                        nc.vector.tensor_scalar(hot[:, s, :], iota[:], dloc[:, bass.ds(n, 1)], None, ALU.is_equal).then_inc(g.one_hot.sem, 1)

                    def message(n, i, j, first):
                        s = j % RING
                        dve.wait_ge(g.core_ready.sem, g.core_ready.at(n + 1))
                        if not (first and j < RING):
                            dve.wait_ge(g.agg_ready.sem, g.agg_ready.at(n - RING + 1))
                        nc.vector.tensor_tensor(msg[:, s, :], ps[0:P, CB, 0:D], b2[:], ALU.add).then_inc(g.msg_done.sem, 1)
                        dve.wait_ge(g.msg_done.sem, g.msg_done.at(2 * n + 1))
                        dve.wait_ge(g.gate_done.sem, g.gate_done.at(n + 1))
                        nc.vector.tensor_tensor(msg[:, s, :], msg[:, s, :], pre[:, s, D:2 * D], ALU.mult).then_inc(g.msg_done.sem, 1)

                    def add(n, i, j, first):
                        if j % RING == 0:
                            windows[:] = starts(dve, nc.vector, (GE // RING) * i + j // RING)
                        b = windows[j % RING]
                        dve.wait_ge(g.agg_ready.sem, g.agg_ready.at(n + 1))
                        dve.wait_ge(g.added.sem, g.added.at(n + 1))
                        f = featT[:, :, bass.ds(b, P)]
                        nc.vector.tensor_tensor(f, f, ps[:, AB + j % 2, 0:KD * P].rearrange("p (k t) -> p k t", k=KD), ALU.add).then_inc(g.added.sem, 1)
                    steps(dve, NCH, GE, [(3, gpre), (1, message), (0, add)])
        gathers_passed(GE // RING)
        for j in range(RING):
            store[j].passed(16 * ((PAIRS - j + RING - 1) // RING))
        g.ea_turned.passed(PAIRS), g.eaT_ready.passed(PAIRS)
        g.loaded.passed(16 * NL), g.added.passed(1 + NCH), g.msg_done.passed(2 * NCH)
        for s in (g.pre_ready, g.tile_ready, g.relu_done, g.gpre_done, g.gate_done, g.core_ready, g.one_hot, g.agg_ready):
            s.passed(NCH)

    def sums_to_xn():
        def use(dve, n, j, c0):
            nc.vector.tensor_tensor(tile_of(xn, n), tile_of(xn, n), ps[0:P, j, 0:D], ALU.add).then_inc(g.chain.sem, 1)
        tiles([], [], turn_back(False), use, 1)

    def choose(L, T, E, softmaxes, picks, iota_e, work, load_scale=None, index_out=None, pw=None):
        ch = g.chain
        marks = []
        t3 = lambda k: work[:, k * T * E:(k + 1) * T * E].rearrange("p (t e) -> p t e", e=E)
        v2 = lambda k: work[:, 6 * T * E + (k - 6) * T:6 * T * E + (k - 5) * T]
        bc = lambda ap: ap.unsqueeze(2).to_broadcast([P, T, E])
        ie = iota_e[:, 0:E].unsqueeze(1).to_broadcast([P, T, E])
        with nc.Block() as block:
            count = [0]

            @block.vector
            def _(dve):
                def link(ins):
                    count[0] += 1
                    ins.then_inc(ch.sem, 1)
                    dve.wait_ge(ch.sem, ch.at(count[0]))

                def exp_of(ap):
                    marks.append((count[0], ap))
                    dve.wait_ge(g.act_step.sem, g.act_step.at(len(marks)))

                def softmax(a):
                    link(nc.vector.tensor_reduce(v2(6), a, X, ALU.max))
                    link(nc.vector.tensor_tensor(a, a, bc(v2(6)), ALU.subtract))
                    exp_of(a)
                    link(nc.vector.tensor_reduce(v2(6), a, X, ALU.add))
                    link(nc.vector.reciprocal(v2(7), v2(6)))
                    link(nc.vector.tensor_tensor(a, a, bc(v2(7)), ALU.mult))

                a = L
                if softmaxes >= 1:
                    softmax(a)
                if softmaxes == 2:
                    cap, per_load = load_scale
                    link(nc.vector.tensor_scalar(t3(0), a, per_load, None, ALU.mult))
                    link(nc.vector.reciprocal(t3(1), t3(0)))
                    link(nc.vector.tensor_scalar(t3(1), t3(1), cap, -1.0, ALU.mult, ALU.add))
                    link(nc.vector.tensor_scalar(t3(0), t3(0), cap, None, ALU.is_gt))
                    link(nc.vector.tensor_scalar(t3(1), t3(1), 3e38, None, ALU.min))
                    link(nc.vector.tensor_tensor(t3(1), t3(1), t3(0), ALU.mult))
                    link(nc.vector.tensor_scalar(t3(1), t3(1), 1.0, None, ALU.add))
                    link(nc.vector.tensor_tensor(a, a, t3(1), ALU.mult))
                    softmax(a)
                for k in range(picks):
                    link(nc.vector.tensor_reduce(v2(8 + k), a, X, ALU.max))
                    link(nc.vector.tensor_tensor(t3(0), a, bc(v2(8 + k)), ALU.not_equal))
                    link(nc.vector.scalar_tensor_tensor(t3(0), t3(0), 1024.0, ie, ALU.mult, ALU.add) if T == 1 else
                         nc.vector.tensor_scalar(t3(0), t3(0), 1024.0, None, ALU.mult))
                    if T > 1:
                        link(nc.vector.tensor_tensor(t3(0), t3(0), ie, ALU.add))
                    link(nc.vector.tensor_reduce(v2(6), t3(0), X, ALU.min))
                    if index_out is not None:
                        link(nc.vector.tensor_copy(index_out[0:1, k:k + 1], v2(6)[0:1, :]))
                    link(nc.vector.tensor_tensor(t3(2 + k), ie, bc(v2(6)), ALU.is_equal))
                    if k + 1 < picks:
                        link(nc.vector.tensor_scalar(t3(1), t3(2 + k), -3e38, None, ALU.mult))
                        link(nc.vector.tensor_tensor(t3(4), t3(2 + k), a, ALU.mult))
                        link(nc.vector.tensor_tensor(a, a, t3(4), ALU.subtract))
                        link(nc.vector.tensor_tensor(a, a, t3(1), ALU.add))
                if picks == 2:
                    link(nc.vector.tensor_tensor(v2(9), v2(9), v2(8), ALU.subtract))
                    exp_of(v2(9))
                    link(nc.vector.tensor_scalar(v2(6), v2(9), 1.0, None, ALU.add))
                    link(nc.vector.reciprocal(v2(6), v2(6)))
                    link(nc.vector.tensor_tensor(v2(7), v2(9), v2(6), ALU.mult))
                    for k in range(2):
                        link(nc.vector.tensor_copy(pw[:, k, :], v2(6 + k)))

            @block.scalar
            def _(act):
                for at, ap in marks:
                    act.wait_ge(ch.sem, ch.at(at))
                    nc.scalar.activation(ap, ap, ACT.Exp).then_inc(g.act_step.sem, 1)
        ch.passed(count[0]), g.act_step.passed(len(marks))

    def expert_index(iota_e):
        with nc.Block() as block:
            @block.gpsimd
            def _(pool):
                nc.gpsimd.iota(iota_e[:], [[1, 32]], base=0, channel_multiplier=0, allow_small_or_imprecise_dtypes=True)

    def route(load, turn, w, bias, L, E):
        per_bank = 512 // E
        banks = -(-NT // per_bank)
        with nc.Block() as block:
            @block.sync
            def _(sp):
                for d, src in load:
                    sp.dma_start(d, src).then_inc(g.loaded.sem, 16)

            @block.tensor
            def _(pe):
                pe.wait_ge(g.loaded.sem, g.loaded.at(16 * len(load)))
                if turn is not None:
                    for k in range(KD):
                        mm = nc.tensor.transpose(ps[0:128, 7, k * E:(k + 1) * E], turn[:, k * 128:(k + 1) * 128], ident[0:E, 0:E])
                    mm.then_inc(g.turned.sem, 1)
                    pe.wait_ge(g.staged.sem, g.staged.at(1))
                for t in range(NT):
                    for k in range(KD):
                        mm = nc.tensor.matmul(ps[0:P, t // per_bank, t % per_bank * E:(t % per_bank + 1) * E], featT[:, k, t * P:(t + 1) * P], w[:, k, :],
                                              start=(k == 0), stop=(k == KD - 1))
                mm.then_inc(g.tile_ready.sem, 1)

            @block.vector
            def _(dve):
                dve.wait_ge(g.loaded.sem, g.loaded.at(16 * len(load)))
                if turn is not None:
                    dve.wait_ge(g.turned.sem, g.turned.at(1))
                    nc.vector.tensor_copy(w.rearrange("p k e -> p (k e)"), ps[0:128, 7, 0:KD * E]).then_inc(g.staged.sem, 1)
                dve.wait_ge(g.tile_ready.sem, g.tile_ready.at(1))
                for b in range(banks):
                    ts = slice(b * per_bank, min(NT, (b + 1) * per_bank))
                    n = ts.stop - ts.start
                    nc.vector.tensor_tensor(L[:, ts, :], ps[0:P, b, 0:n * E].rearrange("p (t e) -> p t e", e=E),
                                            bias.unsqueeze(1).to_broadcast([P, n, E]), ALU.add)
        g.loaded.passed(16 * len(load)), g.tile_ready.passed(1)
        if turn is not None:
            g.turned.passed(1), g.staged.passed(1)

    def two_experts(w1, b1, w2, pw, bias, acc):
        E, F = 2, 4
        with ExitStack() as c:
            hid = sb("f0_hid", [128, E, F, BT * P], F32, c)

            def blocks(eng, body):
                body(0, BT, 0, 0, True)
                with eng.Fori(1, NB) as b:
                    body(b, BT, b * F * E, b * E * BT, False)
                if NT % BT:
                    body(NB, NT % BT, NB * F * E, NB * E * BT, False)

            with nc.Block() as block:
                @block.tensor
                def _(pe):
                    def body(b, nt, h0, y0, first):
                        cols = nt * P

                        def hidden(e):
                            for f in range(F):
                                if not (first and e == 0):
                                    hold_pe(g.hid_done, h0 + (e - 1) * F + f + 1)
                                for k in range(KD):
                                    mm = nc.tensor.matmul(ps[:, f, 0:cols], w1[:, e, k, f * 128:(f + 1) * 128], featT[:, k, bass.ds(b * BT * P, cols)],
                                                          start=(k == 0), stop=(k == KD - 1))
                                mm.then_inc(g.hid_ready.sem, 1)

                        def outputs(e):
                            pe.wait_ge(g.hid_done.sem, g.hid_done.at(h0 + (e + 1) * F))
                            for t in range(nt):
                                if e > 0:
                                    hold_pe(g.y_done, y0 + t + 1)
                                elif not first:
                                    hold_pe(g.y_done, y0 - BT + t + 1)
                                for f in range(F):
                                    mm = nc.tensor.matmul(ps[0:P, F + t, 0:D], hid[:, e, f, t * P:(t + 1) * P], w2[:, e, f, :], start=(f == 0), stop=(f == F - 1))
                                mm.then_inc(g.y_ready.sem, 1)
                        for e in range(E):
                            hidden(e)
                        for e in range(E):
                            outputs(e)
                    blocks(pe, body)

                @block.scalar
                def _(act):
                    def body(b, nt, h0, y0, first):
                        cols = nt * P
                        for e in range(E):
                            if not first:
                                hold_act(g.y_ready, y0 - (E - 1 - e) * BT)
                            for f in range(F):
                                hold_act(g.hid_ready, h0 + e * F + f + 1)
                                nc.scalar.activation(hid[:, e, f, 0:cols], ps[:, f, 0:cols], ACT.Gelu, bias=b1[:, e, f:f + 1]).then_inc(g.hid_done.sem, 1)
                    blocks(act, body)

                @block.vector
                def _(dve):
                    def body(b, nt, h0, y0, first):
                        for e in range(E):
                            for t in range(nt):
                                a = tile_of(acc, BT * b + t)
                                dve.wait_ge(g.y_ready.sem, g.y_ready.at(y0 + e * nt + t + 1))
                                if e > 0:
                                    dve.wait_ge(g.y_done.sem, g.y_done.at(y0 + (e - 1) * nt + t + 1))
                                nc.vector.scalar_tensor_tensor(a, ps[0:P, F + t, 0:D], pw[:, e, :], a, ALU.mult, ALU.add).then_inc(g.y_done.sem, 1)
                        for t in range(nt):
                            a = tile_of(acc, BT * b + t)
                            dve.wait_ge(g.y_done.sem, g.y_done.at(y0 + (E - 1) * nt + t + 1))
                            nc.vector.tensor_tensor(a, a, bias, ALU.add)
                    blocks(dve, body)
        for s in (g.hid_ready, g.hid_done):
            s.passed(F * E * (NB + (1 if NT % BT else 0)))
        g.y_ready.passed(E * NT), g.y_done.passed(E * NT)

    def dispatch(tag, E, picks, work, slot, expert, leads, TS, loads):
        halves_ = ((0, 13), (13, NT))
        with ExitStack() as c:
            upper = sb(tag + "_upper", [P, P], F32, c)
            by_tile = lambda k: work[:, k * NT * E:(k + 1) * NT * E].rearrange("p (t e) -> p t e", e=E)
            hot = lambda k: by_tile(2 + k)
            run = [by_tile(0), by_tile(1)]
            a = by_tile(4)
            cmp = work[:, 5 * NT * E:6 * NT * E].rearrange("p (e t) -> p e t", t=NT)
            step = sb(tag + "_step", [P, NT], F32, c)
            ends = [sb(f"{tag}_ends{q}", [P, E], F32, c) for q in range(2)]
            te = sb(tag + "_te", [P, E], F32, c)
            pos = sb(tag + "_pos", [P, picks, NT], F32, c)
            ecmp = stage[0:1].rearrange("p r c -> p (r c)")[:, 0:TS * E].rearrange("p (s e) -> p s e", e=E)
            ef = sb(tag + "_ef", [1, TS], F32, c)
            count = [0]
            with nc.Block() as block:
                @block.sync
                def _(sp):
                    for d, s in loads:
                        sp.dma_start(d, s).then_inc(g.loaded.sem, 16)

                @block.gpsimd
                def _(pool):
                    nc.gpsimd.affine_select(out=upper[:], in_=ones[0:P, 0:P], pattern=[[1, P]], compare_op=ALU.is_gt, fill=0.0,
                                            base=0, channel_multiplier=-1).then_inc(g.pool_step.sem, 1)
                    pool.wait_ge(g.turned.sem, g.turned.at(2))
                    for t in range(NT):
                        for k in range(picks):
                            nc.gpsimd.indirect_dma_start(out=t_disp[0:TS * P, :], out_offset=bass.IndirectOffsetOnAxis(ap=slot[:, k, t:t + 1], axis=0),
                                                         in_=xn[:, t, :], in_offset=None).then_inc(g.stored.sem, 16)
                    pool.wait_ge(g.stored.sem, g.stored.at(16 * NT * picks))

                @block.tensor
                def _(pe):
                    pe.wait_ge(g.chain.sem, g.chain.at(1))
                    pe.wait_ge(g.pool_step.sem, g.pool_step.at(1))
                    for q, (t0, t1) in enumerate(halves_):
                        nc.tensor.matmul(ps[0:P, q, 0:(t1 - t0) * E], upper[:], a[:, t0:t1, :].rearrange("p t e -> p (t e)"), start=True, stop=True)
                        mm = nc.tensor.matmul(ps[0:P, 2 + q, 0:(t1 - t0) * E], ones[0:P, 0:P], a[:, t0:t1, :].rearrange("p t e -> p (t e)"), start=True, stop=True)
                    mm.then_inc(g.turned.sem, 1)

                @block.vector
                def _(dve):
                    def link(ins):
                        count[0] += 1
                        ins.then_inc(g.chain.sem, 1)
                        dve.wait_ge(g.chain.sem, g.chain.at(count[0]))

                    def from_psum(b, t0, t1):
                        return ps[0:P, b, 0:(t1 - t0) * E].rearrange("p (t e) -> p t e", e=E)

                    def running(bufs, length, at):
                        q, d = 0, 1
                        while d < length:
                            link(nc.vector.tensor_copy(at(bufs[1 - q], 0, d), at(bufs[q], 0, d)))
                            link(nc.vector.tensor_tensor(at(bufs[1 - q], d, length), at(bufs[q], d, length), at(bufs[q], 0, length - d), ALU.add))
                            q, d = 1 - q, 2 * d
                        return q

                    if picks == 2:
                        link(nc.vector.tensor_tensor(a, hot(0), hot(1), ALU.add))
                    else:
                        link(nc.vector.tensor_copy(a, hot(0)))
                    link(nc.vector.tensor_scalar(step[:], iota[:, 0:NT], float(P), None, ALU.mult))
                    dve.wait_ge(g.turned.sem, g.turned.at(1))
                    for q, (t0, t1) in enumerate(halves_):
                        link(nc.vector.tensor_copy(run[0][:, t0:t1, :], from_psum(2 + q, t0, t1)))
                    r = running(run, NT, lambda b, u, v: b[:, u:v, :])
                    total = run[r][:, NT - 1:NT, :].rearrange("p a e -> p (a e)")
                    link(nc.vector.tensor_tensor(cmp, total.unsqueeze(2).to_broadcast([P, E, NT]), step[:].unsqueeze(1).to_broadcast([P, E, NT]), ALU.is_gt))
                    link(nc.vector.tensor_reduce(te[:], cmp, X, ALU.add))
                    link(nc.vector.tensor_copy(ends[0][:], te[:]))
                    z = running(ends, E, lambda b, u, v: b[:, u:v])
                    link(nc.vector.tensor_tensor(ecmp, iota[0:1, 0:TS].unsqueeze(2).to_broadcast([1, TS, E]), ends[z][0:1, :].unsqueeze(1).to_broadcast([1, TS, E]), ALU.is_ge))
                    link(nc.vector.tensor_reduce(ef[:], ecmp, X, ALU.add))
                    link(nc.vector.tensor_scalar(ef[:], ef[:], float(E - 1), None, ALU.min))
                    link(nc.vector.memset(expert[:], 0))
                    for l, lead in enumerate(leads):
                        link(nc.vector.tensor_copy(expert[:, l, 0:TS - lead], ef[:, lead:TS]))
                    link(nc.vector.tensor_tensor(te[:], ends[z][:], te[:], ALU.subtract))
                    link(nc.vector.tensor_scalar(te[:], te[:], float(P), None, ALU.mult))
                    for q, (t0, t1) in enumerate(halves_):
                        link(nc.vector.tensor_tensor(run[r][:, t0:t1, :], run[r][:, t0:t1, :], from_psum(2 + q, t0, t1), ALU.subtract))
                        link(nc.vector.tensor_tensor(run[r][:, t0:t1, :], run[r][:, t0:t1, :], from_psum(q, t0, t1), ALU.add))
                    link(nc.vector.tensor_tensor(run[r], run[r], te[:].unsqueeze(1).to_broadcast([P, NT, E]), ALU.add))
                    for k in range(picks):
                        link(nc.vector.tensor_tensor(run[1 - r], run[r], hot(k), ALU.mult))
                        link(nc.vector.tensor_reduce(pos[:, k, :], run[1 - r], X, ALU.add))
                    nc.vector.tensor_copy(slot[:], pos[:]).then_inc(g.turned.sem, 1)
            g.chain.passed(count[0]), g.turned.passed(2), g.pool_step.passed(1), g.stored.passed(16 * NT * picks)

    def expert_tiles(E, TS, expert, leads, LD, layers):
        NLAY = len(layers)
        R = 4
        RI = LOT
        cut = Carver(featT[:].rearrange("p k n -> p (k n)"))
        xd = stage[0:P].rearrange("p r c -> p (r c)")[:, 0:RI * D].rearrange("p (r d) -> p r d", r=RI)
        inT = [cut.take(128, R * P * ((w[0] + 127) // 128)).rearrange("p (r k t) -> p r k t", r=R, t=P) for w in layers]
        pre = [cut.take(P, R * w[1]).rearrange("p (r d) -> p r d", r=R) for w in layers]

        def tile_experts(eng, ns, l):
            held = []

            def of(n, j):
                if j == leads[l]:
                    reads[0] += 1
                    regs = [eng.alloc_register(f"expert{reads[0]}_{r}") for r in range(LOT)]
                    ns.load(regs, expert[0:1, l, bass.ds(n - leads[l], LOT)])
                    held[:] = [ns.snap(r, donate=True, min_val=0, max_val=E - 1) for r in regs]
                return held[(j - leads[l]) % LOT] if held else ns.value_load(expert[0:1, NLAY - 1, n:n + 1], min_val=0, max_val=E - 1)
            return of

        TB = lambda l: 2 * l
        MB = lambda l: 2 * l + 1
        turned = [g.turned, g.pre_ready, g.hid_ready]
        in_ready = [g.evicted, g.relu_done, g.hid_done]
        product = [g.tile_ready, g.core_ready, g.y_ready]
        biased = [g.staged, g.msg_done, g.y_done]
        with nc.Block() as block:
            @block.sync
            def _(sp):
                def rows_in(n, i, j, first):
                    if not first:
                        sp.wait_ge(turned[0].sem, turned[0].at(n - RI + 1))
                    sp.dma_start(xd[:, j, :], t_disp[bass.ds(P * n, P), :]).then_inc(wload[j].sem, 16)
                steps(sp, TS, RI, [(0, rows_in)])

            @block.gpsimd
            def _(pool):
                def rows_out(n, i, j, first):
                    hold_pool(biased[NLAY - 1], n + 1)
                    pool.dma_start(t_back[bass.ds(P * n, P), :], pre[-1][:, j, :]).then_inc(gath[j].sem, 16)
                steps(pool, TS, R, [(0, rows_out)])
                for j in range(R):
                    pool.wait_ge(gath[j].sem, gath[j].at(16 * ((TS - j + R - 1) // R)))

            @block.tensor
            def _(pe):
                pe.wait_ge(g.loaded.sem, g.loaded.at(16 * LD))

                def turn(l):
                    wide = layers[l][0]

                    def f(n, i, j, first):
                        if l == 0:
                            hold_pe(wload[j], 16 * (i + 1))
                        else:
                            hold_pe(biased[l - 1], n + 1)
                        if not (first and j == 0):
                            hold_pe(in_ready[l], n)
                        src = xd[:, j, :] if l == 0 else pre[l - 1][:, j % R, :]
                        for k in range((wide + 127) // 128):
                            w = min(128, wide - 128 * k)
                            mm = nc.tensor.transpose(ps[0:w, TB(l), k * P:(k + 1) * P], src[:, 128 * k:128 * k + w], ident[0:P, 0:P])
                        mm.then_inc(turned[l].sem, 1)
                    return f

                def multiply(l):
                    wide, out_w, weights = layers[l][0:3]

                    expert_of = tile_experts(pe, nc.tensor, l)

                    def f(n, i, j, first):
                        e = expert_of(n, j)
                        hold_pe(in_ready[l], n + 1)
                        if not (first and j == 0):
                            hold_pe(biased[l], n)
                        kk = (wide + 127) // 128
                        for k in range(kk):
                            w = min(128, wide - 128 * k)
                            mm = nc.tensor.matmul(ps[0:P, MB(l), 0:out_w], inT[l][0:w, j % R, k, :], weights(e, k), start=(k == 0), stop=(k == kk - 1))
                        mm.then_inc(product[l].sem, 1)
                    return f
                parts = []
                for l in range(NLAY):
                    parts += [(leads[l] + 1, turn(l)), (leads[l], multiply(l))]
                steps(pe, TS, RI, parts)

            @block.scalar
            def _(act):
                def copy_in(l):
                    wide, func = layers[l][0], layers[l][4]

                    def f(n, i, j, first):
                        hold_act(turned[l], n + 1)
                        if not first:
                            hold_act(product[l], n - R + 1)
                        w = min(128, wide)
                        nc.scalar.activation(inT[l][0:w, j], ps[0:w, TB(l), 0:((wide + 127) // 128) * P].rearrange("p (k t) -> p k t", t=P), func).then_inc(in_ready[l].sem, 1)
                    return f
                steps(act, TS, R, [(leads[l] + 1, copy_in(l)) for l in range(NLAY)])

            @block.vector
            def _(dve):
                dve.wait_ge(g.loaded.sem, g.loaded.at(16 * LD))

                def add_bias(l):
                    out_w, bias = layers[l][1], layers[l][3]

                    expert_of = tile_experts(dve, nc.vector, l)

                    def f(n, i, j, first):
                        e = expert_of(n, j)
                        if not (first and j < R):
                            if l + 1 < NLAY:
                                dve.wait_ge(turned[l + 1].sem, turned[l + 1].at(n - R + 1))
                            else:
                                dve.wait_ge(gath[j % R].sem, gath[j % R].at(16 * ((RI // R) * i + j // R)))
                        dve.wait_ge(product[l].sem, product[l].at(n + 1))
                        nc.vector.tensor_tensor(pre[l][:, j % R, :], ps[0:P, MB(l), 0:out_w], bias(e), ALU.add).then_inc(biased[l].sem, 1)
                    return f
                steps(dve, TS, RI, [(leads[l], add_bias(l)) for l in range(NLAY)])
        g.loaded.passed(16 * LD)
        for q in (turned, in_ready, product, biased):
            for l in range(NLAY):
                q[l].passed(TS)
        for j in range(R):
            gath[j].passed(16 * ((TS - j + R - 1) // R))
        for j in range(RI):
            wload[j].passed(16 * ((TS - j + RI - 1) // RI))

    def collect(tag, picks, slot, pw, TS, result=None):
        with ExitStack() as c:
            y = sb(tag + "_y", [P, GR, D], F32, c)
            total = NT * picks
            with nc.Block() as block:
                @block.gpsimd
                def _(pool):
                    for n in range(total):
                        t, k, j = n // picks, n % picks, n % GR
                        if n >= GR:
                            pool.wait_ge(g.used.sem, g.used.at(n - GR + 1))
                        nc.gpsimd.indirect_dma_start(out=y[:, j, :], out_offset=None, in_=t_back[0:TS * P, :],
                                                     in_offset=bass.IndirectOffsetOnAxis(ap=slot[:, k, t:t + 1], axis=0)).then_inc(gath[j].sem, 16)

                @block.vector
                def _(dve):
                    for n in range(total):
                        t, k, j = n // picks, n % picks, n % GR
                        dve.wait_ge(gath[j].sem, gath[j].at(16 * (n // GR + 1)))
                        if k > 0:
                            dve.wait_ge(g.used.sem, g.used.at(n))
                        if pw is not None:
                            ins = nc.vector.scalar_tensor_tensor(xres[:, t, :], y[:, j, :], pw[:, k, t:t + 1], xres[:, t, :], ALU.mult, ALU.add)
                        else:
                            ins = nc.vector.scalar_tensor_tensor(xres[:, t, :], y[:, j, :], 0.0, xres[:, t, :], ALU.max, ALU.add)
                        ins.then_inc(g.used.sem, 1)

                if result is not None:
                    @block.sync
                    def _(sp):
                        for t in range(0, NT, RING):
                            sp.wait_ge(g.used.sem, g.used.at((t + RING) * picks))
                            sp.dma_start(result[t * P:(t + RING) * P, :].rearrange("(t p) d -> p t d", p=P), xres[:, t:t + RING, :]).then_inc(g.loaded.sem, 16)
                        sp.wait_ge(g.loaded.sem, g.loaded.at(16 * NT // RING))
        g.used.passed(total)
        if result is not None:
            g.loaded.passed(16 * NT // RING)
        for j in range(GR):
            gath[j].passed(16 * ((total - j + GR - 1) // GR))

    def ffn0():
        E = 8
        CAP = float(-((-N * 5) // (4 * E)))
        with ExitStack() as c:
            wr = sb("f0_wr", [128, KD, E], F32, c)
            br = sb("f0_br", [P, E], F32, c)
            mean = sb("f0_mean", [128, KD, P + 1], F32, c)
            L = sb("f0_L", [P, 1, E], F32, c)
            pw = sb("f0_pw", [P, 2, 1], F32, c)
            iota_e = sb("f0_iota", [P, 32], F32, c)
            work = sb("f0_work", [P, 6 * E + 4], F32, c)
            pick = sb("f0_pick", [1, 2], I32, c)
            w1 = sb("f0_w1", [128, 2, KD, 512], F32, c)
            w2 = sb("f0_w2", [128, 2, 4, D], F32, c)
            b1 = sb("f0_b1", [128, 2, 4], F32, c)
            b2 = sb("f0_b2", [P, 2, D], F32, c)
            bias = sb("f0_bias", [P, D], F32, c)
            b1rows = sb("f0_b1r", [4, 2, 128], F32, c)
            expert_index(iota_e)
            with nc.Block() as block:
                @block.sync
                def _(sp):
                    sp.dma_start(wr[:], halves(io["L0_ffn_Wr"])).then_inc(g.loaded.sem, 16)
                    sp.dma_start(br[:], io["L0_ffn_br"].partition_broadcast(P)).then_inc(g.loaded.sem, 16)

                @block.vector
                def _(dve):
                    nc.vector.tensor_reduce(mean[:, :, P:P + 1], featT[:, :, 0:N], X, ALU.add).then_inc(g.chain.sem, 1)
                    wait_chain(dve, 1)
                    nc.vector.tensor_scalar(mean[:, :, P:P + 1], mean[:, :, P:P + 1], 1.0 / N, None, ALU.mult).then_inc(g.chain.sem, 1)
                    wait_chain(dve, 2)
                    nc.vector.tensor_copy(mean[:, :, 0:P], mean[:, :, P:P + 1].to_broadcast([128, KD, P])).then_inc(g.chain.sem, 1)
                    dve.wait_ge(g.turned.sem, g.turned.at(1))
                    nc.vector.tensor_tensor(L[:, 0, :], ps[0:P, 0, 0:E], br[:], ALU.add).then_inc(g.chain.sem, 1)

                @block.tensor
                def _(pe):
                    pe.wait_ge(g.loaded.sem, g.loaded.at(32))
                    pe.wait_ge(g.chain.sem, g.chain.at(3))
                    for k in range(KD):
                        mm = nc.tensor.matmul(ps[0:P, 0, 0:E], mean[:, k, 0:P], wr[:, k, :], start=(k == 0), stop=(k == KD - 1))
                    mm.then_inc(g.turned.sem, 1)
            g.loaded.passed(32), g.chain.passed(4), g.turned.passed(1)
            choose(L[:], 1, E, 2, 2, iota_e, work[:], load_scale=(CAP, float(N)), index_out=pick, pw=pw)
            with nc.Block() as block:
                @block.sync
                def _(sp):
                    for j in range(2):
                        r = nc.sync.value_load(pick[0:1, j:j + 1], min_val=0, max_val=E - 1)
                        sp.dma_start(w1[:, j], io["L0_ffn_W1"][bass.ds(r, 1)].rearrange("e (k p) f -> p (e k) f", p=128)).then_inc(wload[j].sem, 16)
                        sp.dma_start(w2[:, j], io["L0_ffn_W2"][bass.ds(r, 1)].rearrange("e (k p) f -> p (e k) f", p=128)).then_inc(wload[j].sem, 16)
                        sp.dma_start(b1rows[:, j, :], io["L0_ffn_b1"][bass.ds(r, 1)].rearrange("e (f p) -> (e f) p", p=128)).then_inc(wload[j].sem, 16)
                        sp.dma_start(b2[:, j, :], io["L0_ffn_b2"][bass.ds(r, 1)].rearrange("e d -> (e d)").partition_broadcast(P)).then_inc(wload[j].sem, 16)

                @block.tensor
                def _(pe):
                    for j in range(2):
                        pe.wait_ge(wload[j].sem, wload[j].at(64))
                        mm = nc.tensor.transpose(ps[:, 0, 4 * j:4 * j + 4], b1rows[:, j, :], ident[0:4, 0:4])
                    mm.then_inc(g.turned.sem, 1)

                @block.vector
                def _(dve):
                    dve.wait_ge(g.turned.sem, g.turned.at(1))
                    nc.vector.tensor_copy(b1[:].rearrange("p e f -> p (e f)"), ps[:, 0, 0:8])
                    nc.vector.tensor_scalar(bias[:], b2[:, 0, :], pw[:, 0, :], None, ALU.mult).then_inc(g.chain.sem, 1)
                    wait_chain(dve, 1)
                    nc.vector.scalar_tensor_tensor(bias[:], b2[:, 1, :], pw[:, 1, :], bias[:], ALU.mult, ALU.add)
            g.turned.passed(1), g.chain.passed(1)
            for j in range(2):
                wload[j].passed(64)
            two_experts(w1, b1, w2, pw, bias[:], xn)

    def biases(tag, b, rows, cols, dst):
        with ExitStack() as c:
            raw = sb(tag + "_bias_rows", [rows * cols, 128], F32, c)
            with nc.Block() as block:
                @block.sync
                def _(sp):
                    sp.dma_start(raw[:], b).then_inc(g.loaded.sem, 16)

                @block.tensor
                def _(pe):
                    pe.wait_ge(g.loaded.sem, g.loaded.at(16))
                    nc.tensor.transpose(ps[:, 0, 0:rows * cols], raw[:], ident[0:rows * cols, 0:rows * cols]).then_inc(g.turned.sem, 1)

                @block.vector
                def _(dve):
                    dve.wait_ge(g.turned.sem, g.turned.at(1))
                    nc.vector.tensor_copy(dst, ps[:, 0, 0:rows * cols])
            g.loaded.passed(16), g.turned.passed(1)

    def one_row(ap, e):
        return ap[0:P, bass.ds(e, 1), :].rearrange("p a d -> p (a d)")

    def ffn1():
        E, RH = 6, 128
        TS = 2 * NT + E
        with ExitStack() as c:
            pw = sb("f1_pw", [P, 2, NT], F32, c)
            slot = sb("f1_slot", [P, 2, NT], I32, c)
            leads = [2 * l for l in reversed(range(3))]
            expert = sb("f1_expert", [1, 3, -(-TS // LOT) * LOT], I32, c)
            with ExitStack() as c2:
                rw1 = sb("f1_rw1", [128, KD, RH], F32, c2)
                rb1 = sb("f1_rb1", [RH, 1], F32, c2)
                rw2 = sb("f1_rw2", [RH, E], F32, c2)
                rb2 = sb("f1_rb2", [P, E], F32, c2)
                L = sb("f1_L", [P, NT, E], F32, c2)
                iota_e = sb("f1_iota", [P, 32], F32, c2)
                work = featT[0:P].rearrange("p k n -> p (k n)")
                rh = sb("f1_rh", [RH, RING, P], F32, c2)
                expert_index(iota_e)
                biases("f1_r", io["L1_ffn_router_b1"].rearrange("(a p) -> a p", a=1), 1, 1, rb1[:])
                with nc.Block() as block:
                    @block.sync
                    def _(sp):
                        sp.dma_start(rw1[:], halves(io["L1_ffn_router_w1"])).then_inc(g.loaded.sem, 16)
                        sp.dma_start(rw2[:], io["L1_ffn_router_w2"]).then_inc(g.loaded.sem, 16)
                        sp.dma_start(rb2[:], io["L1_ffn_router_b2"].partition_broadcast(P)).then_inc(g.loaded.sem, 16)

                    @block.tensor
                    def _(pe):
                        pe.wait_ge(g.loaded.sem, g.loaded.at(48))

                        def hidden(n, i, j, first):
                            if not first:
                                hold_pe(g.chain, n - RING + 1)
                            for k in range(KD):
                                mm = nc.tensor.matmul(ps[:, j, 0:P], rw1[:, k, :], featT[:, k, bass.ds(P * n, P)], start=(k == 0), stop=(k == KD - 1))
                            mm.then_inc(g.hid_ready.sem, 1)

                        def logits(n, i, j, first):
                            hold_pe(g.staged, n + 1)
                            nc.tensor.matmul(ps[0:P, j, 256:256 + E], rh[:, j, :], rw2[:], start=True, stop=True).then_inc(g.tile_ready.sem, 1)
                        steps(pe, NT, RING, [(3, hidden), (0, logits)])

                    @block.scalar
                    def _(act):
                        def body(i, first):
                            for j in range(RING):
                                n = RING * i + j
                                hold_act(g.hid_ready, n + 1)
                                nc.scalar.activation(rh[:, j, :], ps[:, j, 0:P], ACT.Relu, bias=rb1[:]).then_inc(g.staged.sem, 1)
                        rounds(act, NT // RING, body)

                    @block.vector
                    def _(dve):
                        dve.wait_ge(g.loaded.sem, g.loaded.at(48))
                        def body(i, first):
                            for j in range(RING):
                                n = RING * i + j
                                dve.wait_ge(g.tile_ready.sem, g.tile_ready.at(n + 1))
                                nc.vector.tensor_tensor(tile_of(L, n), ps[0:P, j, 256:256 + E], rb2[:], ALU.add).then_inc(g.chain.sem, 1)
                        rounds(dve, NT // RING, body)
                g.loaded.passed(48)
                for s in (g.hid_ready, g.staged, g.tile_ready, g.chain):
                    s.passed(NT)
                choose(L[:], NT, E, 1, 2, iota_e, work, pw=pw)
            w = [sb(f"f1_w{i}", [128, E, KD, D], F32, c) for i in range(3)]
            b = [sb(f"f1_b{i}", [128, E, D], F32, c) for i in range(3)]
            loads = []
            for i in range(3):
                loads.append((w[i][:].rearrange("p e k f -> p (e k) f"), io[f"L1_ffn_expert_w{i + 1}"].rearrange("e (k p) f -> p (e k) f", p=128)))
                loads.append((b[i][:].rearrange("p e f -> p (e f)"), io[f"L1_ffn_expert_b{i + 1}"].rearrange("e f -> (e f)").partition_broadcast(128)))
            dispatch("f1d", E, 2, work, slot, expert, leads, TS, loads)
            expert_tiles(E, TS, expert, leads, len(loads),
                         [(D, D, (lambda i: lambda e, k: w[i][:, bass.ds(e, 1), k, :].rearrange("p a f -> p (a f)"))(i),
                           (lambda i: lambda e: one_row(b[i], e))(i), ACT.Copy if i == 0 else ACT.Relu) for i in range(3)])
            collect("f1c", 2, slot, pw, TS)

    def ffn2():
        E, H = 32, 64
        TS = NT + E
        with ExitStack() as c:
            slot = sb("f2_slot", [P, 1, NT], I32, c)
            leads = [2 * l for l in reversed(range(2))]
            expert = sb("f2_expert", [1, 2, -(-TS // LOT) * LOT], I32, c)
            with ExitStack() as c2:
                raw = sb("f2_rw", [E, D], F32, c2)
                rw = sb("f2_rwT", [128, KD, E], F32, c2)
                rb = sb("f2_rb", [P, E], F32, c2)
                L = sb("f2_L", [P, NT, E], F32, c2)
                iota_e = sb("f2_iota", [P, 32], F32, c2)
                work = featT[0:P].rearrange("p k n -> p (k n)")
                expert_index(iota_e)

                route([(raw[:], io["L2_ffn_router_w"]), (rb[:], io["L2_ffn_router_b"].partition_broadcast(P))], raw[:], rw[:], rb[:], L[:], E)
                choose(L[:], NT, E, 0, 1, iota_e, work)
            w1 = sb("f2_w1", [128, E, KD, H], F32, c)
            w2 = sb("f2_w2", [H, E, D], F32, c)
            b1 = sb("f2_b1", [128, E, H], F32, c)
            b2 = sb("f2_b2", [128, E, D], F32, c)
            loads = [(w1[:].rearrange("p e k h -> p (e k) h"), io["L2_ffn_W1"].rearrange("e (k p) h -> p (e k) h", p=128)),
                     (w2[:], io["L2_ffn_W2"].rearrange("e h d -> h e d")),
                     (b1[:].rearrange("p e h -> p (e h)"), io["L2_ffn_b1"].rearrange("e h -> (e h)").partition_broadcast(128)),
                     (b2[:].rearrange("p e d -> p (e d)"), io["L2_ffn_b2"].rearrange("e d -> (e d)").partition_broadcast(128))]
            dispatch("f2d", E, 1, work, slot, expert, leads, TS, loads)
            expert_tiles(E, TS, expert, leads, len(loads),
                         [(D, H, lambda e, k: w1[:, bass.ds(e, 1), k, :].rearrange("p a h -> p (a h)"), lambda e: one_row(b1, e), ACT.Copy),
                          (H, D, lambda e, k: w2[:, bass.ds(e, 1), :].rearrange("p a d -> p (a d)"), lambda e: one_row(b2, e), ACT.Relu)])
            collect("f2c", 1, slot, None, TS)

    def ffn3():
        E, H = 8, 512
        TS = 2 * NT + E
        with ExitStack() as c:
            pw = sb("f3_pw", [P, 2, NT], F32, c)
            slot = sb("f3_slot", [P, 2, NT], I32, c)
            leads = [2 * l for l in reversed(range(2))]
            expert = sb("f3_expert", [1, 2, -(-TS // LOT) * LOT], I32, c)
            with ExitStack() as c2:
                wr = sb("f3_wr", [128, KD, E], F32, c2)
                br = sb("f3_br", [P, E], F32, c2)
                L = sb("f3_L", [P, NT, E], F32, c2)
                iota_e = sb("f3_iota", [P, 32], F32, c2)
                work = featT[0:P].rearrange("p k n -> p (k n)")
                expert_index(iota_e)

                route([(wr[:], halves(io["L3_ffn_Wr"])), (br[:], io["L3_ffn_br"].partition_broadcast(P))], None, wr[:], br[:], L[:], E)
                choose(L[:], NT, E, 0, 2, iota_e, work, pw=pw)
            w1 = sb("f3_w1", [128, E, KD, H], F32, c)
            w2 = sb("f3_w2", [128, E, H // 128, D], F32, c)
            b1 = sb("f3_b1", [128, E, H], F32, c)
            b2 = sb("f3_b2", [128, E, D], F32, c)
            loads = [(w1[:].rearrange("p e k f -> p (e k) f"), io["L3_ffn_W1"].rearrange("e (k p) f -> p (e k) f", p=128)),
                     (w2[:].rearrange("p e k f -> p (e k) f"), io["L3_ffn_W2"].rearrange("e (k p) f -> p (e k) f", p=128)),
                     (b1[:].rearrange("p e f -> p (e f)"), io["L3_ffn_b1"].rearrange("e f -> (e f)").partition_broadcast(128)),
                     (b2[:].rearrange("p e f -> p (e f)"), io["L3_ffn_b2"].rearrange("e f -> (e f)").partition_broadcast(128))]
            dispatch("f3d", E, 2, work, slot, expert, leads, TS, loads)
            expert_tiles(E, TS, expert, leads, len(loads),
                         [(D, H, lambda e, k: w1[:, bass.ds(e, 1), k, :].rearrange("p a f -> p (a f)"), lambda e: one_row(b1, e), ACT.Copy),
                          (H, D, lambda e, k: w2[:, bass.ds(e, 1), k, :].rearrange("p a f -> p (a f)"), lambda e: one_row(b2, e), ACT.Gelu)])
            collect("f3c", 2, slot, pw, TS, result=out)

    def attention():
        with ExitStack() as c:
            hst = sb("hst", [P, NT, 2 * HEADS], F32, c)
            own = sb("own", [P, NT, HEADS], F32, c)
            shift = sb("shift", [P, NT, HEADS], F32, c)
            top = sb("top", [P, 2, HEADS], F32, c)
            sums = sb("att_sums", [128, KD + 1, N + P], F32, c)
            att_project(hst)
            att_shift(hst, own, shift, top)
            att_pass(own, top, sums)
            att_finish(sums, own, shift, top)

    stages = [
        lambda: (prepare(), normalize("n0", xres, to_featT=True), attention()),
        lambda: (normalize("n1", xres, to_xn=True, to_featT=True), ffn0(),
                 normalize("n2", xn, gamma=io["L0_ffn_gamma"], beta=io["L0_ffn_beta"], add_to_x=True)),
        lambda: (normalize("n3", xres, table=t_row), edge_pass("sum", t_row, weight=ew, clear=t_disp), sum_finish()),
        lambda: (normalize("n4", xres, to_xn=True, to_featT=True), ffn1()),
        lambda: (normalize("n5", xres, table=t_row, scale=dinv), edge_pass("c1", t_row, loops=True), conv_finish(1, t_row2),
                 edge_pass("c2", t_row2, loops=True), conv_finish(2, t_row), edge_pass("c3", t_row, loops=True), conv_finish(3, None)),
        lambda: (normalize("n6", xres, to_xn=True, to_featT=True), ffn2()),
        lambda: (normalize("n7", xres, to_xn=True, to_featT=True), edge_project(), edge_gated(), sums_to_xn(),
                 normalize("n8", xn, gamma=io["L3_gnn_gamma"], beta=io["L3_gnn_beta"], add_to_x=True)),
        lambda: (normalize("n9", xres, to_xn=True),
                 normalize("n10", xn, gamma=io["L3_ffn_gamma"], beta=io["L3_ffn_beta"], to_xn=True, to_featT=True), ffn3()),
    ]
    for s in stages:
        s()


_INS = ["x", "src", "dst", "edge_attr_64", "edge_weight", "L0_gnn_W", "L0_gnn_b", "L0_gnn_a_src", "L0_gnn_a_trg", "L0_ffn_Wr",
        "L0_ffn_br", "L0_ffn_W1", "L0_ffn_b1", "L0_ffn_W2", "L0_ffn_b2", "L0_ffn_gamma", "L0_ffn_beta", "L1_gnn_weight",
        "L1_ffn_router_w1", "L1_ffn_router_b1", "L1_ffn_router_w2", "L1_ffn_router_b2", "L1_ffn_expert_w1", "L1_ffn_expert_b1",
        "L1_ffn_expert_w2", "L1_ffn_expert_b2", "L1_ffn_expert_w3", "L1_ffn_expert_b3", "L2_gnn_W1", "L2_gnn_b1", "L2_gnn_W2",
        "L2_gnn_b2", "L2_gnn_W3", "L2_gnn_b3", "L2_ffn_router_w", "L2_ffn_router_b", "L2_ffn_W1", "L2_ffn_b1", "L2_ffn_W2",
        "L2_ffn_b2", "L3_gnn_W1", "L3_gnn_b1", "L3_gnn_W2", "L3_gnn_b2", "L3_gnn_Wg", "L3_gnn_bg", "L3_gnn_gamma", "L3_gnn_beta",
        "L3_ffn_gamma", "L3_ffn_beta", "L3_ffn_Wr", "L3_ffn_br", "L3_ffn_W1", "L3_ffn_b1", "L3_ffn_W2", "L3_ffn_b2"]


def kernel(**inputs):
    import numpy as _np
    import concourse.bacc as _bacc
    from concourse import mybir as _mybir
    from concourse.bass_utils import run_bass_kernel_spmd as _run

    nc = _bacc.Bacc("TRN2", target_bir_lowering=False, num_devices=1)
    arrays, io = {}, {}
    for name in _INS:
        a = _np.ascontiguousarray(inputs[name])
        arrays["in_" + name] = a
        io[name] = nc.dram_tensor("in_" + name, a.shape, _mybir.dt.from_np(a.dtype), kind="ExternalInput").ap()
    out = nc.dram_tensor("out_x", (N, D), F32, kind="ExternalOutput").ap()
    build(nc, io, out)
    r = _run(nc, [arrays], core_ids=[0])
    return r.results[0]["out_x"]
```
